# Optimizing a Trainium2 kernel written in Bass

```python
import numpy as np
import jax
import jax.numpy as jnp

def _softmax(x, axis=-1):
    return jax.nn.softmax(x, axis=axis)

def _gelu(x):
    return jax.nn.gelu(x, approximate=True)

def _silu(x):
    return jax.nn.silu(x)

def _sigmoid(x):
    return jax.nn.sigmoid(x)

def _layernorm(x, axis=-1, eps=1e-05):
    m = jnp.mean(x, axis=axis, keepdims=True)
    v = jnp.var(x, axis=axis, keepdims=True)
    return (x - m) / jnp.sqrt(v + eps)

def _scatter_add(tgt, idx, src, axis=0):
    return tgt.at[idx].add(src)

def _segment_sum(src, seg, n):
    return jax.ops.segment_sum(src, seg, n)
kernel_name = 'mk_adj_ffn_d2_adj_r2_faf27a'

def setup_inputs(seed: int=0):
    np.random.seed(seed)
    _w = jnp.asarray

    def _rec_inputs():
        import jax
        import jax.numpy as jnp
        _gk = jax.random.key(seed)
        x = -0.0003929 + 0.9999 * jax.random.normal(jax.random.fold_in(_gk, 1), (128, 128, 128), jnp.float32)
        _w = (1.0 + jnp.arange(128, dtype=jnp.float32)) ** (-0.5)
        _w = _w / _w.mean()
        _pij = jnp.clip(0.03125 * _w[:, None] * _w[None, :], 0.0, 1.0)
        _a = jax.random.uniform(jax.random.fold_in(_gk, 2), (128, 128)) < _pij
        _a = jnp.logical_or(_a, jnp.swapaxes(_a, -1, -2))
        _a = jnp.logical_or(_a, jnp.eye(128, dtype=bool))
        _af = _a.astype(jnp.float32)
        _af = _af * jax.random.uniform(jax.random.fold_in(_gk, 3), (128, 128), jnp.float32, 0.05, 0.999963)
        adj = _af
        return (x, adj)
    x, adj = _rec_inputs()

    def _L0_gnn_setup():
        import jax, jax.numpy as jnp
        import numpy as np
        BT, N, D, HEADS, E = (512, 64, 128, 4, 256)
        LRELU_SLOPE = 0.2
        EPS = 1e-08
        key = jax.random.key(seed)
        ks = jax.random.split(key, 8)
        d = D
        return {'H': jax.random.normal(ks[0], (BT, N, d), jnp.float32), 'W_lin': jax.random.normal(ks[1], (d, d), jnp.float32) / np.sqrt(d).astype(np.float32), 'W_val': jax.random.normal(ks[2], (d, d), jnp.float32) / np.sqrt(d).astype(np.float32), 'a': jax.random.normal(ks[3], (HEADS, d // HEADS), jnp.float32), 'W_out': jax.random.normal(ks[4], (d, d), jnp.float32) / np.sqrt(d).astype(np.float32), 'A0': jax.random.uniform(ks[5], (N, N), jnp.float32), 'src': jax.random.randint(ks[6], (E,), 0, N, jnp.int32), 'dst': jax.random.randint(ks[7], (E,), 0, N, jnp.int32)}
    _L0_gnn_all = _L0_gnn_setup()
    _L0_gnn_in = {k: v for k, v in _L0_gnn_all.items() if k in ('W_lin', 'W_val', 'a', 'W_out', 'src', 'dst')}
    del _L0_gnn_all

    def _L0_ffn_setup():
        import jax, jax.numpy as jnp
        import numpy as np
        E, D, H, TOP_K = (6, 128, 128, 2)
        ROUTER_H = D // 2
        key = jax.random.key(seed)
        ks = jax.random.split(key, 12)
        s = 1.0 / np.sqrt(D)
        sh = 1.0 / np.sqrt(H)
        sr = 1.0 / np.sqrt(ROUTER_H)
        return {'features': jax.random.normal(ks[0], (8, 2048, D), dtype=jnp.float32), 'router_w1': jax.random.uniform(ks[1], (D, ROUTER_H), jnp.float32, -s, s), 'router_b1': jnp.zeros((ROUTER_H,), jnp.float32), 'router_w2': jax.random.uniform(ks[2], (ROUTER_H, E), jnp.float32, -sr, sr), 'router_b2': jnp.zeros((E,), jnp.float32), 'expert_w1': jax.random.uniform(ks[3], (E, D, H), jnp.float32, -s, s), 'expert_b1': jnp.zeros((E, H), jnp.float32), 'expert_w2': jax.random.uniform(ks[4], (E, H, H), jnp.float32, -sh, sh), 'expert_b2': jnp.zeros((E, H), jnp.float32), 'expert_w3': jax.random.uniform(ks[5], (E, H, D), jnp.float32, -sh, sh), 'expert_b3': jnp.zeros((E, D), jnp.float32)}
    _L0_ffn_all = _L0_ffn_setup()
    _L0_ffn_in = {k: v for k, v in _L0_ffn_all.items() if k in ('router_w1', 'router_b1', 'router_w2', 'router_b2', 'expert_w1', 'expert_b1', 'expert_w2', 'expert_b2', 'expert_w3', 'expert_b3')}
    del _L0_ffn_all

    def _L1_gnn_setup():
        import jax, jax.numpy as jnp
        import numpy as np
        B, T, D, H = (64, 1024, 128, 128)
        MAX_SKIP = 4

        def _lstm_last(Wih, Whh, bih, bhh, xs):
            N, _, Hd = xs.shape
            bias = bih + bhh

            def step(carry, x_t):
                h, c = carry
                g = x_t @ Wih.T + h @ Whh.T + bias
                i, f, gg, o = jnp.split(g, 4, axis=-1)
                c = jax.nn.sigmoid(f) * c + jax.nn.sigmoid(i) * jnp.tanh(gg)
                h = jax.nn.sigmoid(o) * jnp.tanh(c)
                return ((h, c), None)
            init = (jnp.zeros((N, Hd), xs.dtype), jnp.zeros((N, Hd), xs.dtype))
            (h_last, _), _ = jax.lax.scan(step, init, jnp.swapaxes(xs, 0, 1))
            return h_last
        key = jax.random.key(seed)
        ks = jax.random.split(key, 8)
        s = 0.05
        x = jax.random.normal(ks[0], (B, T, D), jnp.float32)
        adj = jax.random.uniform(ks[1], (T, T), jnp.float32) / T
        Wg0 = jax.random.normal(ks[2], (D, H), jnp.float32) * s
        bg0 = jnp.zeros((H,), jnp.float32)
        Wg1 = jax.random.normal(ks[3], (H, H), jnp.float32) * s
        bg1 = jnp.zeros((H,), jnp.float32)
        Wih = jax.random.normal(ks[4], (MAX_SKIP, 4 * H, H), jnp.float32) * s
        Whh = jax.random.normal(ks[5], (MAX_SKIP, 4 * H, H), jnp.float32) * s
        bih = jax.random.normal(ks[6], (MAX_SKIP, 4 * H), jnp.float32) * s
        bhh = jax.random.normal(ks[7], (MAX_SKIP, 4 * H), jnp.float32) * s
        return dict(x=x, adj=adj, Wg0=Wg0, bg0=bg0, Wg1=Wg1, bg1=bg1, Wih=Wih, Whh=Whh, bih=bih, bhh=bhh)
    _L1_gnn_all = _L1_gnn_setup()
    _L1_gnn_in = {k: v for k, v in _L1_gnn_all.items() if k in ('Wg0', 'bg0', 'Wg1', 'bg1', 'Wih', 'Whh', 'bih', 'bhh')}
    del _L1_gnn_all

    def _L1_ffn_setup():
        import jax, jax.numpy as jnp
        import numpy as np
        B, S, D, F, E, K = (8, 1024, 128, 512, 8, 2)
        key = jax.random.key(seed)
        ks = jax.random.split(key, 10)
        s = 0.02
        return {'x': jax.random.normal(ks[0], (B, S, D), dtype=jnp.float32), 'Wr': jax.random.normal(ks[1], (D, E), dtype=jnp.float32) * s, 'W1s': jax.random.normal(ks[2], (D, F), dtype=jnp.float32) * s, 'b1s': jnp.zeros((F,), dtype=jnp.float32), 'W2s': jax.random.normal(ks[3], (F, D), dtype=jnp.float32) * s, 'b2s': jnp.zeros((D,), dtype=jnp.float32), 'W1p': jax.random.normal(ks[4], (E, D, F), dtype=jnp.float32) * s, 'b1p': jnp.zeros((E, F), dtype=jnp.float32), 'W2p': jax.random.normal(ks[5], (E, F, D), dtype=jnp.float32) * s, 'b2p': jnp.zeros((E, D), dtype=jnp.float32)}
    _L1_ffn_all = _L1_ffn_setup()
    _L1_ffn_in = {k: v for k, v in _L1_ffn_all.items() if k in ('Wr', 'W1s', 'b1s', 'W2s', 'b2s', 'W1p', 'b1p', 'W2p', 'b2p')}
    del _L1_ffn_all
    return {'x': x, 'adj': adj, 'L0_gnn_W_lin': _L0_gnn_in['W_lin'], 'L0_gnn_W_val': _L0_gnn_in['W_val'], 'L0_gnn_a': _L0_gnn_in['a'], 'L0_gnn_W_out': _L0_gnn_in['W_out'], 'L0_gnn_src': _L0_gnn_in['src'], 'L0_gnn_dst': _L0_gnn_in['dst'], 'L0_ffn_router_w1': _L0_ffn_in['router_w1'], 'L0_ffn_router_b1': _L0_ffn_in['router_b1'], 'L0_ffn_router_w2': _L0_ffn_in['router_w2'], 'L0_ffn_router_b2': _L0_ffn_in['router_b2'], 'L0_ffn_expert_w1': _L0_ffn_in['expert_w1'], 'L0_ffn_expert_b1': _L0_ffn_in['expert_b1'], 'L0_ffn_expert_w2': _L0_ffn_in['expert_w2'], 'L0_ffn_expert_b2': _L0_ffn_in['expert_b2'], 'L0_ffn_expert_w3': _L0_ffn_in['expert_w3'], 'L0_ffn_expert_b3': _L0_ffn_in['expert_b3'], 'L1_gnn_Wg0': _L1_gnn_in['Wg0'], 'L1_gnn_bg0': _L1_gnn_in['bg0'], 'L1_gnn_Wg1': _L1_gnn_in['Wg1'], 'L1_gnn_bg1': _L1_gnn_in['bg1'], 'L1_gnn_Wih': _L1_gnn_in['Wih'], 'L1_gnn_Whh': _L1_gnn_in['Whh'], 'L1_gnn_bih': _L1_gnn_in['bih'], 'L1_gnn_bhh': _L1_gnn_in['bhh'], 'L1_ffn_Wr': _L1_ffn_in['Wr'], 'L1_ffn_W1s': _L1_ffn_in['W1s'], 'L1_ffn_b1s': _L1_ffn_in['b1s'], 'L1_ffn_W2s': _L1_ffn_in['W2s'], 'L1_ffn_b2s': _L1_ffn_in['b2s'], 'L1_ffn_W1p': _L1_ffn_in['W1p'], 'L1_ffn_b1p': _L1_ffn_in['b1p'], 'L1_ffn_W2p': _L1_ffn_in['W2p'], 'L1_ffn_b2p': _L1_ffn_in['b2p']}

def reference(x, adj, L0_gnn_W_lin, L0_gnn_W_val, L0_gnn_a, L0_gnn_W_out, L0_gnn_src, L0_gnn_dst, L0_ffn_router_w1, L0_ffn_router_b1, L0_ffn_router_w2, L0_ffn_router_b2, L0_ffn_expert_w1, L0_ffn_expert_b1, L0_ffn_expert_w2, L0_ffn_expert_b2, L0_ffn_expert_w3, L0_ffn_expert_b3, L1_gnn_Wg0, L1_gnn_bg0, L1_gnn_Wg1, L1_gnn_bg1, L1_gnn_Wih, L1_gnn_Whh, L1_gnn_bih, L1_gnn_bhh, L1_ffn_Wr, L1_ffn_W1s, L1_ffn_b1s, L1_ffn_W2s, L1_ffn_b2s, L1_ffn_W1p, L1_ffn_b1p, L1_ffn_W2p, L1_ffn_b2p):
    import jax
    import jax.numpy as jnp

    def _L0_gnn_ref(H, W_lin, W_val, a, W_out, A0, src, dst):
        import jax, jax.numpy as jnp
        import numpy as np
        BT, N, D, HEADS, E = (512, 64, 128, 4, 256)
        LRELU_SLOPE = 0.2
        EPS = 1e-08
        bt, n, d = H.shape
        h, dh = a.shape
        Xq = (H @ W_lin.T).reshape(bt, n, h, dh)
        Xv = (H @ W_val.T).reshape(bt, n, h, dh)
        Qs = Xq[:, src]
        Kt = Xq[:, dst]
        e = jnp.einsum('behd,hd->beh', jax.nn.leaky_relu(Qs + Kt, LRELU_SLOPE), a)
        e = e + jnp.log(A0[src, dst] + EPS)[None, :, None]
        e_t = e.transpose(1, 0, 2)
        m = jax.ops.segment_max(e_t, src, num_segments=n)
        ex = jnp.exp(e_t - m[src])
        denom = jax.ops.segment_sum(ex, src, num_segments=n)
        attn = ex / denom[src]
        Vt = Xv[:, dst].transpose(1, 0, 2, 3)
        Y = jax.ops.segment_sum(attn[..., None] * Vt, src, num_segments=n)
        Y = Y.transpose(1, 0, 2, 3).reshape(bt, n, d)
        return Y @ W_out.T

    def _L0_ffn_ref(features, router_w1, router_b1, router_w2, router_b2, expert_w1, expert_b1, expert_w2, expert_b2, expert_w3, expert_b3):
        import jax, jax.numpy as jnp
        import numpy as np
        E, D, H, TOP_K = (6, 128, 128, 2)
        ROUTER_H = D // 2
        rh = jax.nn.relu(features @ router_w1 + router_b1)
        expert_logits = jax.nn.softmax(rh @ router_w2 + router_b2, axis=-1)
        top_w, top_i = jax.lax.top_k(expert_logits, TOP_K)
        routing_weights = jax.nn.softmax(top_w, axis=-1)
        h1 = jax.nn.relu(jnp.einsum('bsd,edh->bseh', features, expert_w1) + expert_b1)
        h2 = jax.nn.relu(jnp.einsum('bseh,ehf->bsef', h1, expert_w2) + expert_b2)
        expert_out = jnp.einsum('bsef,efo->bseo', h2, expert_w3) + expert_b3
        sel = jnp.take_along_axis(expert_out, top_i[:, :, :, None], axis=2)
        combined = jnp.sum(sel * routing_weights[..., None], axis=2)
        return combined

    def _L1_gnn_ref(x, adj, Wg0, bg0, Wg1, bg1, Wih, Whh, bih, bhh):
        import jax, jax.numpy as jnp
        import numpy as np
        B, T, D, H = (64, 1024, 128, 128)
        MAX_SKIP = 4

        def _lstm_last(Wih, Whh, bih, bhh, xs):
            N, _, Hd = xs.shape
            bias = bih + bhh

            def step(carry, x_t):
                h, c = carry
                g = x_t @ Wih.T + h @ Whh.T + bias
                i, f, gg, o = jnp.split(g, 4, axis=-1)
                c = jax.nn.sigmoid(f) * c + jax.nn.sigmoid(i) * jnp.tanh(gg)
                h = jax.nn.sigmoid(o) * jnp.tanh(c)
                return ((h, c), None)
            init = (jnp.zeros((N, Hd), xs.dtype), jnp.zeros((N, Hd), xs.dtype))
            (h_last, _), _ = jax.lax.scan(step, init, jnp.swapaxes(xs, 0, 1))
            return h_last
        h = jax.nn.relu(jnp.einsum('ts,bsh->bth', adj, x @ Wg0 + bg0))
        h = jax.nn.relu(jnp.einsum('ts,bsh->bth', adj, h @ Wg1 + bg1))
        Bv, Tv, Hd = h.shape
        for p in range(1, MAX_SKIP + 1):
            nw = Tv // p
            wins = h[:, :nw * p, :].reshape(Bv * nw, p, Hd)
            last = _lstm_last(Wih[p - 1], Whh[p - 1], bih[p - 1], bhh[p - 1], wins)
            idx = jnp.arange(nw) * p + (p - 1)
            h = h.at[:, idx, :].set(last.reshape(Bv, nw, Hd))
        return h

    def _L1_ffn_ref(x, Wr, W1s, b1s, W2s, b2s, W1p, b1p, W2p, b2p):
        import jax, jax.numpy as jnp
        import numpy as np
        B, S, D, F, E, K = (8, 1024, 128, 512, 8, 2)
        gelu = lambda t: jax.nn.gelu(t, approximate=False)
        shared = gelu(x @ W1s + b1s) @ W2s + b2s
        rw = jax.nn.softmax(x @ Wr, axis=-1)
        topw, topi = jax.lax.top_k(rw, K)
        topw = topw / jnp.sum(topw, axis=-1, keepdims=True)
        mask = jnp.sum(jax.nn.one_hot(topi, E, dtype=topw.dtype) * topw[..., None], axis=-2)
        h = gelu(jnp.einsum('bsd,edf->bsef', x, W1p) + b1p)
        priv = jnp.einsum('bsef,efd->bsed', h, W2p) + b2p
        routed = jnp.einsum('bsed,bse->bsd', priv, mask)
        return shared + routed
    x = x + _L0_gnn_ref(_layernorm(x, axis=-1), L0_gnn_W_lin, L0_gnn_W_val, L0_gnn_a, L0_gnn_W_out, adj, L0_gnn_src, L0_gnn_dst)
    x = x + _L0_ffn_ref(_layernorm(x, axis=-1), L0_ffn_router_w1, L0_ffn_router_b1, L0_ffn_router_w2, L0_ffn_router_b2, L0_ffn_expert_w1, L0_ffn_expert_b1, L0_ffn_expert_w2, L0_ffn_expert_b2, L0_ffn_expert_w3, L0_ffn_expert_b3)
    x = x + _L1_gnn_ref(_layernorm(x, axis=-1), adj, L1_gnn_Wg0, L1_gnn_bg0, L1_gnn_Wg1, L1_gnn_bg1, L1_gnn_Wih, L1_gnn_Whh, L1_gnn_bih, L1_gnn_bhh)
    x = x + _L1_ffn_ref(_layernorm(x, axis=-1), L1_ffn_Wr, L1_ffn_W1s, L1_ffn_b1s, L1_ffn_W2s, L1_ffn_b2s, L1_ffn_W1p, L1_ffn_b1p, L1_ffn_W2p, L1_ffn_b2p)
    return x

_drawn_inputs = setup_inputs


def setup_inputs(seed=0):
    import zlib

    import numpy as np

    out = dict(_drawn_inputs(seed))
    spreads = {'L0_ffn_router_b1': (0.0, 0.1),
     'L0_ffn_router_b2': (0.0, 0.1),
     'L0_ffn_expert_b1': (0.0, 0.677),
     'L0_ffn_expert_b2': (0.0, 0.288),
     'L0_ffn_expert_b3': (0.0, 0.1),
     'L1_gnn_bg0': (0.0, 0.1),
     'L1_gnn_bg1': (0.0, 0.375),
     'L1_ffn_b1s': (0.0, 0.415),
     'L1_ffn_b2s': (0.0, 0.1),
     'L1_ffn_b1p': (0.0, 0.545),
     'L1_ffn_b2p': (0.0, 0.1)}
    factors = {'L1_gnn_Whh': 8.0, 'L1_gnn_bih': 3.16, 'L1_gnn_bhh': 3.231}
    for name, (base, spread) in spreads.items():
        noise = np.random.default_rng([zlib.crc32(name.encode()), seed]).standard_normal(out[name].shape)
        drawn = base * np.exp(spread * noise) if base else spread * noise
        out[name] = jnp.asarray(drawn.astype(out[name].dtype))
    for name, factor in factors.items():
        out[name] = (out[name] * factor).astype(out[name].dtype)
    return out
```

```python
from contextlib import ExitStack

import numpy as np

import concourse.bass as bass
from concourse import mybir

STOP = "H"

ALU = mybir.AluOpType
ACT = mybir.ActivationFunctionType
AXX = mybir.AxisListType.X
F32 = mybir.dt.float32
I32 = mybir.dt.int32

P = 128
B = 128
D = 128
NB = 4
G = B // NB
W = NB * D
HEADS = 4
EDGES = 256
EC = EDGES // P
E0 = 6
E1 = 8
FK = 4
SKIPS = 4
BIG = 3.0e38
LN_EPS = 1e-5
LOG_EPS = 1e-8

SMALL = [("ident", 128), ("iota", 256), ("pidx", 1), ("eidx", EC), ("ones", 128),
         ("rank0", E0), ("rank1", E1),
         ("wq", D), ("wv", D), ("wout", D), ("ahead", HEADS), ("adj", P), ("adjT", P),
         ("rw1", 64), ("rb1", 1), ("rw2", E0), ("rb2", E0),
         ("wg0", D), ("bg0", D), ("wg1", D), ("bg1", D), ("wr", E1)]
SMALL_AT = {}
SMALL_COLS = 0
for _name, _n in SMALL:
    SMALL_AT[_name] = (SMALL_COLS, SMALL_COLS + _n)
    SMALL_COLS += _n
FFN0_COLS = E0 * 3 * D + E0 * 2 + D
LSTM_COLS = SKIPS * 8 * D + SKIPS * 8
FFN1_COLS = (E1 + 1) * (2 * FK * D + FK) + D


class Steps:

    def __init__(self, sem, ahead=0):
        self.sem, self.ahead = sem, ahead

    def open(self, eng):
        eng.sem_inc(self.sem, self.ahead)

    def done(self, n):
        return n + (self.ahead + 1)


def build(nc, xT, small, edges, ffn0, lstm, ffn1, out, stop):
    order = "CDGH"
    upto = order.index(stop)
    ctx = ExitStack()
    with ctx:
        def sb(name, shape, dt=F32):
            return ctx.enter_context(nc.sbuf_tensor(name, shape, dt))

        def sem(name):
            return ctx.enter_context(nc.semaphore(name))

        def steps(name, ahead=0):
            return Steps(sem(name), ahead)

        X = sb("X", [P, B * D])
        Y = sb("Y", [P, B * D])
        small_sb = sb("small_sb", [P, SMALL_COLS])
        STAT = sb("STAT", [P, B, 6])
        MEAN = sb("MEAN", [P, B])
        RSTD = sb("RSTD", [P, B])
        NT = sb("NT", [P, 2, B])
        ARENA = 17350
        arena = sb("arena", [P, ARENA])
        banks = [ctx.enter_context(nc.psum_tensor(f"bank{i}", [P, 512], F32)) for i in range(8)]

        def cst(name):
            a, b = SMALL_AT[name]
            return small_sb[:, a:b]

        def carve(start=0):
            at = [start]

            def take(*shape):
                n = int(np.prod(shape))
                v = arena[:, at[0]:at[0] + n]
                at[0] += n
                assert at[0] <= ARENA, at[0]
                if len(shape) == 2:
                    v = v.rearrange("p (a b) -> p a b", a=shape[0])
                if len(shape) == 3:
                    v = v.rearrange("p (a b c) -> p a b c", a=shape[0], b=shape[1])
                return v
            take.at = at
            return take

        ident = cst("ident")
        X3 = X[:, :].rearrange("p (b d) -> p b d", d=D)
        Y3 = Y[:, :].rearrange("p (b d) -> p b d", d=D)

        s_small = sem("s_small")
        s_edges = sem("s_edges")
        s_x = [sem(f"s_x{i}") for i in range(8)]
        s_ffn0 = sem("s_ffn0")
        s_lstm = sem("s_lstm")
        s_ffn1 = sem("s_ffn1")
        s_out = sem("s_out")
        s_chain = sem("s_chain")
        chained = [0]

        def link(ins):
            chained[0] += 1
            ins.then_inc(s_chain, 1)
            nc.vector.wait_ge(s_chain, chained[0])

        def group_stats(g):
            for b in range(NB):
                ins = nc.vector.bn_stats(STAT[:, bass.ds(g * NB + b, 1), :], X3[:, bass.ds(g * NB + b, 1), :])
            return ins

        with nc.Block() as block:
            stat_ready = sem("stat_ready0")

            @block.sync
            def _(sp):
                sp.dma_start(small_sb[:, :], small).then_inc(s_small, 16)
                for i in range(8):
                    n = B * D // 8
                    sp.dma_start(X[:, i * n:(i + 1) * n], xT[:, i * n:(i + 1) * n]).then_inc(s_x[i], 16)

            @block.vector
            def _(dve):
                for i in range(8):
                    dve.wait_ge(s_x[i], 16)
                    with dve.Fori(0, G // 8) as it:
                        group_stats(it + i * (G // 8)).then_inc(stat_ready, 1)
                dve.wait_ge(stat_ready, G)

        def finish_rstd(tag):
            ve_ready, root_ready = sem("ve" + tag), sem("root" + tag)
            with nc.Block() as block:
                @block.vector
                def _(dve):
                    even, odd = STAT[:, :, 1], STAT[:, :, 4]
                    link(nc.vector.tensor_tensor(MEAN[:, :], even, odd, ALU.add))
                    link(nc.vector.tensor_scalar(MEAN[:, :], MEAN[:, :], 0.5, None, ALU.mult))
                    link(nc.vector.tensor_tensor(NT[:, 1, :], even, odd, ALU.subtract))
                    link(nc.vector.tensor_tensor(NT[:, 1, :], NT[:, 1, :], NT[:, 1, :], ALU.mult))
                    link(nc.vector.tensor_scalar(NT[:, 1, :], NT[:, 1, :], 0.25, LN_EPS, ALU.mult, ALU.add))
                    link(nc.vector.tensor_tensor(NT[:, 0, :], STAT[:, :, 2], STAT[:, :, 5], ALU.add))
                    nc.vector.scalar_tensor_tensor(NT[:, 0, :], NT[:, 0, :], 1.0 / D, NT[:, 1, :], ALU.mult, ALU.add)\
                        .then_inc(ve_ready, 1)
                    dve.wait_ge(root_ready, 1)
                    link(nc.vector.reciprocal(RSTD[:, :], NT[:, 1, :]))
                    link(nc.vector.tensor_tensor(NT[:, 1, :], RSTD[:, :], RSTD[:, :], ALU.mult))
                    link(nc.vector.tensor_tensor(NT[:, 1, :], NT[:, 1, :], NT[:, 0, :], ALU.mult))
                    link(nc.vector.tensor_scalar(NT[:, 1, :], NT[:, 1, :], -0.5, 1.5, ALU.mult, ALU.add))
                    link(nc.vector.tensor_tensor(RSTD[:, :], RSTD[:, :], NT[:, 1, :], ALU.mult))

                @block.scalar
                def _(act):
                    act.wait_ge(ve_ready, 1)
                    nc.scalar.activation(NT[:, 1, :], NT[:, 0, :], ACT.Sqrt).then_inc(root_ready, 1)

        def normalise(dst, g):
            for b in range(NB):
                ins = nc.vector.tensor_scalar(dst[:, b * D:(b + 1) * D], X3[:, bass.ds(g * NB + b, 1), :],
                                              MEAN[:, bass.ds(g * NB + b, 1)], RSTD[:, bass.ds(g * NB + b, 1)],
                                              ALU.subtract, ALU.mult)
            return ins

        def cols(g):
            return bass.ds(g * W, W)

        take = carve()
        sd_int = take(2 * EDGES + 2 * EC).bitcast(I32)
        sd = take(2 * EDGES + 2 * EC)
        perm = take(EC, EDGES)
        srcB = take(EC, P)
        dstB = take(EC, P)
        rowS = take(EDGES)
        rowD = take(EDGES)
        colSD = take(EC, 2)
        ohsT = take(EDGES)
        ohdT = take(EDGES)
        ohsum = take(EDGES)
        ohs = take(EC, P)
        ohd = take(EC, P)
        reset = take(EDGES)
        same = take(EC, EDGES)
        lastsel = take(EC, EDGES)
        key = take(EDGES)
        keyc = take(EC)
        rank = take(EC)
        later = take(EC)
        islast = take(EC)
        adjv = take(EC)
        logadj = take(EC)
        logeps = take(1)
        tmp = take(EDGES)
        S = take(EC, B * HEADS)
        att = take(EC, B * HEADS)
        stage = take.at[0]
        rmax = take(EC, B * HEADS)
        ST = take(4, EDGES)
        RUN = take(4, EDGES)
        take = carve(stage)
        xn = take(2, W)
        xnT = take(2, W)
        qs = take(2, W)
        s02 = take(4, 512)
        lr = take(4, 512)
        take = carve(stage)
        wv = take(2, EC, W)
        yT = take(2, W)

        with nc.Block() as block:
            perm_ready, sorted_done, sorted_ready, oh_ready, adj_done, adj_ready = (
                sem(n) for n in ("perm_ready", "sorted_done", "sorted_ready", "oh_ready", "adj_done", "adj_ready"))

            @block.sync
            def _(sp):
                sp.dma_start(sd_int, edges).then_inc(s_edges, 16)

            @block.vector
            def _(dve):
                dve.wait_ge(s_small, 16)
                dve.wait_ge(s_edges, 16)
                iota = cst("iota")
                ones = cst("ones")
                link(nc.vector.memset(logeps, LOG_EPS))
                link(nc.vector.tensor_copy(sd, sd_int))
                link(nc.vector.scalar_tensor_tensor(key, sd[:, 0:EDGES], float(EDGES), iota, ALU.mult, ALU.add))
                for c in range(EC):
                    scol = sd[:, 2 * EDGES + 2 * c:2 * EDGES + 2 * c + 1]
                    dcol = sd[:, 2 * EDGES + 2 * c + 1:2 * EDGES + 2 * c + 2]
                    link(nc.vector.scalar_tensor_tensor(keyc[:, c:c + 1], scol, float(EDGES), cst("eidx")[:, c:c + 1],
                                                        ALU.mult, ALU.add))
                    link(nc.vector.tensor_scalar(tmp, key, keyc[:, c:c + 1], None, ALU.is_lt))
                    link(nc.vector.reduce_sum(rank[:, c:c + 1], tmp, AXX))
                    link(nc.vector.tensor_scalar(perm[:, c, :], iota, rank[:, c:c + 1], None, ALU.is_equal))
                    link(nc.vector.tensor_scalar(srcB[:, c, :], ones, scol, None, ALU.mult))
                    ins = nc.vector.tensor_scalar(dstB[:, c, :], ones, dcol, None, ALU.mult)
                    link(ins)
                nc.vector.tensor_copy(tmp, key).then_inc(perm_ready, 1)
                dve.wait_ge(sorted_done, 1)
                link(nc.vector.tensor_copy(rowS, banks[0][:, 0:EDGES]))
                link(nc.vector.tensor_copy(rowD, banks[1][:, 0:EDGES]))
                link(nc.vector.tensor_copy(colSD.rearrange("p a b -> p (a b)"), banks[2][:, 0:2 * EC]))
                link(nc.vector.tensor_scalar(ohsT, rowS, cst("pidx"), None, ALU.is_equal))
                link(nc.vector.tensor_scalar(ohdT, rowD, cst("pidx"), None, ALU.is_equal))
                link(nc.vector.tensor_tensor(ohsum, ohsT, ohdT, ALU.add))
                link(nc.vector.memset(reset, 0.0))
                link(nc.vector.tensor_tensor(reset[:, 1:EDGES], rowS[:, 1:EDGES], rowS[:, 0:EDGES - 1], ALU.not_equal))
                link(nc.vector.tensor_scalar(reset, reset, -BIG, None, ALU.mult))
                for c in range(EC):
                    link(nc.vector.tensor_scalar(ohs[:, c, :], iota[:, 0:P], colSD[:, c, 0:1], None, ALU.is_equal))
                    link(nc.vector.tensor_scalar(ohd[:, c, :], iota[:, 0:P], colSD[:, c, 1:2], None, ALU.is_equal))
                    link(nc.vector.tensor_scalar(same[:, c, :], rowS, colSD[:, c, 0:1], None, ALU.is_equal))
                    link(nc.vector.tensor_scalar(tmp, iota, cst("eidx")[:, c:c + 1], None, ALU.is_gt))
                    link(nc.vector.tensor_tensor(tmp, tmp, same[:, c, :], ALU.mult))
                    link(nc.vector.reduce_sum(later[:, c:c + 1], tmp, AXX))
                    link(nc.vector.tensor_scalar(islast[:, c:c + 1], later[:, c:c + 1], 0.0, None, ALU.is_equal))
                    link(nc.vector.tensor_scalar(lastsel[:, c, :], same[:, c, :], islast[:, c:c + 1], None, ALU.mult))
                nc.vector.tensor_copy(tmp, key).then_inc(oh_ready, 1)
                dve.wait_ge(adj_done, 1)
                for c in range(EC):
                    link(nc.vector.tensor_tensor(tmp[:, 0:P], banks[3][:, c * P:(c + 1) * P], ohd[:, c, :], ALU.mult))
                    link(nc.vector.reduce_sum(adjv[:, c:c + 1], tmp[:, 0:P], AXX))
                nc.vector.tensor_copy(tmp, key).then_inc(adj_ready, 1)

            @block.tensor
            def _(pe):
                pe.wait_ge(s_small, 16)
                pe.wait_ge(perm_ready, 1)
                for dst, src in ((banks[0], srcB), (banks[1], dstB)):
                    for c in range(EC):
                        nc.tensor.matmul(dst[:, 0:EDGES], src[:, c, :], perm[:, c, :], start=c == 0, stop=c == EC - 1)
                for r in range(EC):
                    for c in range(EC):
                        last = nc.tensor.matmul(banks[2][:, 2 * r:2 * r + 2], perm[:, c, r * P:(r + 1) * P],
                                                sd[:, 2 * EDGES + 2 * c:2 * EDGES + 2 * c + 2],
                                                start=c == 0, stop=c == EC - 1)
                last.then_inc(sorted_done, 1)
                pe.wait_ge(oh_ready, 1)
                for c in range(EC):
                    last = nc.tensor.matmul(banks[3][:, c * P:(c + 1) * P], ohsT[:, c * P:(c + 1) * P], cst("adj"),
                                            start=True, stop=True)
                last.then_inc(adj_done, 1)

            @block.scalar
            def _(act):
                act.wait_ge(adj_ready, 1)
                nc.scalar.activation(logadj, adjv, ACT.Ln, bias=logeps)

        finish_rstd("0")

        with nc.Block() as block:
            xn_ready = steps("a_xn_ready", 2)
            t_done = steps("a_t_done", 2)
            xnT_ready = steps("a_xnT_ready", 2)
            qv_done = steps("a_qv_done", 2)
            q_ready = steps("a_q_ready", 2)
            v_ready = steps("a_v_ready", 2)
            pair_done = steps("a_pair_done", 4)
            low_ready = steps("a_low_ready", 4)
            lr_ready = steps("a_lr_ready", 4)
            score_done = steps("a_score_done", 2)
            score_used = steps("a_score_used", 2)
            psT = banks[0:2]
            psQ, psV = banks[2], banks[3]
            psG = banks[4:8]

            @block.vector
            def _(dve):
                for s in (xn_ready, q_ready, lr_ready, score_used):
                    s.open(dve)
                with dve.Fori(0, G // 2) as it:
                    for u in range(2):
                        g = it * 2 + u
                        dve.wait_ge(t_done.sem, t_done.done(g - 2))
                        normalise(xn[:, u, :], g).then_inc(xn_ready.sem, 1)
                    for u in range(2):
                        g = it * 2 + u
                        dve.wait_ge(qv_done.sem, qv_done.done(g))
                        dve.wait_ge(pair_done.sem, pair_done.done(g * 2 - 3))
                        nc.vector.tensor_copy(qs[:, u, :], psQ[:, :]).then_inc(q_ready.sem, 1)
                    for u in range(2):
                        for j in range(2):
                            h = it * 4 + (2 * u + j)
                            k = 2 * u + j
                            dve.wait_ge(low_ready.sem, low_ready.done(h))
                            dve.wait_ge(score_done.sem, score_done.done(it * 2 + (u - 2)))
                            nc.vector.tensor_tensor(lr[:, k, :], psG[k][:, :], s02[:, k, :], ALU.max)\
                                .then_inc(lr_ready.sem, 1)
                    for u in range(2):
                        g = it * 2 + u
                        dve.wait_ge(score_done.sem, score_done.done(g))
                        for c in range(EC):
                            ins = nc.vector.tensor_scalar(S[:, c, bass.ds(g * NB * HEADS, NB * HEADS)],
                                                          psT[u][:, c * 16:(c + 1) * 16], logadj[:, c:c + 1], None,
                                                          ALU.add)
                        ins.then_inc(score_used.sem, 1)

            @block.scalar
            def _(act):
                for s in (xnT_ready, v_ready, low_ready):
                    s.open(act)
                with act.Fori(0, G // 2) as it:
                    for u in range(2):
                        g = it * 2 + u
                        act.wait_ge(t_done.sem, t_done.done(g))
                        act.wait_ge(qv_done.sem, qv_done.done(g - 2))
                        nc.scalar.copy(xnT[:, u, :], psT[u][:, :]).then_inc(xnT_ready.sem, 1)
                    for u in range(2):
                        g = it * 2 + u
                        act.wait_ge(qv_done.sem, qv_done.done(g))
                        nc.scalar.copy(Y[:, cols(g)], psV[:, :]).then_inc(v_ready.sem, 1)
                    for k in range(4):
                        h = it * 4 + k
                        act.wait_ge(pair_done.sem, pair_done.done(h))
                        act.wait_ge(lr_ready.sem, lr_ready.done(h - 4))
                        nc.scalar.mul(s02[:, k, :], psG[k][:, :], 0.2).then_inc(low_ready.sem, 1)

            @block.tensor
            def _(pe):
                for s in (t_done, qv_done, pair_done, score_done):
                    s.open(pe)
                with pe.Fori(0, G // 2) as it:
                    for u in range(2):
                        g = it * 2 + u
                        pe.wait_ge(xn_ready.sem, xn_ready.done(g))
                        pe.wait_ge(score_used.sem, score_used.done(g - 2))
                        for b in range(NB):
                            last = nc.tensor.transpose(psT[u][:, b * P:(b + 1) * P], xn[:, u, b * D:(b + 1) * D], ident)
                        last.then_inc(t_done.sem, 1)
                    for u in range(2):
                        g = it * 2 + u
                        pe.wait_ge(xnT_ready.sem, xnT_ready.done(g))
                        pe.wait_ge(q_ready.sem, q_ready.done(g - 1))
                        pe.wait_ge(v_ready.sem, v_ready.done(g - 1))
                        for b in range(NB):
                            xb = xnT[:, u, b * P:(b + 1) * P]
                            nc.tensor.matmul(psQ[:, b * D:(b + 1) * D], xb, cst("wq"), start=True, stop=True)
                            last = nc.tensor.matmul(psV[:, b * D:(b + 1) * D], xb, cst("wv"), start=True, stop=True)
                        last.then_inc(qv_done.sem, 1)
                    for u in range(2):
                        g = it * 2 + u
                        pe.wait_ge(q_ready.sem, q_ready.done(g))
                        for j in range(2):
                            h = it * 4 + (2 * u + j)
                            pe.wait_ge(lr_ready.sem, lr_ready.done(h - 4))
                            for i in range(2):
                                b = 2 * j + i
                                last = nc.tensor.matmul(psG[2 * u + j][:, i * EDGES:(i + 1) * EDGES],
                                                        qs[:, u, b * D:(b + 1) * D], ohsum, start=True, stop=True)
                            last.then_inc(pair_done.sem, 1)
                    for u in range(2):
                        g = it * 2 + u
                        pe.wait_ge(lr_ready.sem, lr_ready.done(it * 4 + (2 * u + 1)))
                        for b in range(NB):
                            for c in range(EC):
                                at = (b % 2) * EDGES + c * P
                                last = nc.tensor.matmul(psT[u][:, c * 16 + b * HEADS:c * 16 + (b + 1) * HEADS],
                                                        lr[:, 2 * u + b // 2, at:at + P], cst("ahead"),
                                                        start=True, stop=True)
                        last.then_inc(score_done.sem, 1)

        with nc.Block() as block:
            st_done, st_ready, run_ready, back_done, back_ready, m_done, sub_ready, ex_ready, den_done = (
                sem(n) for n in ("st_done", "st_ready", "run_ready", "back_done", "back_ready", "m_done",
                                 "sub_ready", "ex_ready", "den_done"))

            @block.tensor
            def _(pe):
                for t in range(4):
                    for c in range(EC):
                        k = t * EC + c
                        last = nc.tensor.transpose(banks[k // 4][:, (k % 4) * P:(k % 4 + 1) * P],
                                                   S[:, c, t * P:(t + 1) * P], ident)
                last.then_inc(st_done, 1)
                pe.wait_ge(run_ready, 1)
                for c in range(EC):
                    for t in range(4):
                        last = nc.tensor.transpose(banks[2 + c][:, t * P:(t + 1) * P],
                                                   RUN[:, t, c * P:(c + 1) * P], ident)
                last.then_inc(back_done, 1)
                pe.wait_ge(back_ready, 1)
                for c in range(EC):
                    for k in range(EC):
                        last = nc.tensor.matmul(banks[4 + c][:, :], lastsel[:, k, c * P:(c + 1) * P], rmax[:, k, :],
                                                start=k == 0, stop=k == EC - 1)
                last.then_inc(m_done, 1)
                pe.wait_ge(ex_ready, 1)
                for c in range(EC):
                    for k in range(EC):
                        last = nc.tensor.matmul(banks[6 + c][:, :], same[:, k, c * P:(c + 1) * P], att[:, k, :],
                                                start=k == 0, stop=k == EC - 1)
                last.then_inc(den_done, 1)

            @block.vector
            def _(dve):
                dve.wait_ge(st_done, 1)
                for k in range(2):
                    link(nc.vector.tensor_copy(ST[:, 2 * k:2 * k + 2, :].rearrange("p a b -> p (a b)"), banks[k][:, :]))
                for t in range(4):
                    ins = nc.vector.tensor_tensor_scan(RUN[:, t, :], reset, ST[:, t, :], -BIG, ALU.add, ALU.max)
                ins.then_inc(run_ready, 1)
                dve.wait_ge(back_done, 1)
                for c in range(EC):
                    ins = nc.vector.tensor_copy(rmax[:, c, :], banks[2 + c][:, :])
                ins.then_inc(back_ready, 1)
                dve.wait_ge(m_done, 1)
                for c in range(EC):
                    ins = nc.vector.tensor_tensor(S[:, c, :], S[:, c, :], banks[4 + c][:, :], ALU.subtract)
                ins.then_inc(sub_ready, 1)
                dve.wait_ge(den_done, 1)
                for c in range(EC):
                    link(nc.vector.reciprocal(rmax[:, c, :], banks[6 + c][:, :]))
                    link(nc.vector.tensor_tensor(att[:, c, :], att[:, c, :], rmax[:, c, :], ALU.mult))

            @block.scalar
            def _(act):
                act.wait_ge(sub_ready, 1)
                for c in range(EC):
                    ins = nc.scalar.activation(att[:, c, :], S[:, c, :], ACT.Exp)
                ins.then_inc(ex_ready, 1)

        with nc.Block() as block:
            val_done = steps("c_val_done", 4)
            wv_ready = steps("c_wv_ready", 4)
            y_done = steps("c_y_done", 2)
            yT_ready = steps("c_yT_ready", 2)
            o_done = steps("c_o_done", 2)
            o_used = steps("c_o_used", 2)
            psVal = banks[0:4]
            psY = banks[4:6]
            psO = banks[6:8]

            @block.tensor
            def _(pe):
                for s in (val_done, y_done, o_done):
                    s.open(pe)
                with pe.Fori(0, G // 2) as it:
                    for u in range(2):
                        g = it * 2 + u
                        for c in range(EC):
                            n = it * 4 + (2 * u + c)
                            pe.wait_ge(wv_ready.sem, wv_ready.done(n - 4))
                            nc.tensor.matmul(psVal[2 * u + c][:, :], ohdT[:, c * P:(c + 1) * P], Y[:, cols(g)],
                                             start=True, stop=True).then_inc(val_done.sem, 1)
                    for u in range(2):
                        g = it * 2 + u
                        pe.wait_ge(wv_ready.sem, wv_ready.done(it * 4 + (2 * u + 1)))
                        pe.wait_ge(yT_ready.sem, yT_ready.done(g - 2))
                        for b in range(NB):
                            for c in range(EC):
                                last = nc.tensor.matmul(psY[u][:, b * P:(b + 1) * P], wv[:, u, c, b * D:(b + 1) * D],
                                                        ohs[:, c, :], start=c == 0, stop=c == EC - 1)
                        last.then_inc(y_done.sem, 1)
                    for u in range(2):
                        g = it * 2 + u
                        pe.wait_ge(yT_ready.sem, yT_ready.done(g))
                        pe.wait_ge(o_used.sem, o_used.done(g - 2))
                        for b in range(NB):
                            last = nc.tensor.matmul(psO[u][:, b * D:(b + 1) * D], yT[:, u, b * P:(b + 1) * P],
                                                    cst("wout"), start=True, stop=True)
                        last.then_inc(o_done.sem, 1)

            @block.scalar
            def _(act):
                yT_ready.open(act)
                with act.Fori(0, G // 2) as it:
                    for u in range(2):
                        g = it * 2 + u
                        act.wait_ge(y_done.sem, y_done.done(g))
                        act.wait_ge(o_done.sem, o_done.done(g - 2))
                        nc.scalar.copy(yT[:, u, :], psY[u][:, :]).then_inc(yT_ready.sem, 1)

            @block.vector
            def _(dve):
                for s in (wv_ready, o_used):
                    s.open(dve)
                with dve.Fori(0, G // 2) as it:
                    for u in range(2):
                        for c in range(EC):
                            n = it * 4 + (2 * u + c)
                            g = it * 2 + u
                            dve.wait_ge(val_done.sem, val_done.done(n))
                            dve.wait_ge(y_done.sem, y_done.done(g - 2))
                            weight = att[:, c, bass.ds(g * NB * HEADS, NB * HEADS)].unsqueeze(2)\
                                .broadcast_to([P, NB * HEADS, D // HEADS])
                            nc.vector.tensor_tensor(
                                wv[:, u, c, :].rearrange("p (a b) -> p a b", b=D // HEADS),
                                psVal[2 * u + c][:, :].rearrange("p (a b) -> p a b", b=D // HEADS),
                                weight, ALU.mult).then_inc(wv_ready.sem, 1)
                    for u in range(2):
                        g = it * 2 + u
                        dve.wait_ge(o_done.sem, o_done.done(g))
                        ins = nc.vector.tensor_tensor(X[:, cols(g)], X[:, cols(g)], psO[u][:, :], ALU.add)
                        ins.then_inc(o_used.sem, 1)
                        dve.wait_ge(o_used.sem, o_used.done(g))
                        group_stats(g)

        def store_x():
            with nc.Block() as block:
                @block.sync
                def _(sp):
                    sp.dma_start(out, X[:, :]).then_inc(s_out, 16)
                    sp.wait_ge(s_out, 16)

        if stop == "C":
            store_x()
            return

        def route(tag, logits, p, q, w, sel, small_t, rank_row, E, pair_softmax):
            exp_ready, pair_ready, shifted_ready, diff_ready = (
                sem(n + tag) for n in ("exp_ready", "pair_ready", "shifted_ready", "diff_ready"))

            def wide(v):
                return v.unsqueeze(2).broadcast_to([P, B, E])

            m, m1, m2, w1 = (small_t[:, i, :] for i in range(4))
            ranks = rank_row.unsqueeze(1).broadcast_to([P, B, E])
            tt, red = nc.vector.tensor_tensor, nc.vector.tensor_reduce
            with nc.Block() as block:
                @block.vector
                def _(dve):
                    link(red(m, logits, AXX, ALU.max))
                    tt(logits, logits, wide(m), ALU.subtract).then_inc(shifted_ready, 1)
                    dve.wait_ge(exp_ready, 1)
                    link(red(m, p, AXX, ALU.add))
                    link(nc.vector.reciprocal(m, m))
                    link(tt(p, p, wide(m), ALU.mult))

                    def first_of_largest(largest, chosen):
                        link(red(largest, p, AXX, ALU.max))
                        link(tt(q, p, wide(largest), ALU.is_equal))
                        link(tt(w, q, ranks, ALU.mult))
                        link(red(m, w, AXX, ALU.max))
                        link(tt(chosen, w, wide(m), ALU.is_equal))

                    first_of_largest(m1, sel)
                    link(nc.vector.scalar_tensor_tensor(p, sel, -2.0, p, ALU.mult, ALU.add))
                    first_of_largest(m2, q)
                    if pair_softmax:
                        tt(m2, m2, m1, ALU.subtract).then_inc(diff_ready, 1)
                        dve.wait_ge(pair_ready, 1)
                        link(nc.vector.tensor_scalar(m, m2, 1.0, None, ALU.add))
                        link(nc.vector.reciprocal(w1, m))
                    else:
                        link(tt(m, m1, m2, ALU.add))
                        link(nc.vector.reciprocal(m, m))
                        link(tt(w1, m1, m, ALU.mult))
                        link(nc.vector.tensor_copy(w1, w1))
                    link(tt(m2, m2, w1 if pair_softmax else m, ALU.mult))
                    link(tt(sel, sel, wide(w1), ALU.mult))
                    link(tt(q, q, wide(m2), ALU.mult))
                    link(tt(sel, sel, q, ALU.add))

                @block.scalar
                def _(act):
                    act.wait_ge(shifted_ready, 1)
                    nc.scalar.activation(p, logits, ACT.Exp).then_inc(exp_ready, 1)
                    if pair_softmax:
                        act.wait_ge(diff_ready, 1)
                        nc.scalar.activation(m2, m2, ACT.Exp).then_inc(pair_ready, 1)

        finish_rstd("1")
        take = carve()
        ffn0_sb = take(FFN0_COLS)
        w3of = [[ffn0_sb[:, (l * E0 + e) * D:(l * E0 + e + 1) * D] for e in range(E0)] for l in range(3)]
        at = 3 * E0 * D
        b12 = [[ffn0_sb[:, at + l * E0 + e:at + l * E0 + e + 1] for e in range(E0)] for l in range(2)]
        b3rows = ffn0_sb[:, at + 2 * E0:at + 2 * E0 + D]
        logits0 = take(B, E0)
        prob0 = take(B, E0)
        tq0 = take(B, E0)
        tw0 = take(B, E0)
        mask0 = take(B, E0)
        small_t = take(4, B)
        stage = take.at[0]
        xn = take(2, W)
        rh = take(2, W)
        take = carve(stage)
        h1 = take(2, W)
        h2 = take(2, W)
        mk = take(2, NB * E0)
        mkT = take(2, W)

        with nc.Block() as block:
            xn_ready = steps("d_xn_ready", 2)
            t_done = steps("d_t_done", 2)
            xnT_ready = steps("d_xnT_ready", 2)
            r_done = steps("d_r_done", 2)
            rh_ready = steps("d_rh_ready", 2)
            l_done = steps("d_l_done", 2)
            l_used = steps("d_l_used", 2)
            psT, psR, psL = banks[0:2], banks[2:4], banks[4:6]

            @block.sync
            def _(sp):
                sp.dma_start(ffn0_sb, ffn0).then_inc(s_ffn0, 16)

            @block.vector
            def _(dve):
                for s in (xn_ready, l_used):
                    s.open(dve)
                bias = cst("rb2").unsqueeze(1).broadcast_to([P, NB, E0])
                with dve.Fori(0, G // 2) as it:
                    for u in range(2):
                        g = it * 2 + u
                        dve.wait_ge(t_done.sem, t_done.done(g - 2))
                        normalise(xn[:, u, :], g).then_inc(xn_ready.sem, 1)
                    for u in range(2):
                        g = it * 2 + u
                        dve.wait_ge(l_done.sem, l_done.done(g))
                        nc.vector.tensor_tensor(logits0[:, bass.ds(g * NB, NB), :],
                                                psL[u][:, 0:NB * E0].rearrange("p (a b) -> p a b", b=E0),
                                                bias, ALU.add).then_inc(l_used.sem, 1)

            @block.scalar
            def _(act):
                for s in (xnT_ready, rh_ready):
                    s.open(act)
                with act.Fori(0, G // 2) as it:
                    for u in range(2):
                        g = it * 2 + u
                        act.wait_ge(t_done.sem, t_done.done(g))
                        nc.scalar.copy(Y[:, cols(g)], psT[u][:, :]).then_inc(xnT_ready.sem, 1)
                    for u in range(2):
                        g = it * 2 + u
                        act.wait_ge(r_done.sem, r_done.done(g))
                        act.wait_ge(l_done.sem, l_done.done(g - 2))
                        nc.scalar.activation(rh[0:64, u, :], psR[u][0:64, :], ACT.Relu, bias=cst("rb1")[0:64, :])\
                            .then_inc(rh_ready.sem, 1)

            @block.tensor
            def _(pe):
                for s in (t_done, r_done, l_done):
                    s.open(pe)
                with pe.Fori(0, G // 2) as it:
                    for u in range(2):
                        g = it * 2 + u
                        pe.wait_ge(xn_ready.sem, xn_ready.done(g))
                        pe.wait_ge(xnT_ready.sem, xnT_ready.done(g - 2))
                        for b in range(NB):
                            last = nc.tensor.transpose(psT[u][:, b * P:(b + 1) * P], xn[:, u, b * D:(b + 1) * D], ident)
                        last.then_inc(t_done.sem, 1)
                    for u in range(2):
                        g = it * 2 + u
                        pe.wait_ge(xnT_ready.sem, xnT_ready.done(g))
                        pe.wait_ge(rh_ready.sem, rh_ready.done(g - 2))
                        nc.tensor.matmul(psR[u][0:64, :], cst("rw1"), Y[:, cols(g)], start=True, stop=True)\
                            .then_inc(r_done.sem, 1)
                    for u in range(2):
                        g = it * 2 + u
                        pe.wait_ge(rh_ready.sem, rh_ready.done(g))
                        pe.wait_ge(l_used.sem, l_used.done(g - 2))
                        for b in range(NB):
                            last = nc.tensor.matmul(psL[u][:, b * E0:(b + 1) * E0], rh[0:64, u, b * P:(b + 1) * P],
                                                    cst("rw2")[0:64, :], start=True, stop=True)
                        last.then_inc(l_done.sem, 1)

        route("0", logits0, prob0, tq0, tw0, mask0, small_t, cst("rank0"), E0, True)

        def mask_rows(pe, dve_ready, mk_slot, dst_bank, E):
            for b in range(NB):
                last = nc.tensor.transpose(dst_bank[0:E, b * P:(b + 1) * P], mk_slot[:, b * E:(b + 1) * E], ident)
            return last

        with nc.Block() as block:
            mk_ready = steps("e_mk_ready", 2)
            mt_done = steps("e_mt_done", 2)
            mkT_ready = steps("e_mkT_ready", 2)
            bias_done = steps("e_bias_done", 2)
            bias_used = steps("e_bias_used", 2)
            h1_done = steps("e_h1_done", 2)
            h1_ready = steps("e_h1_ready", 2)
            h2_done = steps("e_h2_done", 2)
            h2_ready = steps("e_h2_ready", 2)
            o_done = steps("e_o_done", 2)
            o_used = steps("e_o_used", 2)
            psH1, psH2, psO, psM, psB = banks[0:2], banks[2:4], banks[4:6], banks[6], banks[7]

            @block.tensor
            def _(pe):
                pe.wait_ge(s_ffn0, 16)
                for s in (mt_done, bias_done, h1_done, h2_done, o_done):
                    s.open(pe)

                def layer1(it, u, e):
                    n = it * (2 * E0) + (u * E0 + e)
                    pe.wait_ge(h1_ready.sem, h1_ready.done(n - 2))
                    nc.tensor.matmul(psH1[e % 2][:, :], w3of[0][e], Y[:, cols(it * 2 + u)], start=True, stop=True)\
                        .then_inc(h1_done.sem, 1)

                def layer2(it, u, e):
                    n = it * (2 * E0) + (u * E0 + e)
                    pe.wait_ge(h1_ready.sem, h1_ready.done(n))
                    pe.wait_ge(h2_ready.sem, h2_ready.done(n - 2))
                    nc.tensor.matmul(psH2[e % 2][:, :], w3of[1][e], h1[:, e % 2, :], start=True, stop=True)\
                        .then_inc(h2_done.sem, 1)

                def layer3(it, u, e):
                    n = it * (2 * E0) + (u * E0 + e)
                    pe.wait_ge(h2_ready.sem, h2_ready.done(n))
                    pe.wait_ge(o_used.sem, o_used.done(n - 2))
                    for b in range(NB):
                        last = nc.tensor.matmul(psO[e % 2][:, b * D:(b + 1) * D], h2[:, e % 2, b * P:(b + 1) * P],
                                                w3of[2][e], start=True, stop=True)
                    last.then_inc(o_done.sem, 1)

                with pe.Fori(0, G // 2) as it:
                    for u in range(2):
                        g = it * 2 + u
                        pe.wait_ge(mk_ready.sem, mk_ready.done(g))
                        pe.wait_ge(mkT_ready.sem, mkT_ready.done(g - 1))
                        for b in range(NB):
                            last = nc.tensor.transpose(psM[0:E0, b * P:(b + 1) * P], mk[:, u, b * E0:(b + 1) * E0], ident)
                        last.then_inc(mt_done.sem, 1)
                        layer1(it, u, 0)
                        layer1(it, u, 1)
                        pe.wait_ge(mkT_ready.sem, mkT_ready.done(g))
                        pe.wait_ge(bias_used.sem, bias_used.done(g - 1))
                        for b in range(NB):
                            last = nc.tensor.matmul(psB[:, b * D:(b + 1) * D], mkT[0:E0, u, b * P:(b + 1) * P],
                                                    b3rows[0:E0, :], start=True, stop=True)
                        last.then_inc(bias_done.sem, 1)
                        for e in range(E0 + 1):
                            if e < E0:
                                layer2(it, u, e)
                            if e + 2 < E0:
                                layer1(it, u, e + 2)
                            if e >= 1:
                                layer3(it, u, e - 1)

            @block.scalar
            def _(act):
                for s in (mkT_ready, h1_ready, h2_ready):
                    s.open(act)

                def relu1(it, u, e):
                    n = it * (2 * E0) + (u * E0 + e)
                    act.wait_ge(h1_done.sem, h1_done.done(n))
                    act.wait_ge(h2_done.sem, h2_done.done(n - 2))
                    nc.scalar.activation(h1[:, e % 2, :], psH1[e % 2][:, :], ACT.Relu, bias=b12[0][e])\
                        .then_inc(h1_ready.sem, 1)

                def relu2(it, u, e):
                    n = it * (2 * E0) + (u * E0 + e)
                    act.wait_ge(h2_done.sem, h2_done.done(n))
                    act.wait_ge(o_done.sem, o_done.done(n - 2))
                    nc.scalar.activation(h2[:, e % 2, :], psH2[e % 2][:, :], ACT.Relu, bias=b12[1][e])\
                        .then_inc(h2_ready.sem, 1)

                act.wait_ge(s_ffn0, 16)
                with act.Fori(0, G // 2) as it:
                    for u in range(2):
                        g = it * 2 + u
                        act.wait_ge(mt_done.sem, mt_done.done(g))
                        act.wait_ge(bias_done.sem, bias_done.done(g - 2))
                        nc.scalar.copy(mkT[0:E0, u, :], psM[0:E0, :]).then_inc(mkT_ready.sem, 1)
                        relu1(it, u, 0)
                        relu1(it, u, 1)
                        for e in range(E0):
                            relu2(it, u, e)
                            if e + 2 < E0:
                                relu1(it, u, e + 2)

            @block.vector
            def _(dve):
                for s in (bias_used, o_used):
                    s.open(dve)
                x_ready = sem("e_x_ready")
                with dve.Fori(0, G // 2) as it:
                    for u in range(2):
                        g = it * 2 + u
                        dve.wait_ge(bias_done.sem, bias_done.done(g))
                        nc.vector.tensor_tensor(X[:, cols(g)], X[:, cols(g)], psB[:, :], ALU.add)\
                            .then_inc(bias_used.sem, 1)
                        dve.wait_ge(bias_used.sem, bias_used.done(g))
                        for e in range(E0):
                            n = it * (2 * E0) + (u * E0 + e)
                            dve.wait_ge(o_done.sem, o_done.done(n))
                            for b in range(NB):
                                xb = X[:, bass.ds(g * W + b * D, D)]
                                ins = nc.vector.scalar_tensor_tensor(xb, psO[e % 2][:, b * D:(b + 1) * D],
                                                                     mask0[:, bass.ds(g * NB + b, 1), e], xb,
                                                                     ALU.mult, ALU.add)
                            ins.then_inc(o_used.sem, 1)
                            dve.wait_ge(o_used.sem, o_used.done(n))
                        group_stats(g)

            @block.gpsimd
            def _(pool):
                mk_ready.open(pool)
                with pool.Fori(0, G // 2) as it:
                    for u in range(2):
                        g = it * 2 + u
                        pool.wait_ge(mt_done.sem, mt_done.done(g - 2))
                        nc.gpsimd.tensor_copy(mk[:, u, :].rearrange("p (a b) -> p a b", b=E0),
                                              mask0[:, bass.ds(g * NB, NB), :]).then_inc(mk_ready.sem, 1)

        if stop == "D":
            store_x()
            return

        finish_rstd("2")
        take = carve()
        lstm_sb = take(LSTM_COLS)
        wih = [[lstm_sb[:, (p * 4 + k) * D:(p * 4 + k + 1) * D] for k in range(4)] for p in range(SKIPS)]
        whh = [[lstm_sb[:, ((SKIPS + p) * 4 + k) * D:((SKIPS + p) * 4 + k + 1) * D] for k in range(4)]
               for p in range(SKIPS)]
        at = SKIPS * 8 * D
        bih, bhh = lstm_sb[:, at:at + 4 * SKIPS], lstm_sb[:, at + 4 * SKIPS:at + 8 * SKIPS]
        bias_g = take(4 * SKIPS)
        stage = take.at[0]
        xn = take(2, W)
        xnT = take(2, W)
        v1 = take(2, W)
        h1T = take(2, W)
        v2 = take(2, W)
        take = carve(stage)
        gates = [[take(W) for _ in range(4)] for _ in range(2)]
        cell = [take(W) for _ in range(2)]
        tcell = [take(W) for _ in range(2)]
        hid = [take(W) for _ in range(2)]

        with nc.Block() as block:
            xn_ready = steps("g_xn_ready", 2)
            t_done = steps("g_t_done", 2)
            xnT_ready = steps("g_xnT_ready", 2)
            v1_done = steps("g_v1_done", 2)
            v1_ready = steps("g_v1_ready", 2)
            m1_done = steps("g_m1_done", 2)
            h1_ready = steps("g_h1_ready", 2)
            v2_done = steps("g_v2_done", 2)
            v2_ready = steps("g_v2_ready", 2)
            m2_done = steps("g_m2_done", 2)
            h2_ready = steps("g_h2_ready", 2)
            psA, psB = banks[0:2], banks[2:4]

            @block.sync
            def _(sp):
                sp.dma_start(lstm_sb, lstm).then_inc(s_lstm, 16)

            @block.vector
            def _(dve):
                for s in (xn_ready, v1_ready, v2_ready):
                    s.open(dve)

                def biased(dst, src, row):
                    return nc.vector.tensor_tensor(dst.rearrange("p (a b) -> p a b", b=D),
                                                   src.rearrange("p (a b) -> p a b", b=D),
                                                   row.unsqueeze(1).broadcast_to([P, NB, D]), ALU.add)

                with dve.Fori(0, G // 2) as it:
                    for u in range(2):
                        g = it * 2 + u
                        dve.wait_ge(t_done.sem, t_done.done(g - 2))
                        normalise(xn[:, u, :], g).then_inc(xn_ready.sem, 1)
                    for u in range(2):
                        g = it * 2 + u
                        dve.wait_ge(v1_done.sem, v1_done.done(g))
                        dve.wait_ge(m1_done.sem, m1_done.done(g - 2))
                        biased(v1[:, u, :], psB[u][:, :], cst("bg0")).then_inc(v1_ready.sem, 1)
                    for u in range(2):
                        g = it * 2 + u
                        dve.wait_ge(v2_done.sem, v2_done.done(g))
                        dve.wait_ge(m2_done.sem, m2_done.done(g - 2))
                        biased(v2[:, u, :], psB[u][:, :], cst("bg1")).then_inc(v2_ready.sem, 1)
                dve.wait_ge(s_lstm, 16)
                nc.vector.tensor_tensor(bias_g, bih, bhh, ALU.add)

            @block.scalar
            def _(act):
                for s in (xnT_ready, h1_ready, h2_ready):
                    s.open(act)
                with act.Fori(0, G // 2) as it:
                    for u in range(2):
                        g = it * 2 + u
                        act.wait_ge(t_done.sem, t_done.done(g))
                        act.wait_ge(v1_done.sem, v1_done.done(g - 2))
                        nc.scalar.copy(xnT[:, u, :], psA[u][:, :]).then_inc(xnT_ready.sem, 1)
                    for u in range(2):
                        g = it * 2 + u
                        act.wait_ge(m1_done.sem, m1_done.done(g))
                        act.wait_ge(v2_done.sem, v2_done.done(g - 2))
                        nc.scalar.activation(h1T[:, u, :], psA[u][:, :], ACT.Relu).then_inc(h1_ready.sem, 1)
                    for u in range(2):
                        g = it * 2 + u
                        act.wait_ge(m2_done.sem, m2_done.done(g))
                        nc.scalar.activation(Y[:, cols(g)], psA[u][:, :], ACT.Relu).then_inc(h2_ready.sem, 1)

            @block.tensor
            def _(pe):
                for s in (t_done, v1_done, m1_done, v2_done, m2_done):
                    s.open(pe)

                def four(dst, src, rhs, done):
                    for b in range(NB):
                        last = nc.tensor.matmul(dst[:, b * P:(b + 1) * P], src[:, b * P:(b + 1) * P], rhs,
                                                start=True, stop=True)
                    last.then_inc(done.sem, 1)

                with pe.Fori(0, G // 2) as it:
                    for u in range(2):
                        g = it * 2 + u
                        pe.wait_ge(xn_ready.sem, xn_ready.done(g))
                        pe.wait_ge(h2_ready.sem, h2_ready.done(g - 2))
                        for b in range(NB):
                            last = nc.tensor.transpose(psA[u][:, b * P:(b + 1) * P], xn[:, u, b * D:(b + 1) * D], ident)
                        last.then_inc(t_done.sem, 1)
                    for u in range(2):
                        pe.wait_ge(xnT_ready.sem, xnT_ready.done(it * 2 + u))
                        pe.wait_ge(v2_ready.sem, v2_ready.done(it * 2 + (u - 2)))
                        four(psB[u], xnT[:, u, :], cst("wg0"), v1_done)
                    for u in range(2):
                        pe.wait_ge(v1_ready.sem, v1_ready.done(it * 2 + u))
                        four(psA[u], v1[:, u, :], cst("adjT"), m1_done)
                    for u in range(2):
                        pe.wait_ge(h1_ready.sem, h1_ready.done(it * 2 + u))
                        four(psB[u], h1T[:, u, :], cst("wg1"), v2_done)
                    for u in range(2):
                        pe.wait_ge(v2_ready.sem, v2_ready.done(it * 2 + u))
                        four(psA[u], v2[:, u, :], cst("adjT"), m2_done)

        for p in range(1, SKIPS + 1):
            nw = P // p
            nbc = {1: 4, 2: 8, 3: 8, 4: 16}[p]
            n = nbc * nw
            turns = B // nbc // 2
            i_, f_, g_, o_ = range(4)

            def active(j):
                return (i_, g_, o_) if j == 0 else (i_, f_, g_, o_)

            with nc.Block() as block:
                gates_done = steps(f"l{p}_gates_done", 2 * p)
                gates_ready = steps(f"l{p}_gates_ready", 2 * p)
                cell_ready = steps(f"l{p}_cell_ready", 2 * p)
                tcell_ready = steps(f"l{p}_tcell_ready", 2 * p)
                hid_ready = steps(f"l{p}_hid_ready", 2 * p)

                def item(it, j, u):
                    return it * (2 * p) + (2 * j + u)

                def at_step(it, j, u):
                    return Y3[:, bass.ds((it * 2 + u) * nbc, nbc), j:j + (nw - 1) * p + 1:p]

                def bank(u, k):
                    return banks[4 * u + k][:, 0:n]

                @block.tensor
                def _(pe, p=p, n=n):
                    gates_done.open(pe)
                    with pe.Fori(0, turns) as it:
                        for j in range(p):
                            for u in range(2):
                                m = item(it, j, u)
                                pe.wait_ge(gates_ready.sem, gates_ready.done(m - 2))
                                for k in active(j):
                                    last = nc.tensor.matmul(bank(u, k).rearrange("p (a b) -> p a b", a=nbc),
                                                            wih[p - 1][k], at_step(it, j, u), start=True, stop=j == 0)
                                if j > 0:
                                    pe.wait_ge(hid_ready.sem, hid_ready.done(m - 2))
                                    for k in active(j):
                                        last = nc.tensor.matmul(bank(u, k), whh[p - 1][k], hid[u][:, 0:n],
                                                                start=False, stop=True)
                                last.then_inc(gates_done.sem, 1)

                @block.scalar
                def _(act, p=p, n=n):
                    gates_ready.open(act)
                    tcell_ready.open(act)
                    with act.Fori(0, turns) as it:
                        for j in range(p):
                            for u in range(2):
                                m = item(it, j, u)
                                act.wait_ge(gates_done.sem, gates_done.done(m))
                                act.wait_ge(hid_ready.sem, hid_ready.done(m - 2))
                                for k in active(j):
                                    last = nc.scalar.activation(
                                        gates[u][k][:, 0:n], bank(u, k), ACT.Tanh if k == g_ else ACT.Sigmoid,
                                        bias=bias_g[:, (p - 1) * 4 + k:(p - 1) * 4 + k + 1])
                                last.then_inc(gates_ready.sem, 1)
                                act.wait_ge(cell_ready.sem, cell_ready.done(m))
                                nc.scalar.activation(tcell[u][:, 0:n], cell[u][:, 0:n], ACT.Tanh)\
                                    .then_inc(tcell_ready.sem, 1)

                @block.vector
                def _(dve, p=p, n=n):
                    cell_ready.open(dve)
                    hid_ready.open(dve)
                    part_ready = steps(f"l{p}_part_ready", 2 * p)
                    part_ready.open(dve)
                    with dve.Fori(0, turns) as it:
                        for j in range(p):
                            for u in range(2):
                                m = item(it, j, u)
                                i, f, g, o = (gates[u][k][:, 0:n] for k in range(4))
                                c = cell[u][:, 0:n]
                                dve.wait_ge(gates_ready.sem, gates_ready.done(m))
                                if j == 0:
                                    dve.wait_ge(tcell_ready.sem, tcell_ready.done(m - 2))
                                    nc.vector.tensor_tensor(c, i, g, ALU.mult).then_inc(cell_ready.sem, 1)
                                else:
                                    nc.vector.tensor_tensor(i, i, g, ALU.mult)
                                    nc.vector.tensor_tensor(c, f, c, ALU.mult).then_inc(part_ready.sem, 1)
                                    dve.wait_ge(part_ready.sem,
                                                part_ready.done(it * (2 * (p - 1)) + (2 * (j - 1) + u)))
                                    nc.vector.tensor_tensor(c, c, i, ALU.add).then_inc(cell_ready.sem, 1)
                                dve.wait_ge(tcell_ready.sem, tcell_ready.done(m))
                                t = tcell[u][:, 0:n]
                                if j < p - 1:
                                    nc.vector.tensor_tensor(hid[u][:, 0:n], o, t, ALU.mult).then_inc(hid_ready.sem, 1)
                                else:
                                    nc.vector.tensor_tensor(at_step(it, j, u), o.rearrange("p (a b) -> p a b", a=nbc),
                                                            t.rearrange("p (a b) -> p a b", a=nbc), ALU.mult)\
                                        .then_inc(hid_ready.sem, 1)

        take = carve(stage)
        hT = take(2, W)
        with nc.Block() as block:
            h_ready = steps("h_h_ready", 2)
            t_done = steps("h_t_done", 2)
            x_ready = steps("h_x_ready", 2)
            psT = banks[0:2]

            @block.gpsimd
            def _(pool):
                h_ready.open(pool)
                with pool.Fori(0, G // 2) as it:
                    for u in range(2):
                        g = it * 2 + u
                        pool.wait_ge(t_done.sem, t_done.done(g - 2))
                        nc.gpsimd.tensor_copy(hT[:, u, :], Y[:, cols(g)]).then_inc(h_ready.sem, 1)

            @block.tensor
            def _(pe):
                t_done.open(pe)
                with pe.Fori(0, G // 2) as it:
                    for u in range(2):
                        g = it * 2 + u
                        pe.wait_ge(h_ready.sem, h_ready.done(g))
                        pe.wait_ge(x_ready.sem, x_ready.done(g - 2))
                        for b in range(NB):
                            last = nc.tensor.transpose(psT[u][:, b * D:(b + 1) * D], hT[:, u, b * P:(b + 1) * P], ident)
                        last.then_inc(t_done.sem, 1)

            @block.vector
            def _(dve):
                x_ready.open(dve)
                with dve.Fori(0, G // 2) as it:
                    for u in range(2):
                        g = it * 2 + u
                        dve.wait_ge(t_done.sem, t_done.done(g))
                        nc.vector.tensor_tensor(X[:, cols(g)], X[:, cols(g)], psT[u][:, :], ALU.add)\
                            .then_inc(x_ready.sem, 1)
                        dve.wait_ge(x_ready.sem, x_ready.done(g))
                        group_stats(g)

        if stop == "G":
            store_x()
            return

        finish_rstd("3")
        take = carve()
        ffn1_sb = take(FFN1_COLS)
        E9 = E1 + 1
        w1of = [[ffn1_sb[:, (e * FK + k) * D:(e * FK + k + 1) * D] for k in range(FK)] for e in range(E9)]
        at = E9 * FK * D
        w2of = [[ffn1_sb[:, at + (e * FK + k) * D:at + (e * FK + k + 1) * D] for k in range(FK)] for e in range(E9)]
        at = 2 * E9 * FK * D
        b1of = [[ffn1_sb[:, at + e * FK + k:at + e * FK + k + 1] for k in range(FK)] for e in range(E9)]
        b2rows = ffn1_sb[:, at + E9 * FK:at + E9 * FK + D]
        mask1 = take(B, E1)
        stage = take.at[0]
        logits1 = take(B, E1)
        prob1 = take(B, E1)
        tq1 = take(B, E1)
        tw1 = take(B, E1)
        small_t = take(4, B)
        xn = take(W)
        xnT = take(2, W)
        take = carve(stage)
        hf = take(2, FK, W)
        mk = take(2, NB * E9)
        mkT = take(2, W)

        with nc.Block() as block:
            xn_ready = steps("r_xn_ready", 1)
            t_done = steps("r_t_done", 1)
            xnT_ready = steps("r_xnT_ready", 2)
            kept = steps("r_kept", 2)
            l_done = steps("r_l_done", 2)
            l_used = steps("r_l_used", 2)
            psT, psL = banks[0:2], banks[2:4]

            @block.sync
            def _(sp):
                sp.dma_start(ffn1_sb, ffn1).then_inc(s_ffn1, 16)

            @block.vector
            def _(dve):
                for s in (xn_ready, l_used):
                    s.open(dve)
                with dve.Fori(0, G // 2) as it:
                    for u in range(2):
                        g = it * 2 + u
                        dve.wait_ge(t_done.sem, t_done.done(g - 1))
                        normalise(xn, g).then_inc(xn_ready.sem, 1)
                    for u in range(2):
                        g = it * 2 + u
                        dve.wait_ge(l_done.sem, l_done.done(g))
                        nc.vector.tensor_copy(logits1[:, bass.ds(g * NB, NB), :],
                                              psL[u][:, 0:NB * E1].rearrange("p (a b) -> p a b", b=E1))\
                            .then_inc(l_used.sem, 1)

            @block.scalar
            def _(act):
                xnT_ready.open(act)
                with act.Fori(0, G // 2) as it:
                    for u in range(2):
                        g = it * 2 + u
                        act.wait_ge(t_done.sem, t_done.done(g))
                        act.wait_ge(l_done.sem, l_done.done(g - 2))
                        act.wait_ge(kept.sem, kept.done(g - 2))
                        nc.scalar.copy(xnT[:, u, :], psT[u][:, :]).then_inc(xnT_ready.sem, 1)

            @block.gpsimd
            def _(pool):
                kept.open(pool)
                with pool.Fori(0, G // 2) as it:
                    for u in range(2):
                        g = it * 2 + u
                        pool.wait_ge(xnT_ready.sem, xnT_ready.done(g))
                        nc.gpsimd.tensor_copy(Y[:, cols(g)], xnT[:, u, :]).then_inc(kept.sem, 1)

            @block.tensor
            def _(pe):
                for s in (t_done, l_done):
                    s.open(pe)
                with pe.Fori(0, G // 2) as it:
                    for u in range(2):
                        g = it * 2 + u
                        pe.wait_ge(xn_ready.sem, xn_ready.done(g))
                        pe.wait_ge(xnT_ready.sem, xnT_ready.done(g - 2))
                        for b in range(NB):
                            last = nc.tensor.transpose(psT[u][:, b * P:(b + 1) * P], xn[:, b * D:(b + 1) * D], ident)
                        last.then_inc(t_done.sem, 1)
                    for u in range(2):
                        g = it * 2 + u
                        pe.wait_ge(xnT_ready.sem, xnT_ready.done(g))
                        pe.wait_ge(l_used.sem, l_used.done(g - 2))
                        for b in range(NB):
                            last = nc.tensor.matmul(psL[u][:, b * E1:(b + 1) * E1], xnT[:, u, b * P:(b + 1) * P],
                                                    cst("wr"), start=True, stop=True)
                        last.then_inc(l_done.sem, 1)

        route("1", logits1, prob1, tq1, tw1, mask1, small_t, cst("rank1"), E1, False)

        with nc.Block() as block:
            mk_ready = steps("f_mk_ready", 2)
            mt_done = steps("f_mt_done", 2)
            mkT_ready = steps("f_mkT_ready", 2)
            bias_done = steps("f_bias_done", 2)
            bias_used = steps("f_bias_used", 2)
            up_done = steps("f_up_done", 8)
            gelu_ready = steps("f_gelu_ready", 8)
            o_done = steps("f_o_done", 2)
            o_used = steps("f_o_used", 2)
            psU, psO, psM, psB = banks[0:4], banks[4:6], banks[6], banks[7]
            PER = 2 * E9

            @block.tensor
            def _(pe):
                pe.wait_ge(s_ffn1, 16)
                for s in (mt_done, bias_done, up_done, o_done):
                    s.open(pe)

                def up(it, v):
                    u, e = divmod(v, E9)
                    for k in range(FK):
                        n = it * (PER * FK) + (v * FK + k)
                        pe.wait_ge(gelu_ready.sem, gelu_ready.done(n - FK))
                        nc.tensor.matmul(psU[k][:, :], w1of[e][k], Y[:, cols(it * 2 + u)], start=True, stop=True)\
                            .then_inc(up_done.sem, 1)

                def down(it, v):
                    u, e = divmod(v, E9)
                    pe.wait_ge(gelu_ready.sem, gelu_ready.done(it * (PER * FK) + (v * FK + FK - 1)))
                    pe.wait_ge(o_used.sem, o_used.done(it * PER + (v - 2)))
                    for b in range(NB):
                        for k in range(FK):
                            last = nc.tensor.matmul(psO[v % 2][:, b * D:(b + 1) * D], hf[:, v % 2, k, b * P:(b + 1) * P],
                                                    w2of[e][k], start=k == 0, stop=k == FK - 1)
                    last.then_inc(o_done.sem, 1)

                with pe.Fori(0, G // 2) as it:
                    for v in range(PER + 1):
                        if v < PER:
                            up(it, v)
                        if v < PER and v % E9 == 0:
                            u = v // E9
                            g = it * 2 + u
                            pe.wait_ge(mk_ready.sem, mk_ready.done(g))
                            pe.wait_ge(mkT_ready.sem, mkT_ready.done(g - 1))
                            for b in range(NB):
                                last = nc.tensor.transpose(psM[0:E9, b * P:(b + 1) * P], mk[:, u, b * E9:(b + 1) * E9],
                                                           ident)
                            last.then_inc(mt_done.sem, 1)
                        if v >= 1:
                            down(it, v - 1)
                        if v < PER and v % E9 == 1:
                            u = v // E9
                            g = it * 2 + u
                            pe.wait_ge(mkT_ready.sem, mkT_ready.done(g))
                            pe.wait_ge(bias_used.sem, bias_used.done(g - 1))
                            for b in range(NB):
                                last = nc.tensor.matmul(psB[:, b * D:(b + 1) * D], mkT[0:E9, u, b * P:(b + 1) * P],
                                                        b2rows[0:E9, :], start=True, stop=True)
                            last.then_inc(bias_done.sem, 1)

            @block.scalar
            def _(act):
                act.wait_ge(s_ffn1, 16)
                for s in (gelu_ready,):
                    s.open(act)
                with act.Fori(0, G // 2) as it:
                    for v in range(PER):
                        u, e = divmod(v, E9)
                        act.wait_ge(o_done.sem, o_done.done(it * PER + (v - 2)))
                        for k in range(FK):
                            n = it * (PER * FK) + (v * FK + k)
                            act.wait_ge(up_done.sem, up_done.done(n))
                            nc.scalar.activation(hf[:, v % 2, k, :], psU[k][:, :], ACT.Gelu, bias=b1of[e][k])\
                                .then_inc(gelu_ready.sem, 1)

            @block.vector
            def _(dve):
                for s in (mkT_ready, bias_used, o_used):
                    s.open(dve)
                with dve.Fori(0, G // 2) as it:
                    for v in range(PER):
                        u, e = divmod(v, E9)
                        g = it * 2 + u
                        if e == 0:
                            dve.wait_ge(mt_done.sem, mt_done.done(g))
                            dve.wait_ge(bias_done.sem, bias_done.done(g - 2))
                            nc.vector.tensor_copy(mkT[0:E9, u, :], psM[0:E9, :]).then_inc(mkT_ready.sem, 1)
                        n = it * PER + v
                        dve.wait_ge(o_done.sem, o_done.done(n))
                        for b in range(NB):
                            xb = X[:, bass.ds(g * W + b * D, D)]
                            po = psO[v % 2][:, b * D:(b + 1) * D]
                            if e < E1:
                                ins = nc.vector.scalar_tensor_tensor(xb, po, mask1[:, bass.ds(g * NB + b, 1), e], xb,
                                                                     ALU.mult, ALU.add)
                            else:
                                ins = nc.vector.tensor_tensor(xb, xb, po, ALU.add)
                        ins.then_inc(o_used.sem, 1)
                        dve.wait_ge(o_used.sem, o_used.done(n))
                        if e == 0:
                            dve.wait_ge(bias_done.sem, bias_done.done(g))
                            nc.vector.tensor_tensor(X[:, cols(g)], X[:, cols(g)], psB[:, :], ALU.add)\
                                .then_inc(bias_used.sem, 1)
                            dve.wait_ge(bias_used.sem, bias_used.done(g))

            @block.gpsimd
            def _(pool):
                mk_ready.open(pool)
                ones_ready = sem("f_ones_ready")
                nc.gpsimd.memset(mk, 1.0).then_inc(ones_ready, 1)
                pool.wait_ge(ones_ready, 1)
                with pool.Fori(0, G // 2) as it:
                    for u in range(2):
                        g = it * 2 + u
                        pool.wait_ge(mt_done.sem, mt_done.done(g - 2))
                        nc.gpsimd.tensor_copy(mk[:, u, :].rearrange("p (a b) -> p a b", b=E9)[:, :, 0:E1],
                                              mask1[:, bass.ds(g * NB, NB), :]).then_inc(mk_ready.sem, 1)

            @block.sync
            def _(sp):
                with sp.Fori(0, G) as g:
                    sp.wait_ge(o_used.sem, o_used.done(g * E9 + (E9 - 1)))
                    sp.dma_start(out[:, cols(g)], X[:, cols(g)]).then_inc(s_out, 16)
                sp.wait_ge(s_out, 16 * G)


def kernel(**inputs):
    import concourse.bacc as bacc
    from concourse.bass_utils import run_bass_kernel_spmd

    a = {k: np.asarray(v) for k, v in inputs.items()}

    def column(v):
        return v.reshape(-1, 1)

    def rows(v, n=P):
        return np.broadcast_to(v.reshape(1, -1), (n, v.size))

    def pad(v):
        full = np.zeros((P, v.shape[1]), np.float32)
        full[:v.shape[0]] = v
        return full

    ahead = np.zeros((D, HEADS), np.float32)
    for h in range(HEADS):
        ahead[h * (D // HEADS):(h + 1) * (D // HEADS), h] = a["L0_gnn_a"][h]
    idx = np.arange(P, dtype=np.float32)
    parts = {
        "ident": np.eye(P, dtype=np.float32),
        "iota": rows(np.arange(EDGES, dtype=np.float32)),
        "pidx": column(idx),
        "eidx": np.stack([idx + P * c for c in range(EC)], 1),
        "ones": np.ones((P, P), np.float32),
        "rank0": rows(np.arange(E0, 0, -1, dtype=np.float32)),
        "rank1": rows(np.arange(E1, 0, -1, dtype=np.float32)),
        "wq": a["L0_gnn_W_lin"].T, "wv": a["L0_gnn_W_val"].T, "wout": a["L0_gnn_W_out"].T,
        "ahead": ahead, "adj": a["adj"], "adjT": a["adj"].T,
        "rw1": a["L0_ffn_router_w1"], "rb1": pad(column(a["L0_ffn_router_b1"])),
        "rw2": pad(a["L0_ffn_router_w2"]), "rb2": rows(a["L0_ffn_router_b2"]),
        "wg0": a["L1_gnn_Wg0"], "bg0": rows(a["L1_gnn_bg0"]),
        "wg1": a["L1_gnn_Wg1"], "bg1": rows(a["L1_gnn_bg1"]), "wr": a["L1_ffn_Wr"],
    }
    small = np.concatenate([parts[n] for n, _ in SMALL], 1)
    sd = np.stack([a["L0_gnn_src"], a["L0_gnn_dst"]])
    edges = np.concatenate([rows(sd), sd.reshape(2, EC, P).transpose(2, 1, 0).reshape(P, 2 * EC)], 1)
    ffn0 = np.concatenate(
        [a["L0_ffn_expert_w1"].transpose(1, 0, 2).reshape(D, -1),
         a["L0_ffn_expert_w2"].transpose(1, 0, 2).reshape(D, -1),
         a["L0_ffn_expert_w3"].transpose(1, 0, 2).reshape(D, -1),
         a["L0_ffn_expert_b1"].T, a["L0_ffn_expert_b2"].T, pad(a["L0_ffn_expert_b3"])], 1)
    lstm = np.concatenate(
        [a["L1_gnn_Wih"].transpose(2, 0, 1).reshape(D, -1), a["L1_gnn_Whh"].transpose(2, 0, 1).reshape(D, -1),
         a["L1_gnn_bih"].reshape(-1, D).T, a["L1_gnn_bhh"].reshape(-1, D).T], 1)
    w1 = np.concatenate([a["L1_ffn_W1p"], a["L1_ffn_W1s"][None]], 0)
    w2 = np.concatenate([a["L1_ffn_W2p"], a["L1_ffn_W2s"][None]], 0)
    b1 = np.concatenate([a["L1_ffn_b1p"], a["L1_ffn_b1s"][None]], 0)
    b2 = np.concatenate([a["L1_ffn_b2p"], a["L1_ffn_b2s"][None]], 0)
    ffn1 = np.concatenate(
        [w1.transpose(1, 0, 2).reshape(D, -1),
         w2.reshape(E1 + 1, FK, D, D).transpose(2, 0, 1, 3).reshape(D, -1),
         b1.reshape(-1, D).T, pad(b2)], 1)
    arrays = {"xT_dram": a["x"].transpose(1, 0, 2).reshape(P, B * D), "small_dram": small, "edges_dram": edges,
              "ffn0_dram": ffn0, "lstm_dram": lstm, "ffn1_dram": ffn1}
    arrays = {k: np.ascontiguousarray(v) for k, v in arrays.items()}

    nc = bacc.Bacc("TRN2", target_bir_lowering=False, num_devices=1)
    args = [nc.dram_tensor(n, v.shape, mybir.dt.from_np(v.dtype), kind="ExternalInput").ap() for n, v in arrays.items()]
    out = nc.dram_tensor("out_0_dram", (P, B * D), F32, kind="ExternalOutput").ap()
    build(nc, *args, out, STOP)
    r = run_bass_kernel_spmd(nc, [arrays], core_ids=[0])
    return r.results[0]["out_0_dram"].reshape(P, B, D).transpose(1, 0, 2)
```

```python
from contextlib import ExitStack

import numpy as np

import concourse.bass as bass
from concourse import mybir

STOP = "H"

ALU = mybir.AluOpType
ACT = mybir.ActivationFunctionType
AXX = mybir.AxisListType.X
F32 = mybir.dt.float32
I32 = mybir.dt.int32
U32 = mybir.dt.uint32
F32R = mybir.dt.float32r

P = 128
B = 128
D = 128
NB = 4
G = B // NB
W = NB * D
HEADS = 4
EDGES = 256
EC = EDGES // P
E0 = 6
E1 = 8
FK = 4
SKIPS = 4
BIG = 3.0e38
LN_EPS = 1e-5
TOKENS = B * P
BLOCK = 512
NQ = BLOCK // P
BLOCKS = 2 * TOKENS // BLOCK + E1
SLOTS = BLOCKS * BLOCK
ROW = 132
LOG_EPS = 1e-8

SMALL = [("ident", 128), ("iota", 256), ("pidx", 1), ("eidx", EC), ("ones", 128),
         ("below", P), ("blk", BLOCKS), ("blkrow", BLOCKS), ("rank0", E0), ("rank1", E1),
         ("wq", D), ("wv", D), ("wout", D), ("ahead", HEADS), ("adj", P), ("adjT", P),
         ("rw1", 64), ("rb1", 1), ("rw2", E0), ("rb2", E0),
         ("wg0", D), ("bg0", D), ("wg1", D), ("bg1", D), ("wr", E1)]
SMALL_AT = {}
SMALL_COLS = 0
for _name, _n in SMALL:
    SMALL_AT[_name] = (SMALL_COLS, SMALL_COLS + _n)
    SMALL_COLS += _n
FFN0_COLS = E0 * 3 * D + E0 * 2 + D
LSTM_COLS = SKIPS * 8 * D + SKIPS * 8
EW = 2 * FK * D
FFN1_COLS = (E1 + 1) * EW + (E1 + 1) * (FK + 1)


class Steps:

    def __init__(self, sem, ahead=0):
        self.sem, self.ahead = sem, ahead

    def open(self, eng):
        eng.sem_inc(self.sem, self.ahead)

    def done(self, n):
        return n + (self.ahead + 1)


def build(nc, xT, small, edges, ids, ffn0, lstm, ffn1, out, stop):
    order = "CDGH"
    upto = order.index(stop)
    ctx = ExitStack()
    with ctx:
        def sb(name, shape, dt=F32):
            return ctx.enter_context(nc.sbuf_tensor(name, shape, dt))

        phase_sems = []

        def kept_sem(name):
            return ctx.enter_context(nc.semaphore(name))

        def sem(name):
            phase_sems.append(nc.alloc_semaphore(name=name))
            return phase_sems[-1]

        def renew_semaphores():
            nc.clear_and_free_semaphores(phase_sems)
            phase_sems.clear()
            nc.all_engine_barrier()

        def steps(name, ahead=0):
            return Steps(sem(name), ahead)

        X = sb("X", [P, B * D])
        small_sb = sb("small_sb", [P, SMALL_COLS])
        STAT = sb("STAT", [P, B, 6])
        MEAN = sb("MEAN", [P, B])
        RSTD = sb("RSTD", [P, B])
        ids_sb = sb("ids_sb", [P, 2 * B + NQ], I32)
        fill = sb("fill", [P, NQ, ROW])
        NT = sb("NT", [P, 2, B])
        banks = [ctx.enter_context(nc.psum_tensor(f"bank{i}", [P, 512], F32)) for i in range(8)]

        def cst(name):
            a, b = SMALL_AT[name]
            return small_sb[:, a:b]

        scopes = []

        def free(n=1):
            for _ in range(n):
                scopes.pop().close()

        def carve():
            scope = ExitStack()
            scopes.append(scope)

            def take(*shape, dt=F32):
                named[0] += 1
                t = scope.enter_context(nc.sbuf_tensor(f"t{named[0]}", [P, *shape], dt))
                return t[tuple([slice(None)] * (len(shape) + 1))]
            return take

        named = [0]

        ident = cst("ident")
        X3 = X[:, :].rearrange("p (b d) -> p b d", d=D)

        s_small = kept_sem("s_small")
        s_edges = kept_sem("s_edges")
        s_ids = kept_sem("s_ids")
        s_x = [kept_sem(f"s_x{i}") for i in range(8)]
        s_ffn0 = kept_sem("s_ffn0")
        s_lstm = kept_sem("s_lstm")
        s_fill = kept_sem("s_fill")
        rows_dram = nc.dram_tensor("rows_scratch", (SLOTS, ROW), F32, kind="Internal").ap()
        outs_dram = nc.dram_tensor("outs_scratch", (2 * TOKENS + SLOTS, D), F32, kind="Internal").ap()
        s_out = kept_sem("s_out")
        s_chain = kept_sem("s_chain")
        chained = [0]

        def link(ins):
            chained[0] += 1
            ins.then_inc(s_chain, 1)
            nc.vector.wait_ge(s_chain, chained[0])

        def group_stats(g):
            for b in range(NB):
                ins = nc.vector.bn_stats(STAT[:, bass.ds(g * NB + b, 1), :], X3[:, bass.ds(g * NB + b, 1), :])
            return ins

        with nc.Block() as block:
            stat_ready = sem("stat_ready0")

            @block.sync
            def _(sp):
                sp.dma_start(small_sb[:, :], small).then_inc(s_small, 16)
                for i in range(8):
                    n = B * D // 8
                    sp.dma_start(X[:, i * n:(i + 1) * n], xT[:, i * n:(i + 1) * n]).then_inc(s_x[i], 16)

            @block.vector
            def _(dve):
                for i in range(8):
                    dve.wait_ge(s_x[i], 16)
                    with dve.Fori(0, G // 8) as it:
                        group_stats(it + i * (G // 8)).then_inc(stat_ready, 1)
                dve.wait_ge(stat_ready, G)

        def finish_rstd(tag):
            ve_ready, root_ready = sem("ve" + tag), sem("root" + tag)
            with nc.Block() as block:
                @block.vector
                def _(dve):
                    even, odd = STAT[:, :, 1], STAT[:, :, 4]
                    link(nc.vector.tensor_tensor(MEAN[:, :], even, odd, ALU.add))
                    link(nc.vector.tensor_scalar(MEAN[:, :], MEAN[:, :], 0.5, None, ALU.mult))
                    link(nc.vector.tensor_tensor(NT[:, 1, :], even, odd, ALU.subtract))
                    link(nc.vector.tensor_tensor(NT[:, 1, :], NT[:, 1, :], NT[:, 1, :], ALU.mult))
                    link(nc.vector.tensor_scalar(NT[:, 1, :], NT[:, 1, :], 0.25, LN_EPS, ALU.mult, ALU.add))
                    link(nc.vector.tensor_tensor(NT[:, 0, :], STAT[:, :, 2], STAT[:, :, 5], ALU.add))
                    nc.vector.scalar_tensor_tensor(NT[:, 0, :], NT[:, 0, :], 1.0 / D, NT[:, 1, :], ALU.mult, ALU.add)\
                        .then_inc(ve_ready, 1)
                    dve.wait_ge(root_ready, 1)
                    link(nc.vector.reciprocal(RSTD[:, :], NT[:, 1, :]))
                    link(nc.vector.tensor_tensor(NT[:, 1, :], RSTD[:, :], RSTD[:, :], ALU.mult))
                    link(nc.vector.tensor_tensor(NT[:, 1, :], NT[:, 1, :], NT[:, 0, :], ALU.mult))
                    link(nc.vector.tensor_scalar(NT[:, 1, :], NT[:, 1, :], -0.5, 1.5, ALU.mult, ALU.add))
                    link(nc.vector.tensor_tensor(RSTD[:, :], RSTD[:, :], NT[:, 1, :], ALU.mult))

                @block.scalar
                def _(act):
                    act.wait_ge(ve_ready, 1)
                    nc.scalar.activation(NT[:, 1, :], NT[:, 0, :], ACT.Sqrt).then_inc(root_ready, 1)

        def normalise(dst, g):
            for b in range(NB):
                ins = nc.vector.tensor_scalar(dst[:, b * D:(b + 1) * D], X3[:, bass.ds(g * NB + b, 1), :],
                                              MEAN[:, bass.ds(g * NB + b, 1)], RSTD[:, bass.ds(g * NB + b, 1)],
                                              ALU.subtract, ALU.mult)
            return ins

        def cols(g):
            return bass.ds(g * W, W)

        take = carve()
        Y = take(B * D)
        Y3 = Y.rearrange("p (b d) -> p b d", d=D)
        take = carve()
        sd_int = take(2 * EDGES + 2 * EC, dt=I32)
        sd = take(2 * EDGES + 2 * EC)
        perm = take(EC, EDGES)
        srcB = take(EC, P)
        dstB = take(EC, P)
        rowS = take(EDGES)
        rowD = take(EDGES)
        colSD = take(EC, 2)
        ohsT = take(EDGES)
        ohdT = take(EDGES)
        ohsum = take(EDGES)
        ohs = take(EC, P)
        ohd = take(EC, P)
        reset = take(EDGES)
        same = take(EC, EDGES)
        lastsel = take(EC, EDGES)
        key = take(EDGES)
        keyc = take(EC)
        rank = take(EC)
        later = take(EC)
        islast = take(EC)
        adjv = take(EC)
        logadj = take(EC)
        logeps = take(1)
        tmp = take(EDGES)
        S = take(EC, B * HEADS)
        att = take(EC, B * HEADS)

        with nc.Block() as block:
            fill_ready = sem("fill_ready")
            perm_ready, sorted_done, sorted_ready, oh_ready, adj_done, adj_ready = (
                sem(n) for n in ("perm_ready", "sorted_done", "sorted_ready", "oh_ready", "adj_done", "adj_ready"))

            @block.sync
            def _(sp):
                sp.dma_start(sd_int, edges).then_inc(s_edges, 16)
                sp.dma_start(ids_sb[:, :], ids).then_inc(s_ids, 16)
                sp.wait_ge(fill_ready, 2)
                with sp.Fori(0, BLOCKS) as j:
                    sp.dma_start(rows_dram.rearrange("(n q p) c -> p n q c", p=P, q=NQ)[:, bass.ds(j, 1)],
                                 fill[:, :, :]).then_inc(s_fill, 16)

            @block.gpsimd
            def _(pool):
                nc.gpsimd.memset(fill[:, :, :], 0.0).then_inc(fill_ready, 1)
                pool.wait_ge(fill_ready, 1)
                pool.wait_ge(s_ids, 16)
                nc.gpsimd.tensor_copy(fill[:, :, D].bitcast(I32), ids_sb[:, 2 * B:2 * B + NQ])\
                    .then_inc(fill_ready, 1)

            @block.vector
            def _(dve):
                dve.wait_ge(s_small, 16)
                dve.wait_ge(s_edges, 16)
                iota = cst("iota")
                ones = cst("ones")
                link(nc.vector.memset(logeps, LOG_EPS))
                link(nc.vector.tensor_copy(sd, sd_int))
                link(nc.vector.scalar_tensor_tensor(key, sd[:, 0:EDGES], float(EDGES), iota, ALU.mult, ALU.add))
                for c in range(EC):
                    scol = sd[:, 2 * EDGES + 2 * c:2 * EDGES + 2 * c + 1]
                    dcol = sd[:, 2 * EDGES + 2 * c + 1:2 * EDGES + 2 * c + 2]
                    link(nc.vector.scalar_tensor_tensor(keyc[:, c:c + 1], scol, float(EDGES), cst("eidx")[:, c:c + 1],
                                                        ALU.mult, ALU.add))
                    link(nc.vector.tensor_scalar(tmp, key, keyc[:, c:c + 1], None, ALU.is_lt))
                    link(nc.vector.reduce_sum(rank[:, c:c + 1], tmp, AXX))
                    link(nc.vector.tensor_scalar(perm[:, c, :], iota, rank[:, c:c + 1], None, ALU.is_equal))
                    link(nc.vector.tensor_scalar(srcB[:, c, :], ones, scol, None, ALU.mult))
                    ins = nc.vector.tensor_scalar(dstB[:, c, :], ones, dcol, None, ALU.mult)
                    link(ins)
                nc.vector.tensor_copy(tmp, key).then_inc(perm_ready, 1)
                dve.wait_ge(sorted_done, 1)
                link(nc.vector.tensor_copy(rowS, banks[0][:, 0:EDGES]))
                link(nc.vector.tensor_copy(rowD, banks[1][:, 0:EDGES]))
                link(nc.vector.tensor_copy(colSD.rearrange("p a b -> p (a b)"), banks[2][:, 0:2 * EC]))
                link(nc.vector.tensor_scalar(ohsT, rowS, cst("pidx"), None, ALU.is_equal))
                link(nc.vector.tensor_scalar(ohdT, rowD, cst("pidx"), None, ALU.is_equal))
                link(nc.vector.tensor_tensor(ohsum, ohsT, ohdT, ALU.add))
                link(nc.vector.memset(reset, 0.0))
                link(nc.vector.tensor_tensor(reset[:, 1:EDGES], rowS[:, 1:EDGES], rowS[:, 0:EDGES - 1], ALU.not_equal))
                link(nc.vector.tensor_scalar(reset, reset, -BIG, None, ALU.mult))
                for c in range(EC):
                    link(nc.vector.tensor_scalar(ohs[:, c, :], iota[:, 0:P], colSD[:, c, 0:1], None, ALU.is_equal))
                    link(nc.vector.tensor_scalar(ohd[:, c, :], iota[:, 0:P], colSD[:, c, 1:2], None, ALU.is_equal))
                    link(nc.vector.tensor_scalar(same[:, c, :], rowS, colSD[:, c, 0:1], None, ALU.is_equal))
                    link(nc.vector.tensor_scalar(tmp, iota, cst("eidx")[:, c:c + 1], None, ALU.is_gt))
                    link(nc.vector.tensor_tensor(tmp, tmp, same[:, c, :], ALU.mult))
                    link(nc.vector.reduce_sum(later[:, c:c + 1], tmp, AXX))
                    link(nc.vector.tensor_scalar(islast[:, c:c + 1], later[:, c:c + 1], 0.0, None, ALU.is_equal))
                    link(nc.vector.tensor_scalar(lastsel[:, c, :], same[:, c, :], islast[:, c:c + 1], None, ALU.mult))
                nc.vector.tensor_copy(tmp, key).then_inc(oh_ready, 1)
                dve.wait_ge(adj_done, 1)
                for c in range(EC):
                    link(nc.vector.tensor_tensor(tmp[:, 0:P], banks[3][:, c * P:(c + 1) * P], ohd[:, c, :], ALU.mult))
                    link(nc.vector.reduce_sum(adjv[:, c:c + 1], tmp[:, 0:P], AXX))
                nc.vector.tensor_copy(tmp, key).then_inc(adj_ready, 1)

            @block.tensor
            def _(pe):
                pe.wait_ge(s_small, 16)
                pe.wait_ge(perm_ready, 1)
                for dst, src in ((banks[0], srcB), (banks[1], dstB)):
                    for c in range(EC):
                        nc.tensor.matmul(dst[:, 0:EDGES], src[:, c, :], perm[:, c, :], start=c == 0, stop=c == EC - 1)
                for r in range(EC):
                    for c in range(EC):
                        last = nc.tensor.matmul(banks[2][:, 2 * r:2 * r + 2], perm[:, c, r * P:(r + 1) * P],
                                                sd[:, 2 * EDGES + 2 * c:2 * EDGES + 2 * c + 2],
                                                start=c == 0, stop=c == EC - 1)
                last.then_inc(sorted_done, 1)
                pe.wait_ge(oh_ready, 1)
                for c in range(EC):
                    last = nc.tensor.matmul(banks[3][:, c * P:(c + 1) * P], ohsT[:, c * P:(c + 1) * P], cst("adj"),
                                            start=True, stop=True)
                last.then_inc(adj_done, 1)

            @block.scalar
            def _(act):
                act.wait_ge(adj_ready, 1)
                nc.scalar.activation(logadj, adjv, ACT.Ln, bias=logeps)

        finish_rstd("0")

        take = carve()
        xn = take(2, W)
        xnT = take(2, W)
        qs = take(2, W)
        s02 = take(4, 512)
        lr = take(4, 512)
        with nc.Block() as block:
            xn_ready = steps("a_xn_ready", 2)
            t_done = steps("a_t_done", 2)
            xnT_ready = steps("a_xnT_ready", 2)
            qv_done = steps("a_qv_done", 2)
            q_ready = steps("a_q_ready", 2)
            v_ready = steps("a_v_ready", 2)
            pair_done = steps("a_pair_done", 4)
            low_ready = steps("a_low_ready", 4)
            lr_ready = steps("a_lr_ready", 4)
            score_done = steps("a_score_done", 2)
            score_used = steps("a_score_used", 2)
            psT = banks[0:2]
            psQ, psV = banks[2], banks[3]
            psG = banks[4:8]

            @block.vector
            def _(dve):
                for s in (xn_ready, q_ready, lr_ready, score_used):
                    s.open(dve)
                with dve.Fori(0, G // 2) as it:
                    for u in range(2):
                        g = it * 2 + u
                        dve.wait_ge(t_done.sem, t_done.done(g - 2))
                        normalise(xn[:, u, :], g).then_inc(xn_ready.sem, 1)
                    for u in range(2):
                        g = it * 2 + u
                        dve.wait_ge(qv_done.sem, qv_done.done(g))
                        dve.wait_ge(pair_done.sem, pair_done.done(g * 2 - 3))
                        nc.vector.tensor_copy(qs[:, u, :], psQ[:, :]).then_inc(q_ready.sem, 1)
                    for u in range(2):
                        for j in range(2):
                            h = it * 4 + (2 * u + j)
                            k = 2 * u + j
                            dve.wait_ge(low_ready.sem, low_ready.done(h))
                            dve.wait_ge(score_done.sem, score_done.done(it * 2 + (u - 2)))
                            nc.vector.tensor_tensor(lr[:, k, :], psG[k][:, :], s02[:, k, :], ALU.max)\
                                .then_inc(lr_ready.sem, 1)
                    for u in range(2):
                        g = it * 2 + u
                        dve.wait_ge(score_done.sem, score_done.done(g))
                        for c in range(EC):
                            ins = nc.vector.tensor_scalar(S[:, c, bass.ds(g * NB * HEADS, NB * HEADS)],
                                                          psT[u][:, c * 16:(c + 1) * 16], logadj[:, c:c + 1], None,
                                                          ALU.add)
                        ins.then_inc(score_used.sem, 1)

            @block.scalar
            def _(act):
                for s in (xnT_ready, v_ready, low_ready):
                    s.open(act)
                with act.Fori(0, G // 2) as it:
                    for u in range(2):
                        g = it * 2 + u
                        act.wait_ge(t_done.sem, t_done.done(g))
                        act.wait_ge(qv_done.sem, qv_done.done(g - 2))
                        nc.scalar.copy(xnT[:, u, :], psT[u][:, :]).then_inc(xnT_ready.sem, 1)
                    for u in range(2):
                        g = it * 2 + u
                        act.wait_ge(qv_done.sem, qv_done.done(g))
                        nc.scalar.copy(Y[:, cols(g)], psV[:, :]).then_inc(v_ready.sem, 1)
                    for k in range(4):
                        h = it * 4 + k
                        act.wait_ge(pair_done.sem, pair_done.done(h))
                        act.wait_ge(lr_ready.sem, lr_ready.done(h - 4))
                        nc.scalar.mul(s02[:, k, :], psG[k][:, :], 0.2).then_inc(low_ready.sem, 1)

            @block.tensor
            def _(pe):
                for s in (t_done, qv_done, pair_done, score_done):
                    s.open(pe)
                with pe.Fori(0, G // 2) as it:
                    for u in range(2):
                        g = it * 2 + u
                        pe.wait_ge(xn_ready.sem, xn_ready.done(g))
                        pe.wait_ge(score_used.sem, score_used.done(g - 2))
                        for b in range(NB):
                            last = nc.tensor.transpose(psT[u][:, b * P:(b + 1) * P], xn[:, u, b * D:(b + 1) * D], ident)
                        last.then_inc(t_done.sem, 1)
                    for u in range(2):
                        g = it * 2 + u
                        pe.wait_ge(xnT_ready.sem, xnT_ready.done(g))
                        pe.wait_ge(q_ready.sem, q_ready.done(g - 1))
                        pe.wait_ge(v_ready.sem, v_ready.done(g - 1))
                        for b in range(NB):
                            xb = xnT[:, u, b * P:(b + 1) * P]
                            nc.tensor.matmul(psQ[:, b * D:(b + 1) * D], xb, cst("wq"), start=True, stop=True)
                            last = nc.tensor.matmul(psV[:, b * D:(b + 1) * D], xb, cst("wv"), start=True, stop=True)
                        last.then_inc(qv_done.sem, 1)
                    for u in range(2):
                        g = it * 2 + u
                        pe.wait_ge(q_ready.sem, q_ready.done(g))
                        for j in range(2):
                            h = it * 4 + (2 * u + j)
                            pe.wait_ge(lr_ready.sem, lr_ready.done(h - 4))
                            for i in range(2):
                                b = 2 * j + i
                                last = nc.tensor.matmul(psG[2 * u + j][:, i * EDGES:(i + 1) * EDGES],
                                                        qs[:, u, b * D:(b + 1) * D], ohsum, start=True, stop=True)
                            last.then_inc(pair_done.sem, 1)
                    for u in range(2):
                        g = it * 2 + u
                        pe.wait_ge(lr_ready.sem, lr_ready.done(it * 4 + (2 * u + 1)))
                        for b in range(NB):
                            for c in range(EC):
                                at = (b % 2) * EDGES + c * P
                                last = nc.tensor.matmul(psT[u][:, c * 16 + b * HEADS:c * 16 + (b + 1) * HEADS],
                                                        lr[:, 2 * u + b // 2, at:at + P], cst("ahead"),
                                                        start=True, stop=True)
                        last.then_inc(score_done.sem, 1)

        free()
        take = carve()
        rmax = take(EC, B * HEADS)
        ST = take(4, EDGES)
        RUN = take(4, EDGES)
        with nc.Block() as block:
            st_done, st_ready, run_ready, back_done, back_ready, m_done, sub_ready, ex_ready, den_done = (
                sem(n) for n in ("st_done", "st_ready", "run_ready", "back_done", "back_ready", "m_done",
                                 "sub_ready", "ex_ready", "den_done"))

            @block.tensor
            def _(pe):
                for t in range(4):
                    for c in range(EC):
                        k = t * EC + c
                        last = nc.tensor.transpose(banks[k // 4][:, (k % 4) * P:(k % 4 + 1) * P],
                                                   S[:, c, t * P:(t + 1) * P], ident)
                last.then_inc(st_done, 1)
                pe.wait_ge(run_ready, 1)
                for c in range(EC):
                    for t in range(4):
                        last = nc.tensor.transpose(banks[2 + c][:, t * P:(t + 1) * P],
                                                   RUN[:, t, c * P:(c + 1) * P], ident)
                last.then_inc(back_done, 1)
                pe.wait_ge(back_ready, 1)
                for c in range(EC):
                    for k in range(EC):
                        last = nc.tensor.matmul(banks[4 + c][:, :], lastsel[:, k, c * P:(c + 1) * P], rmax[:, k, :],
                                                start=k == 0, stop=k == EC - 1)
                last.then_inc(m_done, 1)
                pe.wait_ge(ex_ready, 1)
                for c in range(EC):
                    for k in range(EC):
                        last = nc.tensor.matmul(banks[6 + c][:, :], same[:, k, c * P:(c + 1) * P], att[:, k, :],
                                                start=k == 0, stop=k == EC - 1)
                last.then_inc(den_done, 1)

            @block.vector
            def _(dve):
                dve.wait_ge(st_done, 1)
                for k in range(2):
                    link(nc.vector.tensor_copy(ST[:, 2 * k:2 * k + 2, :].rearrange("p a b -> p (a b)"), banks[k][:, :]))
                for t in range(4):
                    ins = nc.vector.tensor_tensor_scan(RUN[:, t, :], reset, ST[:, t, :], -BIG, ALU.add, ALU.max)
                ins.then_inc(run_ready, 1)
                dve.wait_ge(back_done, 1)
                for c in range(EC):
                    ins = nc.vector.tensor_copy(rmax[:, c, :], banks[2 + c][:, :])
                ins.then_inc(back_ready, 1)
                dve.wait_ge(m_done, 1)
                for c in range(EC):
                    ins = nc.vector.tensor_tensor(S[:, c, :], S[:, c, :], banks[4 + c][:, :], ALU.subtract)
                ins.then_inc(sub_ready, 1)
                dve.wait_ge(den_done, 1)
                for c in range(EC):
                    link(nc.vector.reciprocal(rmax[:, c, :], banks[6 + c][:, :]))
                    link(nc.vector.tensor_tensor(att[:, c, :], att[:, c, :], rmax[:, c, :], ALU.mult))

            @block.scalar
            def _(act):
                act.wait_ge(sub_ready, 1)
                for c in range(EC):
                    ins = nc.scalar.activation(att[:, c, :], S[:, c, :], ACT.Exp)
                ins.then_inc(ex_ready, 1)

        free()
        take = carve()
        wv = take(2, EC, W)
        yT = take(2, W)
        with nc.Block() as block:
            val_done = steps("c_val_done", 4)
            wv_ready = steps("c_wv_ready", 4)
            y_done = steps("c_y_done", 2)
            yT_ready = steps("c_yT_ready", 2)
            o_done = steps("c_o_done", 2)
            o_used = steps("c_o_used", 2)
            psVal = banks[0:4]
            psY = banks[4:6]
            psO = banks[6:8]

            @block.tensor
            def _(pe):
                for s in (val_done, y_done, o_done):
                    s.open(pe)
                with pe.Fori(0, G // 2) as it:
                    for u in range(2):
                        g = it * 2 + u
                        for c in range(EC):
                            n = it * 4 + (2 * u + c)
                            pe.wait_ge(wv_ready.sem, wv_ready.done(n - 4))
                            nc.tensor.matmul(psVal[2 * u + c][:, :], ohdT[:, c * P:(c + 1) * P], Y[:, cols(g)],
                                             start=True, stop=True).then_inc(val_done.sem, 1)
                    for u in range(2):
                        g = it * 2 + u
                        pe.wait_ge(wv_ready.sem, wv_ready.done(it * 4 + (2 * u + 1)))
                        pe.wait_ge(yT_ready.sem, yT_ready.done(g - 2))
                        for b in range(NB):
                            for c in range(EC):
                                last = nc.tensor.matmul(psY[u][:, b * P:(b + 1) * P], wv[:, u, c, b * D:(b + 1) * D],
                                                        ohs[:, c, :], start=c == 0, stop=c == EC - 1)
                        last.then_inc(y_done.sem, 1)
                    for u in range(2):
                        g = it * 2 + u
                        pe.wait_ge(yT_ready.sem, yT_ready.done(g))
                        pe.wait_ge(o_used.sem, o_used.done(g - 2))
                        for b in range(NB):
                            last = nc.tensor.matmul(psO[u][:, b * D:(b + 1) * D], yT[:, u, b * P:(b + 1) * P],
                                                    cst("wout"), start=True, stop=True)
                        last.then_inc(o_done.sem, 1)

            @block.scalar
            def _(act):
                yT_ready.open(act)
                with act.Fori(0, G // 2) as it:
                    for u in range(2):
                        g = it * 2 + u
                        act.wait_ge(y_done.sem, y_done.done(g))
                        act.wait_ge(o_done.sem, o_done.done(g - 2))
                        nc.scalar.copy(yT[:, u, :], psY[u][:, :]).then_inc(yT_ready.sem, 1)

            @block.vector
            def _(dve):
                for s in (wv_ready, o_used):
                    s.open(dve)
                with dve.Fori(0, G // 2) as it:
                    for u in range(2):
                        for c in range(EC):
                            n = it * 4 + (2 * u + c)
                            g = it * 2 + u
                            dve.wait_ge(val_done.sem, val_done.done(n))
                            dve.wait_ge(y_done.sem, y_done.done(g - 2))
                            weight = att[:, c, bass.ds(g * NB * HEADS, NB * HEADS)].unsqueeze(2)\
                                .broadcast_to([P, NB * HEADS, D // HEADS])
                            nc.vector.tensor_tensor(
                                wv[:, u, c, :].rearrange("p (a b) -> p a b", b=D // HEADS),
                                psVal[2 * u + c][:, :].rearrange("p (a b) -> p a b", b=D // HEADS),
                                weight, ALU.mult).then_inc(wv_ready.sem, 1)
                    for u in range(2):
                        g = it * 2 + u
                        dve.wait_ge(o_done.sem, o_done.done(g))
                        ins = nc.vector.tensor_tensor(X[:, cols(g)], X[:, cols(g)], psO[u][:, :], ALU.add)
                        ins.then_inc(o_used.sem, 1)
                        dve.wait_ge(o_used.sem, o_used.done(g))
                        group_stats(g)

        def store_x():
            with nc.Block() as block:
                @block.sync
                def _(sp):
                    sp.dma_start(out, X[:, :]).then_inc(s_out, 16)
                    sp.wait_ge(s_out, 16)
            free(len(scopes))

        if stop == "C":
            store_x()
            return

        def route(tag, logits, p, q, w, sel, small_t, rank_row, E, pair_softmax):
            exp_ready, pair_ready, shifted_ready, diff_ready = (
                sem(n + tag) for n in ("exp_ready", "pair_ready", "shifted_ready", "diff_ready"))

            def wide(v):
                return v.unsqueeze(2).broadcast_to([P, B, E])

            m, m1, m2, w1 = (small_t[:, i, :] for i in range(4))
            ranks = rank_row.unsqueeze(1).broadcast_to([P, B, E])
            tt, red = nc.vector.tensor_tensor, nc.vector.tensor_reduce
            with nc.Block() as block:
                @block.vector
                def _(dve):
                    link(red(m, logits, AXX, ALU.max))
                    tt(logits, logits, wide(m), ALU.subtract).then_inc(shifted_ready, 1)
                    dve.wait_ge(exp_ready, 1)
                    link(red(m, p, AXX, ALU.add))
                    link(nc.vector.reciprocal(m, m))
                    link(tt(p, p, wide(m), ALU.mult))

                    def first_of_largest(largest, chosen):
                        link(red(largest, p, AXX, ALU.max))
                        link(tt(q, p, wide(largest), ALU.is_equal))
                        link(tt(w, q, ranks, ALU.mult))
                        link(red(m, w, AXX, ALU.max))
                        link(tt(chosen, w, wide(m), ALU.is_equal))

                    first_of_largest(m1, sel)
                    link(nc.vector.scalar_tensor_tensor(p, sel, -2.0, p, ALU.mult, ALU.add))
                    first_of_largest(m2, q)
                    if pair_softmax:
                        tt(m2, m2, m1, ALU.subtract).then_inc(diff_ready, 1)
                        dve.wait_ge(pair_ready, 1)
                        link(nc.vector.tensor_scalar(m, m2, 1.0, None, ALU.add))
                        link(nc.vector.reciprocal(w1, m))
                        link(tt(m2, m2, w1, ALU.mult))
                        link(tt(sel, sel, wide(w1), ALU.mult))
                        link(tt(q, q, wide(m2), ALU.mult))
                        link(tt(sel, sel, q, ALU.add))
                    else:
                        link(tt(m, m1, m2, ALU.add))
                        link(nc.vector.reciprocal(m, m))
                        link(tt(w1, m1, m, ALU.mult))
                        link(tt(m2, m2, m, ALU.mult))

                @block.scalar
                def _(act):
                    act.wait_ge(shifted_ready, 1)
                    nc.scalar.activation(p, logits, ACT.Exp).then_inc(exp_ready, 1)
                    if pair_softmax:
                        act.wait_ge(diff_ready, 1)
                        nc.scalar.activation(m2, m2, ACT.Exp).then_inc(pair_ready, 1)

        free(2)
        finish_rstd("1")
        take = carve()
        ffn0_sb = take(FFN0_COLS)
        w3of = [[ffn0_sb[:, (l * E0 + e) * D:(l * E0 + e + 1) * D] for e in range(E0)] for l in range(3)]
        at = 3 * E0 * D
        b12 = [[ffn0_sb[:, at + l * E0 + e:at + l * E0 + e + 1] for e in range(E0)] for l in range(2)]
        b3rows = ffn0_sb[:, at + 2 * E0:at + 2 * E0 + D]
        logits0 = take(B, E0)
        prob0 = take(B, E0)
        tq0 = take(B, E0)
        tw0 = take(B, E0)
        mask0 = take(B, E0)
        small_t = take(4, B)
        take = carve()
        xn = take(2, W)
        rh = take(2, W)
        h1 = take(2, W)
        h2 = take(2, W)
        mk = take(2, NB * E0)
        mkT = take(2, W)

        with nc.Block() as block:
            xn_ready = steps("d_xn_ready", 2)
            t_done = steps("d_t_done", 2)
            xnT_ready = steps("d_xnT_ready", 2)
            r_done = steps("d_r_done", 2)
            rh_ready = steps("d_rh_ready", 2)
            l_done = steps("d_l_done", 2)
            l_used = steps("d_l_used", 2)
            psT, psR, psL = banks[0:2], banks[2:4], banks[4:6]

            @block.sync
            def _(sp):
                sp.dma_start(ffn0_sb, ffn0).then_inc(s_ffn0, 16)

            @block.vector
            def _(dve):
                for s in (xn_ready, l_used):
                    s.open(dve)
                bias = cst("rb2").unsqueeze(1).broadcast_to([P, NB, E0])
                with dve.Fori(0, G // 2) as it:
                    for u in range(2):
                        g = it * 2 + u
                        dve.wait_ge(t_done.sem, t_done.done(g - 2))
                        normalise(xn[:, u, :], g).then_inc(xn_ready.sem, 1)
                    for u in range(2):
                        g = it * 2 + u
                        dve.wait_ge(l_done.sem, l_done.done(g))
                        nc.vector.tensor_tensor(logits0[:, bass.ds(g * NB, NB), :],
                                                psL[u][:, 0:NB * E0].rearrange("p (a b) -> p a b", b=E0),
                                                bias, ALU.add).then_inc(l_used.sem, 1)

            @block.scalar
            def _(act):
                for s in (xnT_ready, rh_ready):
                    s.open(act)
                with act.Fori(0, G // 2) as it:
                    for u in range(2):
                        g = it * 2 + u
                        act.wait_ge(t_done.sem, t_done.done(g))
                        nc.scalar.copy(Y[:, cols(g)], psT[u][:, :]).then_inc(xnT_ready.sem, 1)
                    for u in range(2):
                        g = it * 2 + u
                        act.wait_ge(r_done.sem, r_done.done(g))
                        act.wait_ge(l_done.sem, l_done.done(g - 2))
                        nc.scalar.activation(rh[0:64, u, :], psR[u][0:64, :], ACT.Relu, bias=cst("rb1")[0:64, :])\
                            .then_inc(rh_ready.sem, 1)

            @block.tensor
            def _(pe):
                for s in (t_done, r_done, l_done):
                    s.open(pe)
                with pe.Fori(0, G // 2) as it:
                    for u in range(2):
                        g = it * 2 + u
                        pe.wait_ge(xn_ready.sem, xn_ready.done(g))
                        pe.wait_ge(xnT_ready.sem, xnT_ready.done(g - 2))
                        for b in range(NB):
                            last = nc.tensor.transpose(psT[u][:, b * P:(b + 1) * P], xn[:, u, b * D:(b + 1) * D], ident)
                        last.then_inc(t_done.sem, 1)
                    for u in range(2):
                        g = it * 2 + u
                        pe.wait_ge(xnT_ready.sem, xnT_ready.done(g))
                        pe.wait_ge(rh_ready.sem, rh_ready.done(g - 2))
                        nc.tensor.matmul(psR[u][0:64, :], cst("rw1"), Y[:, cols(g)], start=True, stop=True)\
                            .then_inc(r_done.sem, 1)
                    for u in range(2):
                        g = it * 2 + u
                        pe.wait_ge(rh_ready.sem, rh_ready.done(g))
                        pe.wait_ge(l_used.sem, l_used.done(g - 2))
                        for b in range(NB):
                            last = nc.tensor.matmul(psL[u][:, b * E0:(b + 1) * E0], rh[0:64, u, b * P:(b + 1) * P],
                                                    cst("rw2")[0:64, :], start=True, stop=True)
                        last.then_inc(l_done.sem, 1)

        route("0", logits0, prob0, tq0, tw0, mask0, small_t, cst("rank0"), E0, True)

        def mask_rows(pe, dve_ready, mk_slot, dst_bank, E):
            for b in range(NB):
                last = nc.tensor.transpose(dst_bank[0:E, b * P:(b + 1) * P], mk_slot[:, b * E:(b + 1) * E], ident)
            return last

        with nc.Block() as block:
            mk_ready = steps("e_mk_ready", 2)
            mt_done = steps("e_mt_done", 2)
            mkT_ready = steps("e_mkT_ready", 2)
            bias_done = steps("e_bias_done", 2)
            bias_used = steps("e_bias_used", 2)
            h1_done = steps("e_h1_done", 2)
            h1_ready = steps("e_h1_ready", 2)
            h2_done = steps("e_h2_done", 2)
            h2_ready = steps("e_h2_ready", 2)
            o_done = steps("e_o_done", 2)
            o_used = steps("e_o_used", 2)
            psH1, psH2, psO, psM, psB = banks[0:2], banks[2:4], banks[4:6], banks[6], banks[7]

            @block.tensor
            def _(pe):
                pe.wait_ge(s_ffn0, 16)
                for s in (mt_done, bias_done, h1_done, h2_done, o_done):
                    s.open(pe)

                def layer1(it, u, e):
                    n = it * (2 * E0) + (u * E0 + e)
                    pe.wait_ge(h1_ready.sem, h1_ready.done(n - 2))
                    nc.tensor.matmul(psH1[e % 2][:, :], w3of[0][e], Y[:, cols(it * 2 + u)], start=True, stop=True)\
                        .then_inc(h1_done.sem, 1)

                def layer2(it, u, e):
                    n = it * (2 * E0) + (u * E0 + e)
                    pe.wait_ge(h1_ready.sem, h1_ready.done(n))
                    pe.wait_ge(h2_ready.sem, h2_ready.done(n - 2))
                    nc.tensor.matmul(psH2[e % 2][:, :], w3of[1][e], h1[:, e % 2, :], start=True, stop=True)\
                        .then_inc(h2_done.sem, 1)

                def layer3(it, u, e):
                    n = it * (2 * E0) + (u * E0 + e)
                    pe.wait_ge(h2_ready.sem, h2_ready.done(n))
                    pe.wait_ge(o_used.sem, o_used.done(n - 2))
                    for b in range(NB):
                        last = nc.tensor.matmul(psO[e % 2][:, b * D:(b + 1) * D], h2[:, e % 2, b * P:(b + 1) * P],
                                                w3of[2][e], start=True, stop=True)
                    last.then_inc(o_done.sem, 1)

                with pe.Fori(0, G // 2) as it:
                    for u in range(2):
                        g = it * 2 + u
                        pe.wait_ge(mk_ready.sem, mk_ready.done(g))
                        pe.wait_ge(mkT_ready.sem, mkT_ready.done(g - 1))
                        for b in range(NB):
                            last = nc.tensor.transpose(psM[0:E0, b * P:(b + 1) * P], mk[:, u, b * E0:(b + 1) * E0], ident)
                        last.then_inc(mt_done.sem, 1)
                        layer1(it, u, 0)
                        layer1(it, u, 1)
                        pe.wait_ge(mkT_ready.sem, mkT_ready.done(g))
                        pe.wait_ge(bias_used.sem, bias_used.done(g - 1))
                        for b in range(NB):
                            last = nc.tensor.matmul(psB[:, b * D:(b + 1) * D], mkT[0:E0, u, b * P:(b + 1) * P],
                                                    b3rows[0:E0, :], start=True, stop=True)
                        last.then_inc(bias_done.sem, 1)
                        for e in range(E0 + 1):
                            if e < E0:
                                layer2(it, u, e)
                            if e + 2 < E0:
                                layer1(it, u, e + 2)
                            if e >= 1:
                                layer3(it, u, e - 1)

            @block.scalar
            def _(act):
                for s in (mkT_ready, h1_ready, h2_ready):
                    s.open(act)

                def relu1(it, u, e):
                    n = it * (2 * E0) + (u * E0 + e)
                    act.wait_ge(h1_done.sem, h1_done.done(n))
                    act.wait_ge(h2_done.sem, h2_done.done(n - 2))
                    nc.scalar.activation(h1[:, e % 2, :], psH1[e % 2][:, :], ACT.Relu, bias=b12[0][e])\
                        .then_inc(h1_ready.sem, 1)

                def relu2(it, u, e):
                    n = it * (2 * E0) + (u * E0 + e)
                    act.wait_ge(h2_done.sem, h2_done.done(n))
                    act.wait_ge(o_done.sem, o_done.done(n - 2))
                    nc.scalar.activation(h2[:, e % 2, :], psH2[e % 2][:, :], ACT.Relu, bias=b12[1][e])\
                        .then_inc(h2_ready.sem, 1)

                act.wait_ge(s_ffn0, 16)
                with act.Fori(0, G // 2) as it:
                    for u in range(2):
                        g = it * 2 + u
                        act.wait_ge(mt_done.sem, mt_done.done(g))
                        act.wait_ge(bias_done.sem, bias_done.done(g - 2))
                        nc.scalar.copy(mkT[0:E0, u, :], psM[0:E0, :]).then_inc(mkT_ready.sem, 1)
                        relu1(it, u, 0)
                        relu1(it, u, 1)
                        for e in range(E0):
                            relu2(it, u, e)
                            if e + 2 < E0:
                                relu1(it, u, e + 2)

            @block.vector
            def _(dve):
                for s in (bias_used, o_used):
                    s.open(dve)
                x_ready = sem("e_x_ready")
                with dve.Fori(0, G // 2) as it:
                    for u in range(2):
                        g = it * 2 + u
                        dve.wait_ge(bias_done.sem, bias_done.done(g))
                        nc.vector.tensor_tensor(X[:, cols(g)], X[:, cols(g)], psB[:, :], ALU.add)\
                            .then_inc(bias_used.sem, 1)
                        dve.wait_ge(bias_used.sem, bias_used.done(g))
                        for e in range(E0):
                            n = it * (2 * E0) + (u * E0 + e)
                            dve.wait_ge(o_done.sem, o_done.done(n))
                            for b in range(NB):
                                xb = X[:, bass.ds(g * W + b * D, D)]
                                ins = nc.vector.scalar_tensor_tensor(xb, psO[e % 2][:, b * D:(b + 1) * D],
                                                                     mask0[:, bass.ds(g * NB + b, 1), e], xb,
                                                                     ALU.mult, ALU.add)
                            ins.then_inc(o_used.sem, 1)
                            dve.wait_ge(o_used.sem, o_used.done(n))
                        group_stats(g)

            @block.gpsimd
            def _(pool):
                mk_ready.open(pool)
                with pool.Fori(0, G // 2) as it:
                    for u in range(2):
                        g = it * 2 + u
                        pool.wait_ge(mt_done.sem, mt_done.done(g - 2))
                        nc.gpsimd.tensor_copy(mk[:, u, :].rearrange("p (a b) -> p a b", b=E0),
                                              mask0[:, bass.ds(g * NB, NB), :]).then_inc(mk_ready.sem, 1)

        if stop == "D":
            store_x()
            return

        free(2)
        finish_rstd("2")
        take = carve()
        lstm_sb = take(LSTM_COLS)
        wih = [[lstm_sb[:, (p * 4 + k) * D:(p * 4 + k + 1) * D] for k in range(4)] for p in range(SKIPS)]
        whh = [[lstm_sb[:, ((SKIPS + p) * 4 + k) * D:((SKIPS + p) * 4 + k + 1) * D] for k in range(4)]
               for p in range(SKIPS)]
        at = SKIPS * 8 * D
        bih, bhh = lstm_sb[:, at:at + 4 * SKIPS], lstm_sb[:, at + 4 * SKIPS:at + 8 * SKIPS]
        bias_g = take(4 * SKIPS)
        take = carve()
        xn = take(2, W)
        xnT = take(2, W)
        v1 = take(2, W)
        h1T = take(2, W)
        v2 = take(2, W)

        with nc.Block() as block:
            xn_ready = steps("g_xn_ready", 2)
            t_done = steps("g_t_done", 2)
            xnT_ready = steps("g_xnT_ready", 2)
            v1_done = steps("g_v1_done", 2)
            v1_ready = steps("g_v1_ready", 2)
            m1_done = steps("g_m1_done", 2)
            h1_ready = steps("g_h1_ready", 2)
            v2_done = steps("g_v2_done", 2)
            v2_ready = steps("g_v2_ready", 2)
            m2_done = steps("g_m2_done", 2)
            h2_ready = steps("g_h2_ready", 2)
            psA, psB = banks[0:2], banks[2:4]

            @block.sync
            def _(sp):
                sp.dma_start(lstm_sb, lstm).then_inc(s_lstm, 16)

            @block.vector
            def _(dve):
                for s in (xn_ready, v1_ready, v2_ready):
                    s.open(dve)

                def biased(dst, src, row):
                    return nc.vector.tensor_tensor(dst.rearrange("p (a b) -> p a b", b=D),
                                                   src.rearrange("p (a b) -> p a b", b=D),
                                                   row.unsqueeze(1).broadcast_to([P, NB, D]), ALU.add)

                with dve.Fori(0, G // 2) as it:
                    for u in range(2):
                        g = it * 2 + u
                        dve.wait_ge(t_done.sem, t_done.done(g - 2))
                        normalise(xn[:, u, :], g).then_inc(xn_ready.sem, 1)
                    for u in range(2):
                        g = it * 2 + u
                        dve.wait_ge(v1_done.sem, v1_done.done(g))
                        dve.wait_ge(m1_done.sem, m1_done.done(g - 2))
                        biased(v1[:, u, :], psB[u][:, :], cst("bg0")).then_inc(v1_ready.sem, 1)
                    for u in range(2):
                        g = it * 2 + u
                        dve.wait_ge(v2_done.sem, v2_done.done(g))
                        dve.wait_ge(m2_done.sem, m2_done.done(g - 2))
                        biased(v2[:, u, :], psB[u][:, :], cst("bg1")).then_inc(v2_ready.sem, 1)
                dve.wait_ge(s_lstm, 16)
                nc.vector.tensor_tensor(bias_g, bih, bhh, ALU.add)

            @block.scalar
            def _(act):
                for s in (xnT_ready, h1_ready, h2_ready):
                    s.open(act)
                with act.Fori(0, G // 2) as it:
                    for u in range(2):
                        g = it * 2 + u
                        act.wait_ge(t_done.sem, t_done.done(g))
                        act.wait_ge(v1_done.sem, v1_done.done(g - 2))
                        nc.scalar.copy(xnT[:, u, :], psA[u][:, :]).then_inc(xnT_ready.sem, 1)
                    for u in range(2):
                        g = it * 2 + u
                        act.wait_ge(m1_done.sem, m1_done.done(g))
                        act.wait_ge(v2_done.sem, v2_done.done(g - 2))
                        nc.scalar.activation(h1T[:, u, :], psA[u][:, :], ACT.Relu).then_inc(h1_ready.sem, 1)
                    for u in range(2):
                        g = it * 2 + u
                        act.wait_ge(m2_done.sem, m2_done.done(g))
                        nc.scalar.activation(Y[:, cols(g)], psA[u][:, :], ACT.Relu).then_inc(h2_ready.sem, 1)

            @block.tensor
            def _(pe):
                for s in (t_done, v1_done, m1_done, v2_done, m2_done):
                    s.open(pe)

                def four(dst, src, rhs, done):
                    for b in range(NB):
                        last = nc.tensor.matmul(dst[:, b * P:(b + 1) * P], src[:, b * P:(b + 1) * P], rhs,
                                                start=True, stop=True)
                    last.then_inc(done.sem, 1)

                with pe.Fori(0, G // 2) as it:
                    for u in range(2):
                        g = it * 2 + u
                        pe.wait_ge(xn_ready.sem, xn_ready.done(g))
                        pe.wait_ge(h2_ready.sem, h2_ready.done(g - 2))
                        for b in range(NB):
                            last = nc.tensor.transpose(psA[u][:, b * P:(b + 1) * P], xn[:, u, b * D:(b + 1) * D], ident)
                        last.then_inc(t_done.sem, 1)
                    for u in range(2):
                        pe.wait_ge(xnT_ready.sem, xnT_ready.done(it * 2 + u))
                        pe.wait_ge(v2_ready.sem, v2_ready.done(it * 2 + (u - 2)))
                        four(psB[u], xnT[:, u, :], cst("wg0"), v1_done)
                    for u in range(2):
                        pe.wait_ge(v1_ready.sem, v1_ready.done(it * 2 + u))
                        four(psA[u], v1[:, u, :], cst("adjT"), m1_done)
                    for u in range(2):
                        pe.wait_ge(h1_ready.sem, h1_ready.done(it * 2 + u))
                        four(psB[u], h1T[:, u, :], cst("wg1"), v2_done)
                    for u in range(2):
                        pe.wait_ge(v2_ready.sem, v2_ready.done(it * 2 + u))
                        four(psA[u], v2[:, u, :], cst("adjT"), m2_done)

        free()
        take = carve()
        gates = [[take(W) for _ in range(4)] for _ in range(2)]
        cell = [take(W) for _ in range(2)]
        tcell = [take(W) for _ in range(2)]
        hid = [take(W) for _ in range(2)]
        for p in range(1, SKIPS + 1):
            nw = P // p
            nbc = {1: 4, 2: 8, 3: 8, 4: 16}[p]
            n = nbc * nw
            turns = B // nbc // 2
            i_, f_, g_, o_ = range(4)

            def active(j):
                return (i_, g_, o_) if j == 0 else (i_, f_, g_, o_)

            with nc.Block() as block:
                gates_done = steps(f"l{p}_gates_done", 2 * p)
                gates_ready = steps(f"l{p}_gates_ready", 2 * p)
                cell_ready = steps(f"l{p}_cell_ready", 2 * p)
                tcell_ready = steps(f"l{p}_tcell_ready", 2 * p)
                hid_ready = steps(f"l{p}_hid_ready", 2 * p)

                def item(it, j, u):
                    return it * (2 * p) + (2 * j + u)

                def at_step(it, j, u):
                    return Y3[:, bass.ds((it * 2 + u) * nbc, nbc), j:j + (nw - 1) * p + 1:p]

                def bank(u, k):
                    return banks[4 * u + k][:, 0:n]

                @block.tensor
                def _(pe, p=p, n=n):
                    gates_done.open(pe)
                    with pe.Fori(0, turns) as it:
                        for j in range(p):
                            for u in range(2):
                                m = item(it, j, u)
                                pe.wait_ge(gates_ready.sem, gates_ready.done(m - 2))
                                for k in active(j):
                                    last = nc.tensor.matmul(bank(u, k).rearrange("p (a b) -> p a b", a=nbc),
                                                            wih[p - 1][k], at_step(it, j, u), start=True, stop=j == 0)
                                if j > 0:
                                    pe.wait_ge(hid_ready.sem, hid_ready.done(m - 2))
                                    for k in active(j):
                                        last = nc.tensor.matmul(bank(u, k), whh[p - 1][k], hid[u][:, 0:n],
                                                                start=False, stop=True)
                                last.then_inc(gates_done.sem, 1)

                @block.scalar
                def _(act, p=p, n=n):
                    gates_ready.open(act)
                    tcell_ready.open(act)
                    with act.Fori(0, turns) as it:
                        for j in range(p):
                            for u in range(2):
                                m = item(it, j, u)
                                act.wait_ge(gates_done.sem, gates_done.done(m))
                                act.wait_ge(hid_ready.sem, hid_ready.done(m - 2))
                                for k in active(j):
                                    last = nc.scalar.activation(
                                        gates[u][k][:, 0:n], bank(u, k), ACT.Tanh if k == g_ else ACT.Sigmoid,
                                        bias=bias_g[:, (p - 1) * 4 + k:(p - 1) * 4 + k + 1])
                                last.then_inc(gates_ready.sem, 1)
                                act.wait_ge(cell_ready.sem, cell_ready.done(m))
                                nc.scalar.activation(tcell[u][:, 0:n], cell[u][:, 0:n], ACT.Tanh)\
                                    .then_inc(tcell_ready.sem, 1)

                @block.vector
                def _(dve, p=p, n=n):
                    cell_ready.open(dve)
                    hid_ready.open(dve)
                    part_ready = steps(f"l{p}_part_ready", 2 * p)
                    part_ready.open(dve)
                    with dve.Fori(0, turns) as it:
                        for j in range(p):
                            for u in range(2):
                                m = item(it, j, u)
                                i, f, g, o = (gates[u][k][:, 0:n] for k in range(4))
                                c = cell[u][:, 0:n]
                                dve.wait_ge(gates_ready.sem, gates_ready.done(m))
                                if j == 0:
                                    dve.wait_ge(tcell_ready.sem, tcell_ready.done(m - 2))
                                    nc.vector.tensor_tensor(c, i, g, ALU.mult).then_inc(cell_ready.sem, 1)
                                else:
                                    nc.vector.tensor_tensor(i, i, g, ALU.mult)
                                    nc.vector.tensor_tensor(c, f, c, ALU.mult).then_inc(part_ready.sem, 1)
                                    dve.wait_ge(part_ready.sem,
                                                part_ready.done(it * (2 * (p - 1)) + (2 * (j - 1) + u)))
                                    nc.vector.tensor_tensor(c, c, i, ALU.add).then_inc(cell_ready.sem, 1)
                                dve.wait_ge(tcell_ready.sem, tcell_ready.done(m))
                                t = tcell[u][:, 0:n]
                                if j < p - 1:
                                    nc.vector.tensor_tensor(hid[u][:, 0:n], o, t, ALU.mult).then_inc(hid_ready.sem, 1)
                                else:
                                    nc.vector.tensor_tensor(at_step(it, j, u), o.rearrange("p (a b) -> p a b", a=nbc),
                                                            t.rearrange("p (a b) -> p a b", a=nbc), ALU.mult)\
                                        .then_inc(hid_ready.sem, 1)

        free()
        take = carve()
        hT = take(2, W)
        with nc.Block() as block:
            h_ready = steps("h_h_ready", 2)
            t_done = steps("h_t_done", 2)
            x_ready = steps("h_x_ready", 2)
            psT = banks[0:2]

            @block.gpsimd
            def _(pool):
                h_ready.open(pool)
                with pool.Fori(0, G // 2) as it:
                    for u in range(2):
                        g = it * 2 + u
                        pool.wait_ge(t_done.sem, t_done.done(g - 2))
                        nc.gpsimd.tensor_copy(hT[:, u, :], Y[:, cols(g)]).then_inc(h_ready.sem, 1)

            @block.tensor
            def _(pe):
                t_done.open(pe)
                with pe.Fori(0, G // 2) as it:
                    for u in range(2):
                        g = it * 2 + u
                        pe.wait_ge(h_ready.sem, h_ready.done(g))
                        pe.wait_ge(x_ready.sem, x_ready.done(g - 2))
                        for b in range(NB):
                            last = nc.tensor.transpose(psT[u][:, b * D:(b + 1) * D], hT[:, u, b * P:(b + 1) * P], ident)
                        last.then_inc(t_done.sem, 1)

            @block.vector
            def _(dve):
                x_ready.open(dve)
                with dve.Fori(0, G // 2) as it:
                    for u in range(2):
                        g = it * 2 + u
                        dve.wait_ge(t_done.sem, t_done.done(g))
                        nc.vector.tensor_tensor(X[:, cols(g)], X[:, cols(g)], psT[u][:, :], ALU.add)\
                            .then_inc(x_ready.sem, 1)
                        dve.wait_ge(x_ready.sem, x_ready.done(g))
                        group_stats(g)

        if stop == "G":
            store_x()
            return

        renew_semaphores()
        finish_rstd("3")
        free(3)
        take = carve()
        WB = take(E1, 4, FK * D, dt=F32R)
        biases = take(E1 + 1, FK + 1)
        slot = take(B, 2, dt=I32)
        pairw = take(2, B)
        owner = take(BLOCKS, dt=I32)
        take = carve()
        WS = take(4, FK * D, dt=F32R)
        take = carve()
        raw = take(2, EW)
        logits1 = take(B, E1)
        prob1 = take(B, E1)
        tq1 = take(B, E1)
        tw1 = take(B, E1)
        sel1 = take(B, E1)
        small_t = take(4, B)
        xn = take(2, W)
        xnT = take(2, W)

        with nc.Block() as block:
            xn_ready = steps("r_xn_ready", 2)
            t_done = steps("r_t_done", 2)
            xnT_ready = steps("r_xnT_ready", 2)
            l_done = steps("r_l_done", 2)
            l_used = steps("r_l_used", 2)
            s_raw = [sem(f"s_raw{i}") for i in range(2)]
            s_bias = sem("s_bias")
            high_ready = sem("r_high_ready")
            low_ready = sem("r_low_ready")
            psT, psL = banks[0:2], banks[2:4]

            def parts(e):
                w = WB[:, e] if e < E1 else WS
                return w.rearrange("p (l h) c -> p l h c", h=2)

            @block.sync
            def _(sp):
                sp.dma_start(biases.rearrange("p a b -> p (a b)"), ffn1[:, (E1 + 1) * EW:FFN1_COLS]).then_inc(s_bias, 16)
                for e in range(E1 + 1):
                    if e >= 2:
                        sp.wait_ge(low_ready, e - 1)
                    sp.dma_start(raw[:, e % 2, :], ffn1[:, e * EW:(e + 1) * EW]).then_inc(s_raw[e % 2], 16)
                sp.wait_ge(s_bias, 16)

            @block.vector
            def _(dve):
                for s in (xn_ready, l_used):
                    s.open(dve)
                with dve.Fori(0, G // 2) as it:
                    for u in range(2):
                        g = it * 2 + u
                        dve.wait_ge(t_done.sem, t_done.done(g - 2))
                        normalise(xn[:, u, :], g).then_inc(xn_ready.sem, 1)
                    for u in range(2):
                        g = it * 2 + u
                        dve.wait_ge(l_done.sem, l_done.done(g))
                        nc.vector.tensor_copy(logits1[:, bass.ds(g * NB, NB), :],
                                              psL[u][:, 0:NB * E1].rearrange("p (a b) -> p a b", b=E1))\
                            .then_inc(l_used.sem, 1)
                for e in range(E1 + 1):
                    dve.wait_ge(high_ready, e + 1)
                    part = parts(e)
                    nc.vector.tensor_tensor(part[:, :, 1, :], raw[:, e % 2, :].rearrange("p (l c) -> p l c", l=2),
                                            part[:, :, 0, :].bitcast(F32), ALU.subtract).then_inc(low_ready, 1)

            @block.scalar
            def _(act):
                xnT_ready.open(act)
                with act.Fori(0, G // 2) as it:
                    for u in range(2):
                        g = it * 2 + u
                        act.wait_ge(t_done.sem, t_done.done(g))
                        act.wait_ge(l_done.sem, l_done.done(g - 2))
                        nc.scalar.copy(xnT[:, u, :], psT[u][:, :]).then_inc(xnT_ready.sem, 1)
                for e in range(E1 + 1):
                    act.wait_ge(s_raw[e % 2], 16 * (e // 2 + 1))
                    nc.scalar.copy(parts(e)[:, :, 0, :], raw[:, e % 2, :].rearrange("p (l c) -> p l c", l=2))\
                        .then_inc(high_ready, 1)

            @block.tensor
            def _(pe):
                for s in (t_done, l_done):
                    s.open(pe)
                with pe.Fori(0, G // 2) as it:
                    for u in range(2):
                        g = it * 2 + u
                        pe.wait_ge(xn_ready.sem, xn_ready.done(g))
                        pe.wait_ge(xnT_ready.sem, xnT_ready.done(g - 2))
                        for b in range(NB):
                            last = nc.tensor.transpose(psT[u][:, b * P:(b + 1) * P], xn[:, u, b * D:(b + 1) * D], ident)
                        last.then_inc(t_done.sem, 1)
                    for u in range(2):
                        g = it * 2 + u
                        pe.wait_ge(xnT_ready.sem, xnT_ready.done(g))
                        pe.wait_ge(l_used.sem, l_used.done(g - 2))
                        for b in range(NB):
                            last = nc.tensor.matmul(psL[u][:, b * E1:(b + 1) * E1], xnT[:, u, b * P:(b + 1) * P],
                                                    cst("wr"), start=True, stop=True)
                        last.then_inc(l_done.sem, 1)

        route("1", logits1, prob1, tq1, tw1, sel1, small_t, cst("rank1"), E1, False)

        chosen, place, total = logits1, prob1, tw1
        upto_b = xn.rearrange("p a b -> p (a b)")[:, 0:B * E1].rearrange("p (a b) -> p a b", b=E1)
        ended = xnT.rearrange("p a b -> p (a b)")[:, 0:BLOCKS * E1].rearrange("p (a b) -> p a b", b=E1)
        counts = small_t[:, 0, 0:4 * E1].rearrange("p (a b) -> p a b", b=E1)
        counts_i = small_t[:, 0, 4 * E1:6 * E1].bitcast(I32).rearrange("p (a b) -> p a b", b=E1)
        slot_f = small_t[:, 1, :]
        own_f = raw[:, 0, 0:BLOCKS]
        with nc.Block() as block:
            chosen_ready, ranked = sem("chosen_ready"), sem("ranked")

            @block.tensor
            def _(pe):
                pe.wait_ge(chosen_ready, 1)
                for h in range(2):
                    rhs = chosen.rearrange("p a b -> p (a b)")[:, h * 512:(h + 1) * 512]
                    nc.tensor.matmul(banks[h][:, :], cst("below"), rhs, start=True, stop=True)
                    last = nc.tensor.matmul(banks[2 + h][:, :], cst("ones"), rhs, start=True, stop=True)
                last.then_inc(ranked, 1)

            @block.vector
            def _(dve):
                tt = nc.vector.tensor_tensor
                link(nc.vector.tensor_copy(pairw[:, 0, :], small_t[:, 3, :]))
                link(nc.vector.tensor_copy(pairw[:, 1, :], small_t[:, 2, :]))
                tt(chosen, sel1, tq1, ALU.add).then_inc(chosen_ready, 1)
                dve.wait_ge(ranked, 1)
                for h in range(2):
                    link(nc.vector.tensor_copy(place.rearrange("p a b -> p (a b)")[:, h * 512:(h + 1) * 512],
                                               banks[h][:, :]))
                    link(nc.vector.tensor_copy(total.rearrange("p a b -> p (a b)")[:, h * 512:(h + 1) * 512],
                                               banks[2 + h][:, :]))
                for e in range(E1):
                    link(nc.vector.tensor_tensor_scan(upto_b[:, :, e], cst("ones")[:, 0:B], total[:, :, e], 0.0,
                                                      ALU.mult, ALU.add))
                link(nc.vector.tensor_scalar(counts_i[:, 0, :], upto_b[:, B - 1, :], float(BLOCK - 1), None, ALU.add))
                link(nc.vector.tensor_scalar(counts_i[:, 1, :], counts_i[:, 0, :], BLOCK.bit_length() - 1, None,
                                             ALU.arith_shift_right))
                link(nc.vector.tensor_copy(counts[:, 1, :], counts_i[:, 1, :]))
                link(nc.vector.tensor_tensor_scan(counts[:, 2, :], cst("ones")[:, 0:E1], counts[:, 1, :], 0.0,
                                                  ALU.mult, ALU.add))
                link(tt(counts[:, 3, :], counts[:, 2, :], counts[:, 1, :], ALU.subtract))
                link(nc.vector.tensor_scalar(counts[:, 3, :], counts[:, 3, :], float(BLOCK), None, ALU.mult))
                link(tt(place, place, upto_b, ALU.add))
                link(tt(place, place, total, ALU.subtract))
                link(tt(place, place, counts[:, 3, :].unsqueeze(1).broadcast_to([P, B, E1]), ALU.add))
                for k, sel in ((0, sel1), (1, tq1)):
                    link(tt(sel, sel, place, ALU.mult))
                    link(nc.vector.tensor_reduce(slot_f, sel, AXX, ALU.add))
                    link(nc.vector.tensor_copy(slot[:, :, k], slot_f))
                link(tt(ended, cst("blk").unsqueeze(2).broadcast_to([P, BLOCKS, E1]),
                        counts[:, 2, :].unsqueeze(1).broadcast_to([P, BLOCKS, E1]), ALU.is_ge))
                link(nc.vector.tensor_reduce(own_f, ended, AXX, ALU.add))
                link(nc.vector.tensor_scalar(own_f, own_f, float(E1 - 1), None, ALU.min))
                link(nc.vector.tensor_copy(owner, own_f))

        free()
        take = carve()
        xa = [take(NB, ROW) for _ in range(2)]
        xb = [take(NB, ROW) for _ in range(2)]
        idx = [[take(NB, dt=I32) for _ in range(2)] for _ in range(2)]
        xT = [[take(W, dt=F32R) for _ in range(2)] for _ in range(2)]
        gf = [take(W) for _ in range(2)]
        gs = [[take(W, dt=F32R) for _ in range(2)] for _ in range(FK)]
        yT = [take(W) for _ in range(2)]

        def product(dst, w_high, w_low, x_high, x_low, start, stop):
            nc.tensor.matmul(dst, w_low, x_high, start=start, stop=False)
            nc.tensor.matmul(dst, w_high, x_low, start=False, stop=False)
            return nc.tensor.matmul(dst, w_high, x_high, start=False, stop=stop)

        with nc.Block() as block:
            pads_ready = sem("s_pads_ready")
            groups_taken = sem("s_groups_taken")
            xa_ready = steps("s_xa_ready", 2)
            xb_ready = steps("s_xb_ready", 2)
            scattered = [sem(f"s_scattered{u}") for u in range(2)]
            PER = 16 * 2 * NB
            t_done = steps("s_t_done", 2)
            high_ready = steps("s_high_ready", 2)
            low_ready = steps("s_low_ready", 2)
            up_done = steps("s_up_done", FK)
            gelu_ready = steps("s_gelu_ready", FK)
            ghigh_ready = steps("s_ghigh_ready", FK)
            split_ready = steps("s_split_ready", FK)
            down_done = steps("s_down_done", FK)
            y_ready = steps("s_y_ready", 2)
            yt_done = steps("s_yt_done", 2)
            x_ready = steps("s_x_ready", 2)
            psU, psT, psO, psY = banks[0:4], banks[4:6], banks[6], banks[7]

            @block.gpsimd
            def _(pool):
                pool.wait_ge(s_fill, 16 * BLOCKS)
                with pool.Fori(0, G // 2) as it:
                    for u in range(2):
                        g = it * 2 + u
                        pool.wait_ge(xa_ready.sem, xa_ready.done(g))
                        pool.wait_ge(xb_ready.sem, xb_ready.done(g))
                        pool.sem_inc(groups_taken, 1)
                        for k, rows in ((0, xa[u]), (1, xb[u])):
                            for b in range(NB):
                                at = idx[u][k][:, b:b + 1].bitcast(U32)
                                nc.gpsimd.indirect_dma_start(rows_dram, bass.IndirectOffsetOnAxis(ap=at, axis=0),
                                                             rows[:, b, :], None).then_inc(scattered[u], 16)
                for u in range(2):
                    pool.wait_ge(scattered[u], PER * (G // 2))

            @block.vector
            def _(dve):
                for s in (xa_ready, low_ready, ghigh_ready, split_ready, x_ready):
                    s.open(dve)
                for u in range(2):
                    nc.vector.memset(xa[u], 0.0)
                    ins = nc.vector.memset(xb[u], 0.0)
                ins.then_inc(pads_ready, 1)
                dve.wait_ge(pads_ready, 1)
                with dve.Fori(0, G // 2) as it:
                    for u in range(2):
                        g = it * 2 + u
                        dve.wait_ge(t_done.sem, t_done.done(g - 2))
                        dve.wait_ge(scattered[u], it * PER)
                        for b in range(NB):
                            nc.vector.tensor_scalar(xa[u][:, b, 0:D], X3[:, bass.ds(g * NB + b, 1), :],
                                                    MEAN[:, bass.ds(g * NB + b, 1)], RSTD[:, bass.ds(g * NB + b, 1)],
                                                    ALU.subtract, ALU.mult)
                        for k in range(2):
                            nc.vector.tensor_copy(idx[u][k], slot[:, bass.ds(g * NB, NB), k])
                        nc.vector.tensor_copy(xb[u][:, :, D].bitcast(I32), ids_sb[:, bass.ds(g * NB + B, NB)])
                        nc.vector.tensor_copy(xa[u][:, :, D].bitcast(I32), ids_sb[:, bass.ds(g * NB, NB)])\
                            .then_inc(xa_ready.sem, 1)
                    for u in range(2):
                        g = it * 2 + u
                        dve.wait_ge(high_ready.sem, high_ready.done(g))
                        nc.vector.tensor_tensor(xT[u][1], psT[u][:, :], xT[u][0].bitcast(F32), ALU.subtract)\
                            .then_inc(low_ready.sem, 1)
                    for u in range(2):
                        g = it * 2 + u
                        for k in range(FK):
                            m = it * (2 * FK) + (u * FK + k)
                            dve.wait_ge(gelu_ready.sem, gelu_ready.done(m))
                            dve.wait_ge(down_done.sem, down_done.done(m - FK))
                            nc.vector.tensor_copy(gs[k][0], gf[k % 2]).then_inc(ghigh_ready.sem, 1)
                            dve.wait_ge(ghigh_ready.sem, ghigh_ready.done(m))
                            nc.vector.tensor_tensor(gs[k][1], gf[k % 2], gs[k][0].bitcast(F32), ALU.subtract)\
                                .then_inc(split_ready.sem, 1)
                        dve.wait_ge(yt_done.sem, yt_done.done(g))
                        nc.vector.tensor_tensor(X[:, cols(g)], X[:, cols(g)], psY[:, :], ALU.add)\
                            .then_inc(x_ready.sem, 1)

            @block.scalar
            def _(act):
                act.wait_ge(pads_ready, 1)
                for s in (xb_ready, high_ready, gelu_ready, y_ready):
                    s.open(act)
                with act.Fori(0, G // 2) as it:
                    for u in range(2):
                        g = it * 2 + u
                        act.wait_ge(xa_ready.sem, xa_ready.done(g))
                        nc.scalar.copy(xb[u][:, :, 0:D], xa[u][:, :, 0:D]).then_inc(xb_ready.sem, 1)
                        act.wait_ge(t_done.sem, t_done.done(g))
                        act.wait_ge(up_done.sem, up_done.done(it * (2 * FK) + ((u - 2) * FK + FK - 1)))
                        nc.scalar.copy(xT[u][0], psT[u][:, :]).then_inc(high_ready.sem, 1)
                    for u in range(2):
                        g = it * 2 + u
                        for k in range(FK):
                            m = it * (2 * FK) + (u * FK + k)
                            act.wait_ge(up_done.sem, up_done.done(m))
                            act.wait_ge(split_ready.sem, split_ready.done(m - 2))
                            nc.scalar.activation(gf[k % 2], psU[k][:, :], ACT.Gelu, bias=biases[:, E1, k:k + 1])\
                                .then_inc(gelu_ready.sem, 1)
                        act.wait_ge(down_done.sem, down_done.done(it * (2 * FK) + (u * FK + FK - 1)))
                        act.wait_ge(yt_done.sem, yt_done.done(g - 2))
                        nc.scalar.activation(yT[u], psO[:, :], ACT.Identity, bias=biases[:, E1, FK:FK + 1])\
                            .then_inc(y_ready.sem, 1)

            @block.tensor
            def _(pe):
                for s in (t_done, up_done, down_done, yt_done):
                    s.open(pe)
                with pe.Fori(0, G // 2) as it:
                    for u in range(2):
                        g = it * 2 + u
                        pe.wait_ge(xa_ready.sem, xa_ready.done(g))
                        pe.wait_ge(low_ready.sem, low_ready.done(g - 2))
                        for b in range(NB):
                            last = nc.tensor.transpose(psT[u][:, b * P:(b + 1) * P], xa[u][:, b, 0:D], ident)
                        last.then_inc(t_done.sem, 1)
                    for u in range(2):
                        g = it * 2 + u
                        pe.wait_ge(low_ready.sem, low_ready.done(g))
                        for k in range(FK):
                            m = it * (2 * FK) + (u * FK + k)
                            at = slice(k * D, (k + 1) * D)
                            pe.wait_ge(gelu_ready.sem, gelu_ready.done(m - FK))
                            product(psU[k][:, :], WS[:, 0, at], WS[:, 1, at], xT[u][0], xT[u][1], True, True)\
                                .then_inc(up_done.sem, 1)
                        pe.wait_ge(y_ready.sem, y_ready.done(g - 1))
                        for k in range(FK):
                            m = it * (2 * FK) + (u * FK + k)
                            at = slice(k * D, (k + 1) * D)
                            pe.wait_ge(split_ready.sem, split_ready.done(m))
                            product(psO[:, :], WS[:, 2, at], WS[:, 3, at], gs[k][0], gs[k][1], k == 0, k == FK - 1)\
                                .then_inc(down_done.sem, 1)
                        pe.wait_ge(y_ready.sem, y_ready.done(g))
                        pe.wait_ge(x_ready.sem, x_ready.done(g - 1))
                        for b in range(NB):
                            last = nc.tensor.transpose(psY[:, b * D:(b + 1) * D], yT[u][:, b * P:(b + 1) * P], ident)
                        last.then_inc(yt_done.sem, 1)

        free(2)
        take = carve()
        w1s = [take(2, FK * D, dt=F32R) for _ in range(2)]
        w2s = [take(2, FK * D, dt=F32R) for _ in range(2)]
        b1s = [take(FK) for _ in range(2)]
        b2s = [take(1) for _ in range(2)]
        xrow = [take(NQ, ROW) for _ in range(2)]
        xT = [[take(W, dt=F32R) for _ in range(2)] for _ in range(2)]
        gf = [take(W) for _ in range(2)]
        gs = [[take(W, dt=F32R) for _ in range(2)] for _ in range(FK)]
        yT = [take(W) for _ in range(2)]
        yrow = [take(NQ, D) for _ in range(2)]
        id_in = [take(NQ, dt=I32) for _ in range(2)]
        spare_by = [take(NQ) for _ in range(2)]
        id_out = [take(NQ, dt=I32) for _ in range(2)]
        LAST = BLOCKS - 1

        def over_blocks(eng, body):
            body(0, 0, at=0)
            with eng.Fori(0, (BLOCKS - 4) // 2) as it:
                body(it, 1)
                body(it + 1, 0)
            for n in range(BLOCKS - 3, BLOCKS):
                body(n // 2, n % 2, at=n)

        with nc.Block() as block:
            loaded = [sem(f"b_loaded{u}") for u in range(2)]
            sent = [sem(f"b_sent{u}") for u in range(2)]
            PER = 16 * NQ
            blocks_taken = sem("b_blocks_taken")
            t_done = steps("b_t_done", 2)
            ids_kept = steps("b_ids_kept", 2)
            ids_out = steps("b_ids_out", 2)
            high_ready = steps("b_high_ready", 2)
            low_ready = steps("b_low_ready", 2)
            w1_ready = steps("b_w1_ready", 2)
            w2_ready = steps("b_w2_ready", 2)
            up_done = steps("b_up_done", 2 * FK)
            gelu_ready = steps("b_gelu_ready", 2 * FK)
            ghigh_ready = steps("b_ghigh_ready", 2 * FK)
            split_ready = steps("b_split_ready", 2 * FK)
            down_done = steps("b_down_done", 2 * FK)
            y_ready = steps("b_y_ready", 2)
            yt_done = steps("b_yt_done", 2)
            row_ready = steps("b_row_ready", 2)
            psU, psO, psT, psY = banks[0:4], banks[4:6], banks[6], banks[7]

            def next_unit(q, u, k):
                k += 3
                return q, u + k // FK, k % FK

            def chunk(k):
                return slice(k * D, (k + 1) * D)

            @block.sync
            def _(sp):
                def load(q, u, d=0):
                    n = q * 2 + u + d
                    sp.wait_ge(t_done.sem, t_done.done(n - 2))
                    sp.wait_ge(ids_kept.sem, ids_kept.done(n - 2))
                    sp.dma_start(xrow[u], rows_dram.rearrange("(n q p) c -> p n q c", p=P, q=NQ)[:, bass.ds(n, 1)])\
                        .then_inc(loaded[u], 16)

                with sp.Fori(0, BLOCKS // 2) as q:
                    load(q, 0)
                    load(q, 1)

            @block.gpsimd
            def _(pool):
                with pool.Fori(0, BLOCKS // 2) as q:
                    for u in range(2):
                        n = q * 2 + u
                        pool.wait_ge(row_ready.sem, row_ready.done(n))
                        pool.wait_ge(ids_out.sem, ids_out.done(n))
                        pool.sem_inc(blocks_taken, 1)
                        for j in range(NQ):
                            at = id_out[u][:, j:j + 1].bitcast(U32)
                            nc.gpsimd.indirect_dma_start(outs_dram, bass.IndirectOffsetOnAxis(ap=at, axis=0),
                                                         yrow[u][:, j, :], None).then_inc(sent[u], 16)
                for u in range(2):
                    pool.wait_ge(sent[u], PER * (BLOCKS // 2))

            @block.tensor
            def _(pe):
                for s in (t_done, up_done, down_done, yt_done):
                    s.open(pe)

                def turn(q, u):
                    pe.wait_ge(loaded[u], q * 16 + 16)
                    pe.wait_ge(low_ready.sem, low_ready.done(q * 2 + (u - 1)))
                    for j in range(NQ):
                        last = nc.tensor.transpose(psT[:, j * P:(j + 1) * P], xrow[u][:, j, 0:D], ident)
                    last.then_inc(t_done.sem, 1)

                def up(q, v, k):
                    u = v % 2
                    m = q * (2 * FK) + (v * FK + k)
                    if k == 0:
                        pe.wait_ge(low_ready.sem, low_ready.done(q * 2 + v))
                        pe.wait_ge(w1_ready.sem, w1_ready.done(q * 2 + v))
                    pe.wait_ge(gelu_ready.sem, gelu_ready.done(m - FK))
                    product(psU[k][:, :], w1s[u][:, 0, chunk(k)], w1s[u][:, 1, chunk(k)], xT[u][0], xT[u][1], True, True)\
                        .then_inc(up_done.sem, 1)

                def down(q, u, k):
                    n = q * 2 + u
                    m = q * (2 * FK) + (u * FK + k)
                    if k == 0:
                        pe.wait_ge(w2_ready.sem, w2_ready.done(n))
                        pe.wait_ge(y_ready.sem, y_ready.done(n - 2))
                    pe.wait_ge(split_ready.sem, split_ready.done(m))
                    product(psO[u][:, :], w2s[u][:, 0, chunk(k)], w2s[u][:, 1, chunk(k)], gs[k][0], gs[k][1],
                            k == 0, k == FK - 1).then_inc(down_done.sem, 1)

                def turn_back(q, v):
                    u = v % 2
                    n = q * 2 + v
                    pe.wait_ge(y_ready.sem, y_ready.done(n))
                    pe.wait_ge(row_ready.sem, row_ready.done(n - 1))
                    for j in range(NQ):
                        last = nc.tensor.transpose(psY[:, j * D:(j + 1) * D], yT[u][:, j * P:(j + 1) * P], ident)
                    last.then_inc(yt_done.sem, 1)

                def body(q, u, at=None):
                    for k in range(FK):
                        if at != LAST or k == 0:
                            up(*next_unit(q, u, k))
                        down(q, u, k)
                        if k == 0 and at != 0:
                            turn_back(q, u - 1)
                        if k == 2 and (at is None or at + 2 <= LAST):
                            turn(q + 1, u)

                turn(0, 0)
                turn(0, 1)
                for k in range(3):
                    up(0, 0, k)
                over_blocks(pe, body)
                turn_back(LAST // 2, LAST % 2)

            @block.scalar
            def _(act):
                for s in (high_ready, w1_ready, w2_ready, gelu_ready, y_ready):
                    s.open(act)

                def expert_of(n):
                    return nc.scalar.value_load(owner[0:1, bass.ds(n, 1)], min_val=0, max_val=E1 - 1)

                def take_w1(q, u):
                    n = q * 2 + u
                    e = expert_of(n)
                    act.wait_ge(up_done.sem, up_done.done(q * (2 * FK) + ((u - 2) * FK + FK - 1)))
                    act.wait_ge(gelu_ready.sem, gelu_ready.done(q * (2 * FK) + ((u - 2) * FK + FK - 1)))
                    nc.scalar.copy(b1s[u], biases[:, bass.ds(e, 1), 0:FK])
                    nc.scalar.copy(w1s[u], WB[:, bass.ds(e, 1), 0:2, :].bitcast(F32)).then_inc(w1_ready.sem, 1)

                def take_w2(q, v):
                    u = v % 2
                    n = q * 2 + v
                    e = expert_of(n)
                    act.wait_ge(down_done.sem, down_done.done(q * (2 * FK) + ((v - 2) * FK + FK - 1)))
                    act.wait_ge(y_ready.sem, y_ready.done(q * 2 + (v - 2)))
                    nc.scalar.copy(b2s[u], biases[:, bass.ds(e, 1), FK:FK + 1])
                    nc.scalar.copy(w2s[u], WB[:, bass.ds(e, 1), 2:4, :].bitcast(F32)).then_inc(w2_ready.sem, 1)

                def high(q, u):
                    act.wait_ge(t_done.sem, t_done.done(q * 2 + u))
                    act.wait_ge(up_done.sem, up_done.done(q * (2 * FK) + ((u - 2) * FK + FK - 1)))
                    nc.scalar.copy(xT[u][0], psT[:, :]).then_inc(high_ready.sem, 1)

                def gelu(q, v, k):
                    u = v % 2
                    m = q * (2 * FK) + (v * FK + k)
                    if k == 0:
                        act.wait_ge(w1_ready.sem, w1_ready.done(q * 2 + v))
                    act.wait_ge(up_done.sem, up_done.done(m))
                    act.wait_ge(split_ready.sem, split_ready.done(m - 2))
                    nc.scalar.activation(gf[k % 2], psU[k][:, :], ACT.Gelu, bias=b1s[u][:, k:k + 1])\
                        .then_inc(gelu_ready.sem, 1)

                def output(q, v):
                    u = v % 2
                    n = q * 2 + v
                    act.wait_ge(w2_ready.sem, w2_ready.done(n))
                    act.wait_ge(down_done.sem, down_done.done(q * (2 * FK) + (v * FK + FK - 1)))
                    act.wait_ge(yt_done.sem, yt_done.done(n - 2))
                    nc.scalar.activation(yT[u], psO[u][:, :], ACT.Identity, bias=b2s[u]).then_inc(y_ready.sem, 1)

                def body(q, u, at=None):
                    for k in range(FK):
                        if k == 0 and at != 0:
                            output(q, u - 1)
                        if at != LAST or k == 0:
                            gelu(*next_unit(q, u, k))
                        if k == 1 and at != LAST:
                            take_w2(q, u + 1)
                        if k == 2 and (at is None or at + 2 <= LAST):
                            high(q + 1, u)
                        if k == 3 and (at is None or at + 2 <= LAST):
                            take_w1(q + 1, u)

                take_w1(0, 0)
                high(0, 0)
                take_w2(0, 0)
                take_w1(0, 1)
                high(0, 1)
                for k in range(3):
                    gelu(0, 0, k)
                over_blocks(act, body)
                output(LAST // 2, LAST % 2)

            @block.vector
            def _(dve):
                for s in (ids_kept, ids_out, low_ready, ghigh_ready, split_ready, row_ready):
                    s.open(dve)

                def low(q, u):
                    dve.wait_ge(high_ready.sem, high_ready.done(q * 2 + u))
                    nc.vector.tensor_tensor(xT[u][1], psT[:, :], xT[u][0].bitcast(F32), ALU.subtract)\
                        .then_inc(low_ready.sem, 1)

                def keep_ids(q, u):
                    dve.wait_ge(loaded[u], q * 16 + 16)
                    dve.wait_ge(ids_out.sem, ids_out.done(q * 2 + (u - 2)))
                    nc.vector.tensor_scalar(spare_by[u], xrow[u][:, :, D].bitcast(I32), float(2 * TOKENS),
                                            cst("blkrow")[:, bass.ds(q * 2 + u, 1)], ALU.is_ge, ALU.mult)
                    nc.vector.tensor_copy(id_in[u], xrow[u][:, :, D].bitcast(I32)).then_inc(ids_kept.sem, 1)

                def pass_ids(q, u):
                    dve.wait_ge(ids_kept.sem, ids_kept.done(q * 2 + u))
                    dve.wait_ge(sent[u], q * PER)
                    nc.vector.tensor_tensor(id_out[u], id_in[u], spare_by[u], ALU.add).then_inc(ids_out.sem, 1)

                def split(q, v, k):
                    m = q * (2 * FK) + (v * FK + k)
                    dve.wait_ge(gelu_ready.sem, gelu_ready.done(m))
                    dve.wait_ge(down_done.sem, down_done.done(m - FK))
                    nc.vector.tensor_copy(gs[k][0], gf[k % 2]).then_inc(ghigh_ready.sem, 1)
                    dve.wait_ge(ghigh_ready.sem, ghigh_ready.done(m))
                    nc.vector.tensor_tensor(gs[k][1], gf[k % 2], gs[k][0].bitcast(F32), ALU.subtract)\
                        .then_inc(split_ready.sem, 1)

                def rows(q, v, q_used):
                    u = v % 2
                    dve.wait_ge(yt_done.sem, yt_done.done(q * 2 + v))
                    dve.wait_ge(sent[u], q_used * PER)
                    nc.vector.tensor_copy(yrow[u].rearrange("p a b -> p (a b)"), psY[:, :]).then_inc(row_ready.sem, 1)

                def body(q, u, at=None):
                    for k in range(FK):
                        if at != LAST or k == 0:
                            split(*next_unit(q, u, k))
                        if k == 1 and at != 0:
                            rows(q, u - 1, q if u else q - 1)
                        if k == 2 and (at is None or at + 2 <= LAST):
                            low(q + 1, u)
                        if k == 3:
                            pass_ids(q, u)
                            if at is None or at + 2 <= LAST:
                                keep_ids(q + 1, u)

                for u in range(2):
                    keep_ids(0, u)
                    low(0, u)
                for k in range(3):
                    split(0, 0, k)
                over_blocks(dve, body)
                rows(LAST // 2, LAST % 2, LAST // 2)

        free()
        take = carve()
        ys = [take(2, NB, D) for _ in range(2)]
        with nc.Block() as block:
            loaded = [sem(f"z_loaded{u}") for u in range(2)]
            one_added = steps("z_one_added", 2)
            x_ready = steps("z_x_ready", 2)

            @block.sync
            def _(sp):
                with sp.Fori(0, G // 2) as q:
                    for u in range(2):
                        g = q * 2 + u
                        sp.wait_ge(x_ready.sem, x_ready.done(g - 2))
                        for k in range(2):
                            sp.dma_start(ys[u][:, k], outs_dram[0:2 * TOKENS, :].rearrange(
                                "(k b p) d -> k p b d", k=2, p=P)[k, :, bass.ds(g * NB, NB), :])\
                                .then_inc(loaded[u], 16)

            @block.vector
            def _(dve):
                one_added.open(dve)
                x_ready.open(dve)
                with dve.Fori(0, G // 2) as q:
                    for u in range(2):
                        g = q * 2 + u
                        dve.wait_ge(loaded[u], q * 32 + 32)
                        for k, s in ((0, one_added), (1, x_ready)):
                            for b in range(NB):
                                xb_ = X[:, bass.ds(g * W + b * D, D)]
                                ins = nc.vector.scalar_tensor_tensor(xb_, ys[u][:, k, b, :],
                                                                     pairw[:, k, bass.ds(g * NB + b, 1)], xb_,
                                                                     ALU.mult, ALU.add)
                            ins.then_inc(s.sem, 1)
                            if k == 0:
                                dve.wait_ge(s.sem, s.done(g))

            @block.scalar
            def _(act):
                with act.Fori(0, G) as g:
                    act.wait_ge(x_ready.sem, x_ready.done(g))
                    act.dma_start(out[:, cols(g)], X[:, cols(g)]).then_inc(s_out, 16)
                act.wait_ge(s_out, 16 * G)
        free(len(scopes))


def kernel(**inputs):
    import concourse.bacc as bacc
    from concourse.bass_utils import run_bass_kernel_spmd

    a = {k: np.asarray(v) for k, v in inputs.items()}

    def column(v):
        return v.reshape(-1, 1)

    def rows(v, n=P):
        return np.broadcast_to(v.reshape(1, -1), (n, v.size))

    def pad(v):
        full = np.zeros((P, v.shape[1]), np.float32)
        full[:v.shape[0]] = v
        return full

    ahead = np.zeros((D, HEADS), np.float32)
    for h in range(HEADS):
        ahead[h * (D // HEADS):(h + 1) * (D // HEADS), h] = a["L0_gnn_a"][h]
    idx = np.arange(P, dtype=np.float32)
    parts = {
        "ident": np.eye(P, dtype=np.float32),
        "iota": rows(np.arange(EDGES, dtype=np.float32)),
        "pidx": column(idx),
        "eidx": np.stack([idx + P * c for c in range(EC)], 1),
        "below": np.triu(np.ones((P, P), np.float32), 1),
        "blk": rows(np.arange(BLOCKS, dtype=np.float32)),
        "blkrow": rows(np.arange(BLOCKS, dtype=np.float32) * BLOCK),
        "ones": np.ones((P, P), np.float32),
        "rank0": rows(np.arange(E0, 0, -1, dtype=np.float32)),
        "rank1": rows(np.arange(E1, 0, -1, dtype=np.float32)),
        "wq": a["L0_gnn_W_lin"].T, "wv": a["L0_gnn_W_val"].T, "wout": a["L0_gnn_W_out"].T,
        "ahead": ahead, "adj": a["adj"], "adjT": a["adj"].T,
        "rw1": a["L0_ffn_router_w1"], "rb1": pad(column(a["L0_ffn_router_b1"])),
        "rw2": pad(a["L0_ffn_router_w2"]), "rb2": rows(a["L0_ffn_router_b2"]),
        "wg0": a["L1_gnn_Wg0"], "bg0": rows(a["L1_gnn_bg0"]),
        "wg1": a["L1_gnn_Wg1"], "bg1": rows(a["L1_gnn_bg1"]), "wr": a["L1_ffn_Wr"],
    }
    small = np.concatenate([parts[n] for n, _ in SMALL], 1)
    sd = np.stack([a["L0_gnn_src"], a["L0_gnn_dst"]])
    edges = np.concatenate([rows(sd), sd.reshape(2, EC, P).transpose(2, 1, 0).reshape(P, 2 * EC)], 1)
    ffn0 = np.concatenate(
        [a["L0_ffn_expert_w1"].transpose(1, 0, 2).reshape(D, -1),
         a["L0_ffn_expert_w2"].transpose(1, 0, 2).reshape(D, -1),
         a["L0_ffn_expert_w3"].transpose(1, 0, 2).reshape(D, -1),
         a["L0_ffn_expert_b1"].T, a["L0_ffn_expert_b2"].T, pad(a["L0_ffn_expert_b3"])], 1)
    lstm = np.concatenate(
        [a["L1_gnn_Wih"].transpose(2, 0, 1).reshape(D, -1), a["L1_gnn_Whh"].transpose(2, 0, 1).reshape(D, -1),
         a["L1_gnn_bih"].reshape(-1, D).T, a["L1_gnn_bhh"].reshape(-1, D).T], 1)
    w1 = np.concatenate([a["L1_ffn_W1p"], a["L1_ffn_W1s"][None]], 0)
    w2 = np.concatenate([a["L1_ffn_W2p"], a["L1_ffn_W2s"][None]], 0)
    b1 = np.concatenate([a["L1_ffn_b1p"], a["L1_ffn_b1s"][None]], 0)
    b2 = np.concatenate([a["L1_ffn_b2p"], a["L1_ffn_b2s"][None]], 0)
    ffn1 = np.concatenate(
        [np.concatenate([w1, w2.reshape(E1 + 1, FK, D, D).transpose(0, 2, 1, 3).reshape(E1 + 1, D, FK * D)], 2)
         .transpose(1, 0, 2).reshape(D, -1),
         np.concatenate([b1.reshape(E1 + 1, FK, D), b2.reshape(E1 + 1, 1, D)], 1).transpose(2, 0, 1).reshape(D, -1)], 1)
    tokid = (np.arange(B)[None] * P + np.arange(P)[:, None]).astype(np.int32)
    spare = (2 * TOKENS + np.arange(NQ)[None] * P + np.arange(P)[:, None]).astype(np.int32)
    ids = np.concatenate([tokid, tokid + TOKENS, spare], 1)
    arrays = {"xT_dram": a["x"].transpose(1, 0, 2).reshape(P, B * D), "small_dram": small, "edges_dram": edges,
              "ids_dram": ids,
              "ffn0_dram": ffn0, "lstm_dram": lstm, "ffn1_dram": ffn1}
    arrays = {k: np.ascontiguousarray(v) for k, v in arrays.items()}

    nc = bacc.Bacc("TRN2", target_bir_lowering=False, num_devices=1)
    args = [nc.dram_tensor(n, v.shape, mybir.dt.from_np(v.dtype), kind="ExternalInput").ap() for n, v in arrays.items()]
    out = nc.dram_tensor("out_0_dram", (P, B * D), F32, kind="ExternalOutput").ap()
    build(nc, *args, out, STOP)
    r = run_bass_kernel_spmd(nc, [arrays], core_ids=[0])
    return r.results[0]["out_0_dram"].reshape(P, B, D).transpose(1, 0, 2)
```

```python
from contextlib import ExitStack

import numpy as np

import concourse.bass as bass
from concourse import mybir

ALU = mybir.AluOpType
ACT = mybir.ActivationFunctionType
AXX = mybir.AxisListType.X
F32 = mybir.dt.float32
I32 = mybir.dt.int32
U32 = mybir.dt.uint32
F32R = mybir.dt.float32r

P = 128
B = 128
D = 128
NB = 4
G = B // NB
W = NB * D
HEADS = 4
EDGES = 256
EC = EDGES // P
E0 = 6
E1 = 8
FK = 4
SKIPS = 4
BIG = 3.0e38
LN_EPS = 1e-5
TOKENS = B * P
BLOCK = 512
NQ = BLOCK // P
BLOCKS = 2 * TOKENS // BLOCK + E1
SLOTS = BLOCKS * BLOCK
ROW = 132
LOG_EPS = 1e-8

SMALL = [("ident", 128), ("iota", 256), ("pidx", 1), ("eidx", EC), ("ones", 128),
         ("below", P), ("blk", BLOCKS), ("blkrow", BLOCKS), ("pos", NQ), ("rank0", E0), ("rank1", E1),
         ("wq", D), ("wv", D), ("wout", D), ("ahead", HEADS), ("adj", P), ("adjT", P),
         ("rw1", 64), ("rb1", 1), ("rw2", E0), ("rb2", E0),
         ("wg0", D), ("bg0", D), ("wg1", D), ("bg1", D), ("wr", E1)]
SMALL_AT = {}
SMALL_COLS = 0
for _name, _n in SMALL:
    SMALL_AT[_name] = (SMALL_COLS, SMALL_COLS + _n)
    SMALL_COLS += _n
FFN0_COLS = E0 * 3 * D + E0 * 2 + D
LSTM_COLS = SKIPS * 8 * D + SKIPS * 8
EW = 2 * FK * D
FFN1_COLS = (E1 + 1) * EW + (E1 + 1) * (FK + 1)


class Steps:

    def __init__(self, sem, ahead=0):
        self.sem, self.ahead = sem, ahead

    def open(self, eng):
        eng.sem_inc(self.sem, self.ahead)

    def done(self, n):
        return n + (self.ahead + 1)


class Turn:

    def __init__(self, it, u, at=None):
        self.it, self.u, self.at = it, u, at

    def has(self, k):
        return self.at is None or 0 <= self.at + k < G

    def group(self, k):
        return self.it * 2 + (self.u + k), (self.u + k) % 2


def over_groups(eng, body, ahead, behind=0):
    first = (behind + 1) // 2
    stop = (G - 2 - ahead) // 2 + 1
    for at in range(-ahead, 2 * first):
        body(Turn(at // 2, at % 2, at))
    with eng.Fori(first, stop) as it:
        for u in range(2):
            body(Turn(it, u))
    for at in range(2 * stop, G + behind):
        body(Turn(at // 2, at % 2, at))


def build(nc, xT, small, edges, ids, ffn0, lstm, ffn1, out):
    ctx = ExitStack()
    with ctx:
        def sb(name, shape, dt=F32):
            return ctx.enter_context(nc.sbuf_tensor(name, shape, dt))

        phase_sems = []

        def kept_sem(name):
            return ctx.enter_context(nc.semaphore(name))

        def sem(name):
            phase_sems.append(nc.alloc_semaphore(name=name))
            return phase_sems[-1]

        def renew_semaphores():
            nc.clear_and_free_semaphores(phase_sems)
            phase_sems.clear()
            nc.all_engine_barrier()

        def steps(name, ahead=0):
            return Steps(sem(name), ahead)

        X = sb("X", [P, B * D])
        small_sb = sb("small_sb", [P, SMALL_COLS])
        STAT = sb("STAT", [P, B, 6])
        MEAN = sb("MEAN", [P, B])
        RSTD = sb("RSTD", [P, B])
        ids_sb = sb("ids_sb", [P, B + 2 * NQ], I32)
        fill = sb("fill", [P, NQ, ROW])
        NT = sb("NT", [P, 2, B])
        banks = [ctx.enter_context(nc.psum_tensor(f"bank{i}", [P, 512], F32)) for i in range(8)]

        def cst(name):
            a, b = SMALL_AT[name]
            return small_sb[:, a:b]

        scopes = []

        def free(n=1):
            for _ in range(n):
                scopes.pop().close()

        def carve():
            scope = ExitStack()
            scopes.append(scope)

            def take(*shape, dt=F32):
                named[0] += 1
                t = scope.enter_context(nc.sbuf_tensor(f"t{named[0]}", [P, *shape], dt))
                return t[tuple([slice(None)] * (len(shape) + 1))]
            return take

        named = [0]

        ident = cst("ident")
        X3 = X[:, :].rearrange("p (b d) -> p b d", d=D)

        s_small = kept_sem("s_small")
        s_edges = kept_sem("s_edges")
        s_ids = kept_sem("s_ids")
        s_x = [kept_sem(f"s_x{i}") for i in range(8)]
        s_ffn0 = kept_sem("s_ffn0")
        s_lstm = kept_sem("s_lstm")
        s_fill = kept_sem("s_fill")
        rows_dram = nc.dram_tensor("rows_scratch", (SLOTS, ROW), F32, kind="Internal").ap()
        outs_dram = nc.dram_tensor("outs_scratch", (2 * TOKENS + SLOTS, D), F32, kind="Internal").ap()
        s_out = kept_sem("s_out")
        s_chain = kept_sem("s_chain")
        chained = [0]

        def link(ins):
            chained[0] += 1
            ins.then_inc(s_chain, 1)
            nc.vector.wait_ge(s_chain, chained[0])

        def group_stats(g):
            for b in range(NB):
                ins = nc.vector.bn_stats(STAT[:, bass.ds(g * NB + b, 1), :], X3[:, bass.ds(g * NB + b, 1), :])
            return ins

        def finish_rstd(tag):
            ve_ready, root_ready = sem("ve" + tag), sem("root" + tag)
            with nc.Block() as block:
                @block.vector
                def _(dve):
                    even, odd = STAT[:, :, 1], STAT[:, :, 4]
                    link(nc.vector.tensor_tensor(MEAN[:, :], even, odd, ALU.add))
                    link(nc.vector.tensor_scalar(MEAN[:, :], MEAN[:, :], 0.5, None, ALU.mult))
                    link(nc.vector.tensor_tensor(NT[:, 1, :], even, odd, ALU.subtract))
                    link(nc.vector.tensor_tensor(NT[:, 1, :], NT[:, 1, :], NT[:, 1, :], ALU.mult))
                    link(nc.vector.tensor_scalar(NT[:, 1, :], NT[:, 1, :], 0.25, LN_EPS, ALU.mult, ALU.add))
                    link(nc.vector.tensor_tensor(NT[:, 0, :], STAT[:, :, 2], STAT[:, :, 5], ALU.add))
                    nc.vector.scalar_tensor_tensor(NT[:, 0, :], NT[:, 0, :], 1.0 / D, NT[:, 1, :], ALU.mult, ALU.add)\
                        .then_inc(ve_ready, 1)
                    dve.wait_ge(root_ready, 1)
                    link(nc.vector.reciprocal(RSTD[:, :], NT[:, 1, :]))
                    link(nc.vector.tensor_tensor(NT[:, 1, :], RSTD[:, :], RSTD[:, :], ALU.mult))
                    link(nc.vector.tensor_tensor(NT[:, 1, :], NT[:, 1, :], NT[:, 0, :], ALU.mult))
                    link(nc.vector.tensor_scalar(NT[:, 1, :], NT[:, 1, :], -0.5, 1.5, ALU.mult, ALU.add))
                    link(nc.vector.tensor_tensor(RSTD[:, :], RSTD[:, :], NT[:, 1, :], ALU.mult))

                @block.scalar
                def _(act):
                    act.wait_ge(ve_ready, 1)
                    nc.scalar.activation(NT[:, 1, :], NT[:, 0, :], ACT.Sqrt).then_inc(root_ready, 1)

        def normalise(dst, g):
            for b in range(NB):
                ins = nc.vector.tensor_scalar(dst[:, b * D:(b + 1) * D], X3[:, bass.ds(g * NB + b, 1), :],
                                              MEAN[:, bass.ds(g * NB + b, 1)], RSTD[:, bass.ds(g * NB + b, 1)],
                                              ALU.subtract, ALU.mult)
            return ins

        def cols(g):
            return bass.ds(g * W, W)

        def turn(pe, g, v, src, banks_, src_ready, bank_used, done):
            pe.wait_ge(src_ready.sem, src_ready.done(g))
            pe.wait_ge(bank_used.sem, bank_used.done(g - 2))
            for b in range(NB):
                last = nc.tensor.transpose(banks_[v][:, b * P:(b + 1) * P], src[:, v, b * P:(b + 1) * P], ident)
            last.then_inc(done.sem, 1)

        def product(dst, w_high, w_low, x_high, x_low, start, stop):
            nc.tensor.matmul(dst, w_low, x_high, start=start, stop=False)
            nc.tensor.matmul(dst, w_high, x_low, start=False, stop=False)
            return nc.tensor.matmul(dst, w_high, x_high, start=False, stop=stop)

        take = carve()
        Y = take(B * D)
        Y3 = Y.rearrange("p (b d) -> p b d", d=D)
        take = carve()
        sd_int = take(2 * EDGES + 2 * EC, dt=I32)
        sd = take(2 * EDGES + 2 * EC)
        perm = take(EC, EDGES)
        srcB = take(EC, P)
        dstB = take(EC, P)
        rowS = take(EDGES)
        rowD = take(EDGES)
        colSD = take(EC, 2)
        ohsT = take(EDGES)
        ohdT = take(EDGES)
        ohsum = take(EDGES)
        ohs = take(EC, P)
        ohd = take(EC, P)
        reset = take(EDGES)
        same = take(EC, EDGES)
        lastsel = take(EC, EDGES)
        key = take(EDGES)
        keyc = take(EC)
        rank = take(EC)
        later = take(EC)
        islast = take(EC)
        adjv = take(EC)
        logadj = take(EC)
        logeps = take(1)
        tmp = take(EC, EDGES)
        S = take(EC, B * HEADS)
        att = take(EC, B * HEADS)

        with nc.Block() as block:
            fill_ready = sem("fill_ready")
            parts = len(s_x)
            perm_ready, sorted_done, oh_ready, adj_done, adj_ready = (
                sem(n) for n in ("perm_ready", "sorted_done", "oh_ready", "adj_done", "adj_ready"))

            @block.sync
            def _(sp):
                sp.dma_start(sd_int, edges).then_inc(s_edges, 16)
                sp.dma_start(small_sb[:, :], small).then_inc(s_small, 16)
                sp.dma_start(ids_sb[:, :], ids).then_inc(s_ids, 16)
                n = B * D // parts
                for i in range(parts):
                    sp.dma_start(X[:, i * n:(i + 1) * n], xT[:, i * n:(i + 1) * n]).then_inc(s_x[i], 16)

            @block.gpsimd
            def _(pool):
                nc.gpsimd.memset(fill[:, :, :], 0.0).then_inc(fill_ready, 1)
                pool.wait_ge(fill_ready, 1)
                pool.wait_ge(s_ids, 16)
                nc.gpsimd.tensor_copy(fill[:, :, D:D + 2].rearrange("p q c -> p c q").bitcast(I32),
                                      ids_sb[:, B:B + 2 * NQ].rearrange("p (c q) -> p c q", c=2))\
                    .then_inc(fill_ready, 1)

            @block.vector
            def _(dve):
                ts, tt, stt = nc.vector.tensor_scalar, nc.vector.tensor_tensor, nc.vector.scalar_tensor_tensor

                def stats_of(first, end):
                    for i in range(first, end):
                        dve.wait_ge(s_x[i], 16)
                        for g in range(i * (G // parts), (i + 1) * (G // parts)):
                            group_stats(g)

                dve.wait_ge(s_small, 16)
                dve.wait_ge(s_edges, 16)
                iota = cst("iota")
                ones = cst("ones")
                nc.vector.memset(logeps, LOG_EPS)
                link(nc.vector.tensor_copy(sd, sd_int))
                for c in range(EC):
                    scol = sd[:, 2 * EDGES + 2 * c:2 * EDGES + 2 * c + 1]
                    dcol = sd[:, 2 * EDGES + 2 * c + 1:2 * EDGES + 2 * c + 2]
                    stt(keyc[:, c:c + 1], scol, float(EDGES), cst("eidx")[:, c:c + 1], ALU.mult, ALU.add)
                    ts(srcB[:, c, :], ones, scol, None, ALU.mult)
                    ts(dstB[:, c, :], ones, dcol, None, ALU.mult)
                link(stt(key, sd[:, 0:EDGES], float(EDGES), iota, ALU.mult, ALU.add))
                for c in range(EC):
                    ins = ts(tmp[:, c, :], key, keyc[:, c:c + 1], None, ALU.is_lt)
                link(ins)
                for c in range(EC):
                    ins = nc.vector.reduce_sum(rank[:, c:c + 1], tmp[:, c, :], AXX)
                link(ins)
                for c in range(EC):
                    ins = ts(perm[:, c, :], iota, rank[:, c:c + 1], None, ALU.is_equal)
                ins.then_inc(perm_ready, 1)
                stats_of(0, 3)
                dve.wait_ge(sorted_done, 1)
                nc.vector.tensor_copy(rowS, banks[0][:, 0:EDGES])
                nc.vector.tensor_copy(rowD, banks[1][:, 0:EDGES])
                nc.vector.tensor_copy(colSD.rearrange("p a b -> p (a b)"), banks[2][:, 0:2 * EC])
                link(nc.vector.memset(reset, 0.0))
                ts(ohsT, rowS, cst("pidx"), None, ALU.is_equal)
                ts(ohdT, rowD, cst("pidx"), None, ALU.is_equal)
                for c in range(EC):
                    ts(ohs[:, c, :], iota[:, 0:P], colSD[:, c, 0:1], None, ALU.is_equal)
                    ts(ohd[:, c, :], iota[:, 0:P], colSD[:, c, 1:2], None, ALU.is_equal)
                    ts(same[:, c, :], rowS, colSD[:, c, 0:1], None, ALU.is_equal)
                    ts(tmp[:, c, :], iota, cst("eidx")[:, c:c + 1], None, ALU.is_gt)
                link(tt(reset[:, 1:EDGES], rowS[:, 1:EDGES], rowS[:, 0:EDGES - 1], ALU.not_equal))
                tt(ohsum, ohsT, ohdT, ALU.add).then_inc(oh_ready, 1)
                for c in range(EC):
                    tt(tmp[:, c, :], tmp[:, c, :], same[:, c, :], ALU.mult)
                link(ts(reset, reset, -BIG, None, ALU.mult))
                for c in range(EC):
                    ins = nc.vector.reduce_sum(later[:, c:c + 1], tmp[:, c, :], AXX)
                link(ins)
                link(ts(islast, later, 0.0, None, ALU.is_equal))
                for c in range(EC):
                    ins = ts(lastsel[:, c, :], same[:, c, :], islast[:, c:c + 1], None, ALU.mult)
                stats_of(3, 5)
                dve.wait_ge(adj_done, 1)
                for c in range(EC):
                    ins = tt(tmp[:, c, 0:P], banks[3][:, c * P:(c + 1) * P], ohd[:, c, :], ALU.mult)
                link(ins)
                for c in range(EC):
                    ins = nc.vector.reduce_sum(adjv[:, c:c + 1], tmp[:, c, 0:P], AXX)
                ins.then_inc(adj_ready, 1)
                stats_of(5, parts)

            @block.tensor
            def _(pe):
                pe.wait_ge(s_small, 16)
                pe.wait_ge(perm_ready, 1)
                for dst, src in ((banks[0], srcB), (banks[1], dstB)):
                    for c in range(EC):
                        nc.tensor.matmul(dst[:, 0:EDGES], src[:, c, :], perm[:, c, :], start=c == 0, stop=c == EC - 1)
                for r in range(EC):
                    for c in range(EC):
                        last = nc.tensor.matmul(banks[2][:, 2 * r:2 * r + 2], perm[:, c, r * P:(r + 1) * P],
                                                sd[:, 2 * EDGES + 2 * c:2 * EDGES + 2 * c + 2],
                                                start=c == 0, stop=c == EC - 1)
                last.then_inc(sorted_done, 1)
                pe.wait_ge(oh_ready, 1)
                for c in range(EC):
                    last = nc.tensor.matmul(banks[3][:, c * P:(c + 1) * P], ohsT[:, c * P:(c + 1) * P], cst("adj"),
                                            start=True, stop=True)
                last.then_inc(adj_done, 1)

            @block.scalar
            def _(act):
                act.wait_ge(adj_ready, 1)
                nc.scalar.activation(logadj, adjv, ACT.Ln, bias=logeps)

        finish_rstd("0")

        take = carve()
        xn = take(2, W)
        xnT = take(2, W)
        qs = [[take(W, dt=F32R) for _ in range(2)] for _ in range(2)]
        ends = take(EDGES, dt=F32R)
        s02 = take(2, 512)
        lr = take(4, 512)
        with nc.Block() as block:
            xn_ready = steps("a_xn_ready", 2)
            t_done = steps("a_t_done", 2)
            xnT_ready = steps("a_xnT_ready", 2)
            qv_done = steps("a_qv_done", 2)
            ends_ready = sem("a_ends_ready")
            q_high = steps("a_q_high", 2)
            q_ready = steps("a_q_ready", 2)
            v_ready = steps("a_v_ready", 2)
            pair_done = steps("a_pair_done", 4)
            low_ready = steps("a_low_ready", 4)
            lr_ready = steps("a_lr_ready", 4)
            score_done = steps("a_score_done", 2)
            score_used = steps("a_score_used", 2)
            psT = banks[0:2]
            psQ, psV = banks[2], banks[3]
            psG = banks[4:6]
            psS = banks[6:8]

            @block.vector
            def _(dve):
                for s in (xn_ready, q_ready, lr_ready, score_used):
                    s.open(dve)
                nc.vector.tensor_copy(ends, ohsum).then_inc(ends_ready, 1)

                def leaky(g, v, j):
                    k = 2 * v + j
                    dve.wait_ge(low_ready.sem, low_ready.done(g * 2 + j))
                    dve.wait_ge(score_done.sem, score_done.done(g - 2))
                    nc.vector.tensor_tensor(lr[:, k, :], psG[j][:, :], s02[:, j, :], ALU.max).then_inc(lr_ready.sem, 1)

                def keep_scores(g, v):
                    dve.wait_ge(score_done.sem, score_done.done(g))
                    for c in range(EC):
                        ins = nc.vector.tensor_scalar(S[:, c, bass.ds(g * (NB * HEADS), NB * HEADS)],
                                                      psS[v][:, c * 16:(c + 1) * 16], logadj[:, c:c + 1], None, ALU.add)
                    ins.then_inc(score_used.sem, 1)

                def keep_q(g, v):
                    dve.wait_ge(q_high.sem, q_high.done(g))
                    nc.vector.tensor_tensor(qs[v][1], psQ[:, :], qs[v][0].bitcast(F32), ALU.subtract)\
                        .then_inc(q_ready.sem, 1)

                def norm(g, v):
                    dve.wait_ge(t_done.sem, t_done.done(g - 2))
                    normalise(xn[:, v, :], g).then_inc(xn_ready.sem, 1)

                def body(t):
                    if t.has(3):
                        norm(*t.group(3))
                    if t.has(0):
                        leaky(*t.group(0), 0)
                    if t.has(1):
                        keep_q(*t.group(1))
                    if t.has(0):
                        leaky(*t.group(0), 1)
                    if t.has(-1):
                        keep_scores(*t.group(-1))

                over_groups(dve, body, ahead=3, behind=1)

            @block.scalar
            def _(act):
                for s in (xnT_ready, q_high, v_ready, low_ready):
                    s.open(act)

                def low(g, v, j):
                    act.wait_ge(pair_done.sem, pair_done.done(g * 2 + j))
                    act.wait_ge(lr_ready.sem, lr_ready.done(g * 2 + (j - 2)))
                    nc.scalar.mul(s02[:, j, :], psG[j][:, :], 0.2).then_inc(low_ready.sem, 1)

                def keep_q(g, v):
                    act.wait_ge(qv_done.sem, qv_done.done(g))
                    act.wait_ge(pair_done.sem, pair_done.done(g * 2 - 3))
                    nc.scalar.copy(qs[v][0], psQ[:, :]).then_inc(q_high.sem, 1)

                def keep_v(g, v):
                    nc.scalar.copy(Y[:, cols(g)], psV[:, :]).then_inc(v_ready.sem, 1)

                def keep_xn(g, v):
                    act.wait_ge(t_done.sem, t_done.done(g))
                    act.wait_ge(qv_done.sem, qv_done.done(g - 2))
                    nc.scalar.copy(xnT[:, v, :], psT[v][:, :]).then_inc(xnT_ready.sem, 1)

                def body(t):
                    if t.has(0):
                        low(*t.group(0), 0)
                    if t.has(2):
                        keep_xn(*t.group(2))
                    if t.has(1):
                        keep_q(*t.group(1))
                        keep_v(*t.group(1))
                    if t.has(0):
                        low(*t.group(0), 1)

                over_groups(act, body, ahead=3, behind=1)

            @block.tensor
            def _(pe):
                for s in (t_done, qv_done, pair_done, score_done):
                    s.open(pe)
                pe.wait_ge(ends_ready, 1)

                def pairs(g, v, j):
                    pe.wait_ge(q_ready.sem, q_ready.done(g))
                    pe.wait_ge(lr_ready.sem, lr_ready.done(g * 2 + (j - 2)))
                    for i in range(2):
                        b = 2 * j + i
                        for part in (1, 0):
                            last = nc.tensor.matmul(psG[j][:, i * EDGES:(i + 1) * EDGES],
                                                    qs[v][part][:, b * D:(b + 1) * D], ends,
                                                    start=part == 1, stop=part == 0)
                    last.then_inc(pair_done.sem, 1)

                def scores(g, v):
                    pe.wait_ge(lr_ready.sem, lr_ready.done(g * 2 + 1))
                    pe.wait_ge(score_used.sem, score_used.done(g - 2))
                    for b in range(NB):
                        for c in range(EC):
                            at = (b % 2) * EDGES + c * P
                            last = nc.tensor.matmul(psS[v][:, c * 16 + b * HEADS:c * 16 + (b + 1) * HEADS],
                                                    lr[:, 2 * v + b // 2, at:at + P], cst("ahead"),
                                                    start=True, stop=True)
                    last.then_inc(score_done.sem, 1)

                def project(g, v):
                    pe.wait_ge(xnT_ready.sem, xnT_ready.done(g))
                    pe.wait_ge(q_ready.sem, q_ready.done(g - 1))
                    pe.wait_ge(v_ready.sem, v_ready.done(g - 1))
                    for b in range(NB):
                        xb = xnT[:, v, b * P:(b + 1) * P]
                        nc.tensor.matmul(psQ[:, b * D:(b + 1) * D], xb, cst("wq"), start=True, stop=True)
                        last = nc.tensor.matmul(psV[:, b * D:(b + 1) * D], xb, cst("wv"), start=True, stop=True)
                    last.then_inc(qv_done.sem, 1)

                def body(t):
                    if t.has(0):
                        pairs(*t.group(0), 0)
                    if t.has(2):
                        turn(pe, *t.group(2), xn, psT, xn_ready, xnT_ready, t_done)
                    if t.has(1):
                        project(*t.group(1))
                    if t.has(0):
                        pairs(*t.group(0), 1)
                    if t.has(-1):
                        scores(*t.group(-1))

                over_groups(pe, body, ahead=3, behind=1)

        free()
        take = carve()
        rmax = take(EC, B * HEADS)
        ST = take(4, EDGES)
        RUN = take(4, EDGES)
        with nc.Block() as block:
            st_done, run_ready, back_done, back_ready, m_done, sub_ready, ex_ready, den_done = (
                sem(n) for n in ("st_done", "run_ready", "back_done", "back_ready", "m_done",
                                 "sub_ready", "ex_ready", "den_done"))

            @block.tensor
            def _(pe):
                for t in range(4):
                    for c in range(EC):
                        k = t * EC + c
                        last = nc.tensor.transpose(banks[k // 4][:, (k % 4) * P:(k % 4 + 1) * P],
                                                   S[:, c, t * P:(t + 1) * P], ident)
                last.then_inc(st_done, 1)
                pe.wait_ge(run_ready, 1)
                for c in range(EC):
                    for t in range(4):
                        last = nc.tensor.transpose(banks[2 + c][:, t * P:(t + 1) * P],
                                                   RUN[:, t, c * P:(c + 1) * P], ident)
                last.then_inc(back_done, 1)
                pe.wait_ge(back_ready, 1)
                for c in range(EC):
                    for k in range(EC):
                        last = nc.tensor.matmul(banks[4 + c][:, :], lastsel[:, k, c * P:(c + 1) * P], rmax[:, k, :],
                                                start=k == 0, stop=k == EC - 1)
                last.then_inc(m_done, 1)
                pe.wait_ge(ex_ready, 1)
                for c in range(EC):
                    for k in range(EC):
                        last = nc.tensor.matmul(banks[6 + c][:, :], same[:, k, c * P:(c + 1) * P], att[:, k, :],
                                                start=k == 0, stop=k == EC - 1)
                last.then_inc(den_done, 1)

            @block.vector
            def _(dve):
                dve.wait_ge(st_done, 1)
                for k in range(2):
                    link(nc.vector.tensor_copy(ST[:, 2 * k:2 * k + 2, :].rearrange("p a b -> p (a b)"), banks[k][:, :]))
                for t in range(4):
                    ins = nc.vector.tensor_tensor_scan(RUN[:, t, :], reset, ST[:, t, :], -BIG, ALU.add, ALU.max)
                ins.then_inc(run_ready, 1)
                dve.wait_ge(back_done, 1)
                for c in range(EC):
                    ins = nc.vector.tensor_copy(rmax[:, c, :], banks[2 + c][:, :])
                ins.then_inc(back_ready, 1)
                dve.wait_ge(m_done, 1)
                for c in range(EC):
                    ins = nc.vector.tensor_tensor(S[:, c, :], S[:, c, :], banks[4 + c][:, :], ALU.subtract)
                ins.then_inc(sub_ready, 1)
                dve.wait_ge(den_done, 1)
                for c in range(EC):
                    link(nc.vector.reciprocal(rmax[:, c, :], banks[6 + c][:, :]))
                    link(nc.vector.tensor_tensor(att[:, c, :], att[:, c, :], rmax[:, c, :], ALU.mult))

            @block.scalar
            def _(act):
                act.wait_ge(sub_ready, 1)
                for c in range(EC):
                    ins = nc.scalar.activation(att[:, c, :], S[:, c, :], ACT.Exp)
                ins.then_inc(ex_ready, 1)

        free()
        take = carve()
        wv = take(2, EC, W)
        yT = take(2, W)
        vs = [[take(W, dt=F32R) for _ in range(2)] for _ in range(2)]
        far = take(EDGES, dt=F32R)
        with nc.Block() as block:
            far_ready = sem("c_far_ready")
            vs_high = steps("c_vs_high", 2)
            vs_low = steps("c_vs_low", 2)
            val_done = steps("c_val_done", 4)
            wv_ready = steps("c_wv_ready", 4)
            y_done = steps("c_y_done", 2)
            yT_ready = steps("c_yT_ready", 2)
            o_done = steps("c_o_done", 2)
            o_used = steps("c_o_used", 2)
            psVal = banks[0:4]
            psY = banks[4:6]
            psO = banks[6:8]

            @block.tensor
            def _(pe):
                for s in (val_done, y_done, o_done):
                    s.open(pe)
                pe.wait_ge(far_ready, 1)

                def values(g, v, c):
                    pe.wait_ge(wv_ready.sem, wv_ready.done(g * 2 + (c - 4)))
                    pe.wait_ge(vs_low.sem, vs_low.done(g))
                    for part in (1, 0):
                        last = nc.tensor.matmul(psVal[2 * v + c][:, :], far[:, c * P:(c + 1) * P], vs[v][part],
                                                start=part == 1, stop=part == 0)
                    last.then_inc(val_done.sem, 1)

                def gather(g, v):
                    pe.wait_ge(wv_ready.sem, wv_ready.done(g * 2 + 1))
                    pe.wait_ge(yT_ready.sem, yT_ready.done(g - 2))
                    for b in range(NB):
                        for c in range(EC):
                            last = nc.tensor.matmul(psY[v][:, b * P:(b + 1) * P], wv[:, v, c, b * D:(b + 1) * D],
                                                    ohs[:, c, :], start=c == 0, stop=c == EC - 1)
                    last.then_inc(y_done.sem, 1)

                def project(g, v):
                    pe.wait_ge(yT_ready.sem, yT_ready.done(g))
                    pe.wait_ge(o_used.sem, o_used.done(g - 2))
                    for b in range(NB):
                        last = nc.tensor.matmul(psO[v][:, b * D:(b + 1) * D], yT[:, v, b * P:(b + 1) * P],
                                                cst("wout"), start=True, stop=True)
                    last.then_inc(o_done.sem, 1)

                def body(t):
                    if t.has(1):
                        for c in range(EC):
                            values(*t.group(1), c)
                    if t.has(-1):
                        project(*t.group(-1))
                    if t.has(0):
                        gather(*t.group(0))

                over_groups(pe, body, ahead=3, behind=1)

            @block.scalar
            def _(act):
                yT_ready.open(act)
                vs_high.open(act)

                def body(t):
                    if t.has(3):
                        g, v = t.group(3)
                        act.wait_ge(val_done.sem, val_done.done(g * 2 - 3))
                        nc.scalar.copy(vs[v][0], Y[:, cols(g)]).then_inc(vs_high.sem, 1)
                    if t.has(0):
                        g, v = t.group(0)
                        act.wait_ge(y_done.sem, y_done.done(g))
                        act.wait_ge(o_done.sem, o_done.done(g - 2))
                        nc.scalar.copy(yT[:, v, :], psY[v][:, :]).then_inc(yT_ready.sem, 1)

                over_groups(act, body, ahead=3, behind=1)

            @block.vector
            def _(dve):
                for s in (vs_low, wv_ready, o_used):
                    s.open(dve)
                nc.vector.tensor_copy(far, ohdT).then_inc(far_ready, 1)

                def weigh(g, v, c):
                    dve.wait_ge(val_done.sem, val_done.done(g * 2 + c))
                    dve.wait_ge(y_done.sem, y_done.done(g - 2))
                    weight = att[:, c, bass.ds(g * (NB * HEADS), NB * HEADS)].unsqueeze(2)\
                        .broadcast_to([P, NB * HEADS, D // HEADS])
                    nc.vector.tensor_tensor(
                        wv[:, v, c, :].rearrange("p (a b) -> p a b", b=D // HEADS),
                        psVal[2 * v + c][:, :].rearrange("p (a b) -> p a b", b=D // HEADS),
                        weight, ALU.mult).then_inc(wv_ready.sem, 1)

                def body(t):
                    if t.has(1):
                        for c in range(EC):
                            weigh(*t.group(1), c)
                    if t.has(-1):
                        g, v = t.group(-1)
                        dve.wait_ge(o_done.sem, o_done.done(g))
                        nc.vector.tensor_tensor(X[:, cols(g)], X[:, cols(g)], psO[v][:, :], ALU.add)\
                            .then_inc(o_used.sem, 1)
                    if t.has(3):
                        g, v = t.group(3)
                        dve.wait_ge(vs_high.sem, vs_high.done(g))
                        nc.vector.tensor_tensor(vs[v][1], Y[:, cols(g)], vs[v][0].bitcast(F32), ALU.subtract)\
                            .then_inc(vs_low.sem, 1)
                    if t.has(-1):
                        g, v = t.group(-1)
                        dve.wait_ge(o_used.sem, o_used.done(g))
                        group_stats(g)

                over_groups(dve, body, ahead=3, behind=1)

        def route(tag, logits, p, q, w, sel, small_t, rank_row, E, pair_softmax):
            exp_ready, pair_ready, shifted_ready, diff_ready = (
                sem(n + tag) for n in ("exp_ready", "pair_ready", "shifted_ready", "diff_ready"))

            def wide(v):
                return v.unsqueeze(2).broadcast_to([P, B, E])

            m, m1, m2, w1 = (small_t[:, i, :] for i in range(4))
            ranks = rank_row.unsqueeze(1).broadcast_to([P, B, E])
            tt, red = nc.vector.tensor_tensor, nc.vector.tensor_reduce
            with nc.Block() as block:
                @block.vector
                def _(dve):
                    link(red(m, logits, AXX, ALU.max))
                    tt(logits, logits, wide(m), ALU.subtract).then_inc(shifted_ready, 1)
                    dve.wait_ge(exp_ready, 1)
                    link(red(m, p, AXX, ALU.add))
                    link(nc.vector.reciprocal(m, m))
                    link(tt(p, p, wide(m), ALU.mult))

                    def first_of_largest(largest, chosen):
                        link(red(largest, p, AXX, ALU.max))
                        link(tt(q, p, wide(largest), ALU.is_equal))
                        link(tt(w, q, ranks, ALU.mult))
                        link(red(m, w, AXX, ALU.max))
                        link(tt(chosen, w, wide(m), ALU.is_equal))

                    first_of_largest(m1, sel)
                    link(nc.vector.scalar_tensor_tensor(p, sel, -2.0, p, ALU.mult, ALU.add))
                    first_of_largest(m2, q)
                    if pair_softmax:
                        tt(m2, m2, m1, ALU.subtract).then_inc(diff_ready, 1)
                        dve.wait_ge(pair_ready, 1)
                        link(nc.vector.tensor_scalar(m, m2, 1.0, None, ALU.add))
                        link(nc.vector.reciprocal(w1, m))
                        link(tt(m2, m2, w1, ALU.mult))
                        link(tt(sel, sel, wide(w1), ALU.mult))
                        link(tt(q, q, wide(m2), ALU.mult))
                        link(tt(sel, sel, q, ALU.add))
                    else:
                        link(tt(m, m1, m2, ALU.add))
                        link(nc.vector.reciprocal(m, m))
                        link(tt(w1, m1, m, ALU.mult))
                        link(tt(m2, m2, m, ALU.mult))

                @block.scalar
                def _(act):
                    act.wait_ge(shifted_ready, 1)
                    nc.scalar.activation(p, logits, ACT.Exp).then_inc(exp_ready, 1)
                    if pair_softmax:
                        act.wait_ge(diff_ready, 1)
                        nc.scalar.activation(m2, m2, ACT.Exp).then_inc(pair_ready, 1)

        free(2)
        finish_rstd("1")
        take = carve()
        ffn0_sb = take(FFN0_COLS)
        w3of = [[ffn0_sb[:, (l * E0 + e) * D:(l * E0 + e + 1) * D] for e in range(E0)] for l in range(3)]
        at = 3 * E0 * D
        b12 = [[ffn0_sb[:, at + l * E0 + e:at + l * E0 + e + 1] for e in range(E0)] for l in range(2)]
        b3rows = ffn0_sb[:, at + 2 * E0:at + 2 * E0 + D]
        mask0 = take(B, E0)
        take = carve()
        logits0 = take(B, E0)
        prob0 = take(B, E0)
        tq0 = take(B, E0)
        tw0 = take(B, E0)
        small_t = take(4, B)
        xn = take(2, W)
        rh = take(2, W)

        with nc.Block() as block:
            xn_ready = steps("d_xn_ready", 2)
            t_done = steps("d_t_done", 2)
            xnT_ready = steps("d_xnT_ready", 2)
            r_done = steps("d_r_done", 2)
            rh_ready = steps("d_rh_ready", 2)
            l_done = steps("d_l_done", 2)
            l_used = steps("d_l_used", 2)
            psT, psR, psL = banks[0:2], banks[2:4], banks[4:6]

            @block.sync
            def _(sp):
                sp.dma_start(ffn0_sb, ffn0).then_inc(s_ffn0, 16)

            @block.vector
            def _(dve):
                for s in (xn_ready, l_used):
                    s.open(dve)
                bias = cst("rb2").unsqueeze(1).broadcast_to([P, NB, E0])

                def body(t):
                    if t.has(4):
                        g, v = t.group(4)
                        dve.wait_ge(t_done.sem, t_done.done(g - 2))
                        normalise(xn[:, v, :], g).then_inc(xn_ready.sem, 1)
                    if t.has(-1):
                        g, v = t.group(-1)
                        dve.wait_ge(l_done.sem, l_done.done(g))
                        nc.vector.tensor_tensor(logits0[:, bass.ds(g * NB, NB), :],
                                                psL[v][:, 0:NB * E0].rearrange("p (a b) -> p a b", b=E0),
                                                bias, ALU.add).then_inc(l_used.sem, 1)

                over_groups(dve, body, ahead=4, behind=1)

            @block.scalar
            def _(act):
                for s in (xnT_ready, rh_ready):
                    s.open(act)

                def body(t):
                    if t.has(3):
                        g, v = t.group(3)
                        act.wait_ge(t_done.sem, t_done.done(g))
                        nc.scalar.copy(Y[:, cols(g)], psT[v][:, :]).then_inc(xnT_ready.sem, 1)
                    if t.has(1):
                        g, v = t.group(1)
                        act.wait_ge(r_done.sem, r_done.done(g))
                        act.wait_ge(l_done.sem, l_done.done(g - 2))
                        nc.scalar.activation(rh[0:64, v, :], psR[v][0:64, :], ACT.Relu, bias=cst("rb1")[0:64, :])\
                            .then_inc(rh_ready.sem, 1)

                over_groups(act, body, ahead=4, behind=1)

            @block.tensor
            def _(pe):
                for s in (t_done, r_done, l_done):
                    s.open(pe)

                def body(t):
                    if t.has(3):
                        turn(pe, *t.group(3), xn, psT, xn_ready, xnT_ready, t_done)
                    if t.has(1):
                        g, v = t.group(1)
                        pe.wait_ge(xnT_ready.sem, xnT_ready.done(g))
                        pe.wait_ge(rh_ready.sem, rh_ready.done(g - 2))
                        nc.tensor.matmul(psR[v][0:64, :], cst("rw1"), Y[:, cols(g)], start=True, stop=True)\
                            .then_inc(r_done.sem, 1)
                    if t.has(-1):
                        g, v = t.group(-1)
                        pe.wait_ge(rh_ready.sem, rh_ready.done(g))
                        pe.wait_ge(l_used.sem, l_used.done(g - 2))
                        for b in range(NB):
                            last = nc.tensor.matmul(psL[v][:, b * E0:(b + 1) * E0], rh[0:64, v, b * P:(b + 1) * P],
                                                    cst("rw2")[0:64, :], start=True, stop=True)
                        last.then_inc(l_done.sem, 1)

                over_groups(pe, body, ahead=4, behind=1)

        route("0", logits0, prob0, tq0, tw0, mask0, small_t, cst("rank0"), E0, True)

        free()
        take = carve()
        ys = [[take(W, dt=F32R) for _ in range(2)] for _ in range(2)]
        w12 = take(2, 2 * E0 * D, dt=F32R)
        h1 = take(2, W)
        h1s = [[take(W, dt=F32R) for _ in range(2)] for _ in range(3)]
        h2 = take(2, W)
        mk = take(2, NB * E0)
        mkT = take(2, W)
        with nc.Block() as block:
            w_high, w_low = sem("e_w_high"), sem("e_w_low")
            ys_high = steps("e_ys_high", 2)
            ys_low = steps("e_ys_low", 2)
            mk_ready = steps("e_mk_ready", 2)
            mt_done = steps("e_mt_done", 2)
            mkT_ready = steps("e_mkT_ready", 2)
            bias_done = steps("e_bias_done", 2)
            bias_used = steps("e_bias_used", 2)
            h1_done = steps("e_h1_done", 2 * E0)
            h1_ready = steps("e_h1_ready", 3)
            h1_high = steps("e_h1_high", 3)
            h1_low = steps("e_h1_low", 3)
            h2_done = steps("e_h2_done", 3)
            h2_ready = steps("e_h2_ready", 2)
            o_done = steps("e_o_done", 2)
            o_used = steps("e_o_used", 2)
            psH1, psH2, psO, psM = banks[0:3], banks[3:5], banks[5:7], banks[7]

            def ahead(e, by):
                return (e + by) // E0, (e + by) % E0

            @block.sync
            def _(sp):
                with sp.Fori(0, BLOCKS) as j:
                    sp.dma_start(rows_dram.rearrange("(n q p) c -> p n q c", p=P, q=NQ)[:, bass.ds(j, 1)],
                                 fill[:, :, :]).then_inc(s_fill, 16)

            @block.tensor
            def _(pe):
                pe.wait_ge(s_ffn0, 16)
                pe.wait_ge(w_high, 1)
                pe.wait_ge(w_low, 1)
                for s in (mt_done, bias_done, h1_done, h2_done, o_done):
                    s.open(pe)

                def layer1(g, v, e):
                    n = g * E0 + e
                    if e == 0:
                        pe.wait_ge(ys_low.sem, ys_low.done(g))
                    pe.wait_ge(h1_ready.sem, h1_ready.done(n - 3))
                    w = slice(e * D, (e + 1) * D)
                    product(psH1[e % 3][:, :], w12[:, 0, w], w12[:, 1, w], ys[v][0], ys[v][1], True, True)\
                        .then_inc(h1_done.sem, 1)

                def layer2(g, v, e):
                    n = g * E0 + e
                    pe.wait_ge(h1_low.sem, h1_low.done(n))
                    pe.wait_ge(h2_ready.sem, h2_ready.done(n - 2))
                    w = slice((E0 + e) * D, (E0 + e + 1) * D)
                    product(psH2[e % 2][:, :], w12[:, 0, w], w12[:, 1, w], h1s[e % 3][0], h1s[e % 3][1], True, True)\
                        .then_inc(h2_done.sem, 1)

                def layer3(g, v, e):
                    n = g * E0 + e
                    pe.wait_ge(h2_ready.sem, h2_ready.done(n))
                    pe.wait_ge(o_used.sem, o_used.done(n - 2))
                    for b in range(NB):
                        last = nc.tensor.matmul(psO[e % 2][:, b * D:(b + 1) * D], h2[:, e % 2, b * P:(b + 1) * P],
                                                w3of[2][e], start=True, stop=True)
                    last.then_inc(o_done.sem, 1)

                def turn_weights(g, v):
                    pe.wait_ge(mk_ready.sem, mk_ready.done(g))
                    pe.wait_ge(bias_used.sem, bias_used.done(g - 1))
                    for b in range(NB):
                        last = nc.tensor.transpose(psM[0:E0, b * P:(b + 1) * P], mk[:, v, b * E0:(b + 1) * E0], ident)
                    last.then_inc(mt_done.sem, 1)

                def biases3(g, v):
                    pe.wait_ge(mkT_ready.sem, mkT_ready.done(g))
                    for b in range(NB):
                        last = nc.tensor.matmul(psM[:, b * D:(b + 1) * D], mkT[0:E0, v, b * P:(b + 1) * P],
                                                b3rows[0:E0, :], start=True, stop=True)
                    last.then_inc(bias_done.sem, 1)

                def body(t):
                    for e in range(E0):
                        if t.has(0):
                            layer2(*t.group(0), e)
                        d, ee = ahead(e, 3)
                        if t.has(d):
                            layer1(*t.group(d), ee)
                        d, ee = ahead(e, -1)
                        if t.has(d):
                            layer3(*t.group(d), ee)
                        if e == 1 and t.has(1):
                            turn_weights(*t.group(1))
                        if e == 3 and t.has(1):
                            biases3(*t.group(1))

                over_groups(pe, body, ahead=1, behind=1)

            @block.scalar
            def _(act):
                for s in (ys_high, mkT_ready, h1_ready, h1_high, h2_ready):
                    s.open(act)
                act.wait_ge(s_ffn0, 16)
                nc.scalar.copy(w12[:, 0, :], ffn0_sb[:, 0:2 * E0 * D]).then_inc(w_high, 1)

                def relu1(g, v, e):
                    n = g * E0 + e
                    act.wait_ge(h1_done.sem, h1_done.done(n))
                    act.wait_ge(h1_low.sem, h1_low.done(n - 2))
                    nc.scalar.activation(h1[:, e % 2, :], psH1[e % 3][:, :], ACT.Relu, bias=b12[0][e])\
                        .then_inc(h1_ready.sem, 1)

                def high1(g, v, e):
                    n = g * E0 + e
                    act.wait_ge(h1_ready.sem, h1_ready.done(n))
                    act.wait_ge(h2_done.sem, h2_done.done(n - 3))
                    nc.scalar.copy(h1s[e % 3][0], h1[:, e % 2, :]).then_inc(h1_high.sem, 1)

                def relu2(g, v, e):
                    n = g * E0 + e
                    act.wait_ge(h2_done.sem, h2_done.done(n))
                    act.wait_ge(o_done.sem, o_done.done(n - 2))
                    nc.scalar.activation(h2[:, e % 2, :], psH2[e % 2][:, :], ACT.Relu, bias=b12[1][e])\
                        .then_inc(h2_ready.sem, 1)

                def high_y(g, v):
                    act.wait_ge(h1_done.sem, h1_done.done((g - 2) * E0 + (E0 - 1)))
                    nc.scalar.copy(ys[v][0], Y[:, cols(g)]).then_inc(ys_high.sem, 1)

                def body(t):
                    for e in range(E0):
                        if t.has(0):
                            relu2(*t.group(0), e)
                        if e == 0 and t.has(1):
                            high_y(*t.group(1))
                        d, ee = ahead(e, 3)
                        if t.has(d):
                            relu1(*t.group(d), ee)
                            high1(*t.group(d), ee)
                        if e == 2 and t.has(1):
                            g, v = t.group(1)
                            act.wait_ge(mt_done.sem, mt_done.done(g))
                            act.wait_ge(bias_done.sem, bias_done.done(g - 2))
                            nc.scalar.copy(mkT[0:E0, v, :], psM[0:E0, :]).then_inc(mkT_ready.sem, 1)

                over_groups(act, body, ahead=1, behind=1)

            @block.vector
            def _(dve):
                for s in (ys_low, h1_low, bias_used, o_used):
                    s.open(dve)
                dve.wait_ge(w_high, 1)
                nc.vector.tensor_tensor(w12[:, 1, :], ffn0_sb[:, 0:2 * E0 * D], w12[:, 0, :].bitcast(F32),
                                        ALU.subtract).then_inc(w_low, 1)

                def low1(g, v, e):
                    n = g * E0 + e
                    dve.wait_ge(h1_high.sem, h1_high.done(n))
                    nc.vector.tensor_tensor(h1s[e % 3][1], h1[:, e % 2, :], h1s[e % 3][0].bitcast(F32), ALU.subtract)\
                        .then_inc(h1_low.sem, 1)

                def low_y(g, v):
                    dve.wait_ge(ys_high.sem, ys_high.done(g))
                    nc.vector.tensor_tensor(ys[v][1], Y[:, cols(g)], ys[v][0].bitcast(F32), ALU.subtract)\
                        .then_inc(ys_low.sem, 1)

                def add(g, v, e):
                    n = g * E0 + e
                    dve.wait_ge(o_done.sem, o_done.done(n))
                    if e > 0:
                        dve.wait_ge(o_used.sem, o_used.done(n - 1))
                    else:
                        dve.wait_ge(bias_used.sem, bias_used.done(g))
                    for b in range(NB):
                        xb = X[:, bass.ds(g * W + b * D, D)]
                        ins = nc.vector.scalar_tensor_tensor(xb, psO[e % 2][:, b * D:(b + 1) * D],
                                                             mask0[:, bass.ds(g * NB + b, 1), e], xb,
                                                             ALU.mult, ALU.add)
                    ins.then_inc(o_used.sem, 1)

                def body(t):
                    for e in range(E0):
                        d, ee = ahead(e, 3)
                        if e == 0 and t.has(1):
                            low_y(*t.group(1))
                        if t.has(d):
                            low1(*t.group(d), ee)
                        d, ee = ahead(e, -1)
                        if t.has(d):
                            add(*t.group(d), ee)
                        if e == 1 and t.has(-1):
                            g, v = t.group(-1)
                            dve.wait_ge(o_used.sem, o_used.done(g * E0 + (E0 - 1)))
                            group_stats(g)
                        if e == 4 and t.has(1):
                            g, v = t.group(1)
                            dve.wait_ge(bias_done.sem, bias_done.done(g))
                            nc.vector.tensor_tensor(X[:, cols(g)], X[:, cols(g)], psM[:, :], ALU.add)\
                                .then_inc(bias_used.sem, 1)

                over_groups(dve, body, ahead=1, behind=1)

            @block.gpsimd
            def _(pool):
                mk_ready.open(pool)
                with pool.Fori(0, G // 2) as it:
                    for u in range(2):
                        g = it * 2 + u
                        pool.wait_ge(mt_done.sem, mt_done.done(g - 2))
                        nc.gpsimd.tensor_copy(mk[:, u, :].rearrange("p (a b) -> p a b", b=E0),
                                              mask0[:, bass.ds(g * NB, NB), :]).then_inc(mk_ready.sem, 1)

        free(2)
        finish_rstd("2")
        take = carve()
        lstm_sb = take(LSTM_COLS)
        at = SKIPS * 8 * D
        bih, bhh = lstm_sb[:, at:at + 4 * SKIPS], lstm_sb[:, at + 4 * SKIPS:at + 8 * SKIPS]
        bias_g = take(4 * SKIPS)
        take = carve()
        xn = take(2, W)
        xnT = take(2, W)
        v1 = take(2, W)
        h1T = take(2, W)
        v2 = take(2, W)

        with nc.Block() as block:
            xn_ready = steps("g_xn_ready", 2)
            t_done = steps("g_t_done", 2)
            xnT_ready = steps("g_xnT_ready", 2)
            v1_done = steps("g_v1_done", 2)
            v1_ready = steps("g_v1_ready", 2)
            m1_done = steps("g_m1_done", 2)
            h1_ready = steps("g_h1_ready", 2)
            v2_done = steps("g_v2_done", 2)
            v2_ready = steps("g_v2_ready", 2)
            m2_done = steps("g_m2_done", 2)
            h2_ready = steps("g_h2_ready", 2)
            psT, psV1, psM1, psV2, psM2 = banks[0:2], banks[2], banks[3], banks[4], banks[5]

            @block.sync
            def _(sp):
                sp.dma_start(lstm_sb, lstm).then_inc(s_lstm, 16)

            @block.vector
            def _(dve):
                for s in (xn_ready, v1_ready, v2_ready):
                    s.open(dve)

                def biased(dst, src, row):
                    return nc.vector.tensor_tensor(dst.rearrange("p (a b) -> p a b", b=D),
                                                   src.rearrange("p (a b) -> p a b", b=D),
                                                   row.unsqueeze(1).broadcast_to([P, NB, D]), ALU.add)

                def body(t):
                    if t.has(1):
                        g, v = t.group(1)
                        dve.wait_ge(v2_done.sem, v2_done.done(g))
                        dve.wait_ge(m2_done.sem, m2_done.done(g - 2))
                        biased(v2[:, v, :], psV2[:, :], cst("bg1")).then_inc(v2_ready.sem, 1)
                    if t.has(3):
                        g, v = t.group(3)
                        dve.wait_ge(v1_done.sem, v1_done.done(g))
                        dve.wait_ge(m1_done.sem, m1_done.done(g - 2))
                        biased(v1[:, v, :], psV1[:, :], cst("bg0")).then_inc(v1_ready.sem, 1)
                    if t.has(5):
                        g, v = t.group(5)
                        dve.wait_ge(t_done.sem, t_done.done(g - 2))
                        normalise(xn[:, v, :], g).then_inc(xn_ready.sem, 1)

                over_groups(dve, body, ahead=5)
                dve.wait_ge(s_lstm, 16)
                nc.vector.tensor_tensor(bias_g, bih, bhh, ALU.add)

            @block.scalar
            def _(act):
                for s in (xnT_ready, h1_ready, h2_ready):
                    s.open(act)

                def body(t):
                    if t.has(0):
                        g, v = t.group(0)
                        act.wait_ge(m2_done.sem, m2_done.done(g))
                        nc.scalar.activation(Y[:, cols(g)], psM2[:, :], ACT.Relu).then_inc(h2_ready.sem, 1)
                    if t.has(2):
                        g, v = t.group(2)
                        act.wait_ge(m1_done.sem, m1_done.done(g))
                        act.wait_ge(v2_done.sem, v2_done.done(g - 2))
                        nc.scalar.activation(h1T[:, v, :], psM1[:, :], ACT.Relu).then_inc(h1_ready.sem, 1)
                    if t.has(4):
                        g, v = t.group(4)
                        act.wait_ge(t_done.sem, t_done.done(g))
                        act.wait_ge(v1_done.sem, v1_done.done(g - 2))
                        nc.scalar.copy(xnT[:, v, :], psT[v][:, :]).then_inc(xnT_ready.sem, 1)

                over_groups(act, body, ahead=5)

            @block.tensor
            def _(pe):
                for s in (t_done, v1_done, m1_done, v2_done, m2_done):
                    s.open(pe)

                def four(g, v, dst, src, rhs, src_ready, bank_used, done):
                    pe.wait_ge(src_ready.sem, src_ready.done(g))
                    pe.wait_ge(bank_used.sem, bank_used.done(g - 1))
                    for b in range(NB):
                        last = nc.tensor.matmul(dst[:, b * P:(b + 1) * P], src[:, v, b * P:(b + 1) * P], rhs,
                                                start=True, stop=True)
                    last.then_inc(done.sem, 1)

                def body(t):
                    if t.has(0):
                        four(*t.group(0), psM2, v2, cst("adjT"), v2_ready, h2_ready, m2_done)
                    if t.has(1):
                        four(*t.group(1), psV2, h1T, cst("wg1"), h1_ready, v2_ready, v2_done)
                    if t.has(2):
                        four(*t.group(2), psM1, v1, cst("adjT"), v1_ready, h1_ready, m1_done)
                    if t.has(3):
                        four(*t.group(3), psV1, xnT, cst("wg0"), xnT_ready, v1_ready, v1_done)
                    if t.has(4):
                        turn(pe, *t.group(4), xn, psT, xn_ready, xnT_ready, t_done)

                over_groups(pe, body, ahead=5)

        free()
        take = carve()
        gates = [[take(W) for _ in range(4)] for _ in range(2)]
        unused = take(SKIPS)
        cell = [take(W) for _ in range(2)]
        xs = [[take(W, dt=F32R) for _ in range(2)] for _ in range(2)]
        hs = [[take(W, dt=F32R) for _ in range(2)] for _ in range(2)]
        ws = take(2, 2, 4 * D, dt=F32R)
        i_, f_, g_, o_ = range(4)
        for p in range(1, SKIPS + 1):
            nw = P // p
            nbc = {1: 4, 2: 8, 3: 8, 4: 16}[p]
            n = nbc * nw
            turns = B // nbc // 2

            def active(j):
                return (i_, g_, o_) if j == 0 else (i_, g_, f_, o_)

            renew_semaphores()
            with nc.Block() as block:
                w_high = sem(f"l{p}_w_high")
                w_low = sem(f"l{p}_w_low")
                done = [steps(f"l{p}_done{k}", 2 * p) for k in range(4)]
                ready = [steps(f"l{p}_ready{k}", 2 * p) for k in range(4)]
                xs_high = steps(f"l{p}_xs_high", 2 * p)
                xs_low = steps(f"l{p}_xs_low", 2 * p)
                part_ready = steps(f"l{p}_part_ready", 2 * p)
                cell_ready = steps(f"l{p}_cell_ready", 2 * p)
                tcell_ready = steps(f"l{p}_tcell_ready", 2 * p)
                hid_ready = steps(f"l{p}_hid_ready", 2 * p)
                hs_high = steps(f"l{p}_hs_high", 2 * p)
                hs_low = steps(f"l{p}_hs_low", 2 * p)

                def item(it, j, u):
                    return it * (2 * p) + (2 * j + u)

                def late(it, j, u):
                    return it * (2 * (p - 1)) + (2 * (j - 1) + u)

                def early(it, j, u):
                    return it * (2 * (p - 1)) + (2 * j + u)

                def of_gate(k, it, j, u):
                    return late(it, j, u) if k == f_ else item(it, j, u)

                def at_step(it, j, u):
                    return Y3[:, bass.ds((it * 2 + u) * nbc, nbc), j:j + (nw - 1) * p + 1:p]

                def flat(t):
                    return t[:, 0:n]

                def by_batch(t):
                    return t[:, 0:n].rearrange("p (a b) -> p a b", a=nbc)

                def following(it, j):
                    return (it, j + 1) if j + 1 < p else (it + 1, 0)

                def finished(u):
                    return (u,) if p > 1 else ((), (0, 1))[u]

                def over_items(eng, body):
                    with eng.Fori(0, turns - 1) as it:
                        for j in range(p):
                            for u in range(2):
                                body(it, j, u, True)
                    for j in range(p):
                        for u in range(2):
                            body(turns - 1, j, u, j + 1 < p)

                @block.tensor
                def _(pe):
                    for k in range(4):
                        done[k].open(pe)
                    pe.wait_ge(w_high, 1)
                    pe.wait_ge(w_low, 1)

                    def body(it, j, u, more):
                        m = item(it, j, u)
                        pe.wait_ge(xs_low.sem, xs_low.done(m))
                        for k in active(j):
                            before = of_gate(k, it, j, u) - 2
                            pe.wait_ge(ready[k].sem, ready[k].done(before))
                            w = slice(k * D, (k + 1) * D)
                            last = product(flat(banks[4 * u + k]), ws[:, 0, 0, w], ws[:, 1, 0, w],
                                           flat(xs[u][0]), flat(xs[u][1]), True, j == 0)
                            if j == 0:
                                last.then_inc(done[k].sem, 1)
                        if j > 0:
                            pe.wait_ge(hs_low.sem, hs_low.done(late(it, j, u)))
                            for k in active(j):
                                w = slice(k * D, (k + 1) * D)
                                product(flat(banks[4 * u + k]), ws[:, 0, 1, w], ws[:, 1, 1, w],
                                        flat(hs[u][0]), flat(hs[u][1]), False, True).then_inc(done[k].sem, 1)

                    over_items(pe, body)

                @block.scalar
                def _(act):
                    for s in ready + [tcell_ready]:
                        s.open(act)
                    for t in range(2):
                        at = lstm_sb[:, ((t * SKIPS + p - 1) * 4) * D:((t * SKIPS + p) * 4) * D]
                        last = nc.scalar.copy(ws[:, 0, t, :], at)
                    last.then_inc(w_high, 1)

                    def high(it, j, u):
                        nc.scalar.copy(by_batch(xs[u][0]), at_step(it, j, u)).then_inc(xs_high.sem, 1)

                    def body(it, j, u, more):
                        m = item(it, j, u)
                        act.wait_ge(hid_ready.sem, hid_ready.done(m - 2))
                        for k in active(j):
                            act.wait_ge(done[k].sem, done[k].done(of_gate(k, it, j, u)))
                            nc.scalar.activation(flat(gates[u][k]), flat(banks[4 * u + k]),
                                                 ACT.Tanh if k == g_ else ACT.Sigmoid,
                                                 bias=bias_g[:, (p - 1) * 4 + k:(p - 1) * 4 + k + 1])\
                                .then_inc(ready[k].sem, 1)
                        if more and p > 1:
                            high(*following(it, j), u)
                        for w in finished(u):
                            act.wait_ge(cell_ready.sem, cell_ready.done(item(it, j, w)))
                            nc.scalar.activation(flat(gates[w][g_]), flat(cell[w]), ACT.Tanh)\
                                .then_inc(tcell_ready.sem, 1)

                    nc.scalar.activation(unused[:, p - 1:p], bias_g[:, 0:1], ACT.Sigmoid)
                    if p > 1:
                        for u in range(2):
                            high(0, 0, u)
                    over_items(act, body)

                @block.vector
                def _(dve):
                    for s in (xs_high, xs_low, part_ready, cell_ready, hid_ready, hs_high, hs_low):
                        s.open(dve)
                    dve.wait_ge(w_high, 1)
                    for t in range(2):
                        at = lstm_sb[:, ((t * SKIPS + p - 1) * 4) * D:((t * SKIPS + p) * 4) * D]
                        last = nc.vector.tensor_tensor(ws[:, 1, t, :], at, ws[:, 0, t, :].bitcast(F32), ALU.subtract)
                    last.then_inc(w_low, 1)

                    def low(it, j, u):
                        if p == 1:
                            nc.vector.tensor_copy(by_batch(xs[u][0]), at_step(it, j, u)).then_inc(xs_high.sem, 1)
                        dve.wait_ge(xs_high.sem, xs_high.done(item(it, j, u)))
                        nc.vector.tensor_tensor(by_batch(xs[u][1]), at_step(it, j, u),
                                                by_batch(xs[u][0]).bitcast(F32), ALU.subtract).then_inc(xs_low.sem, 1)

                    def body(it, j, u, more):
                        m = item(it, j, u)
                        i, f, g = (flat(gates[u][k]) for k in range(3))
                        c = flat(cell[u])
                        dve.wait_ge(ready[i_].sem, ready[i_].done(m))
                        dve.wait_ge(ready[g_].sem, ready[g_].done(m))
                        if j == 0:
                            dve.wait_ge(tcell_ready.sem, tcell_ready.done(m - 2))
                            nc.vector.tensor_tensor(c, i, g, ALU.mult).then_inc(cell_ready.sem, 1)
                        else:
                            nc.vector.tensor_tensor(i, i, g, ALU.mult)
                            dve.wait_ge(ready[f_].sem, ready[f_].done(late(it, j, u)))
                            nc.vector.tensor_tensor(c, f, c, ALU.mult).then_inc(part_ready.sem, 1)
                            dve.wait_ge(part_ready.sem, part_ready.done(late(it, j, u)))
                            nc.vector.tensor_tensor(c, c, i, ALU.add).then_inc(cell_ready.sem, 1)
                        if more:
                            if p == 1:
                                dve.wait_ge(done[o_].sem, done[o_].done(m))
                            low(*following(it, j), u)
                        for w in finished(u):
                            output(it, j, w)

                    def output(it, j, u):
                        m = item(it, j, u)
                        o, g = flat(gates[u][o_]), flat(gates[u][g_])
                        dve.wait_ge(ready[o_].sem, ready[o_].done(m))
                        dve.wait_ge(tcell_ready.sem, tcell_ready.done(m))
                        if j < p - 1:
                            e = early(it, j, u)
                            nc.vector.tensor_tensor(o, o, g, ALU.mult).then_inc(hid_ready.sem, 1)
                            dve.wait_ge(hid_ready.sem, hid_ready.done(m))
                            nc.vector.tensor_copy(flat(hs[u][0]), o).then_inc(hs_high.sem, 1)
                            dve.wait_ge(hs_high.sem, hs_high.done(e))
                            nc.vector.tensor_tensor(flat(hs[u][1]), o, flat(hs[u][0]).bitcast(F32), ALU.subtract)\
                                .then_inc(hs_low.sem, 1)
                        else:
                            nc.vector.tensor_tensor(at_step(it, j, u), by_batch(gates[u][o_]), by_batch(gates[u][g_]),
                                                    ALU.mult).then_inc(hid_ready.sem, 1)

                    for u in range(2):
                        low(0, 0, u)
                    over_items(dve, body)

        free()
        take = carve()
        hT = take(2, W)
        with nc.Block() as block:
            h_ready = steps("h_h_ready", 2)
            t_done = steps("h_t_done", 2)
            x_ready = steps("h_x_ready", 2)
            psT = banks[0:2]

            @block.scalar
            def _(act):
                h_ready.open(act)
                with act.Fori(0, G // 2) as it:
                    for u in range(2):
                        g = it * 2 + u
                        act.wait_ge(t_done.sem, t_done.done(g - 2))
                        nc.scalar.copy(hT[:, u, :], Y[:, cols(g)]).then_inc(h_ready.sem, 1)

            @block.tensor
            def _(pe):
                t_done.open(pe)
                with pe.Fori(0, G // 2) as it:
                    for u in range(2):
                        turn(pe, it * 2 + u, u, hT, psT, h_ready, x_ready, t_done)

            @block.vector
            def _(dve):
                x_ready.open(dve)

                def body(t):
                    if t.has(0):
                        g, v = t.group(0)
                        dve.wait_ge(t_done.sem, t_done.done(g))
                        nc.vector.tensor_tensor(X[:, cols(g)], X[:, cols(g)], psT[v][:, :], ALU.add)\
                            .then_inc(x_ready.sem, 1)
                    if t.has(-1):
                        g, v = t.group(-1)
                        dve.wait_ge(x_ready.sem, x_ready.done(g))
                        group_stats(g)

                over_groups(dve, body, ahead=0, behind=1)

        renew_semaphores()
        finish_rstd("3")
        free(3)
        take = carve()
        WB = take(E1, 4, FK * D, dt=F32R)
        biases = take(E1 + 1, FK + 1)
        slot = take(B, 3, dt=I32)
        pairw = take(2, B)
        owner = take(BLOCKS, dt=I32)
        take = carve()
        WS = take(4, FK * D, dt=F32R)
        take = carve()
        raw = take(2, EW)
        logits1 = take(B, E1)
        prob1 = take(B, E1)
        tq1 = take(B, E1)
        tw1 = take(B, E1)
        sel1 = take(B, E1)
        small_t = take(4, B)
        xn = take(2, W)
        xnT = take(2, W)
        lT = take(2, W)

        with nc.Block() as block:
            xn_ready = steps("r_xn_ready", 2)
            t_done = steps("r_t_done", 2)
            xnT_ready = steps("r_xnT_ready", 2)
            r_done = steps("r_r_done", 2)
            lT_ready = steps("r_lT_ready", 2)
            l_done = steps("r_l_done", 2)
            l_used = steps("r_l_used", 2)
            s_raw = [sem(f"s_raw{i}") for i in range(2)]
            s_bias = sem("s_bias")
            high_ready = sem("r_high_ready")
            low_ready = sem("r_low_ready")
            psT, psR, psL = banks[0:2], banks[2:4], banks[4:6]

            def parts(e):
                w = WB[:, e] if e < E1 else WS
                return w.rearrange("p (l h) c -> p l h c", h=2)

            @block.sync
            def _(sp):
                sp.dma_start(biases.rearrange("p a b -> p (a b)"), ffn1[:, (E1 + 1) * EW:FFN1_COLS]).then_inc(s_bias, 16)
                for e in range(E1 + 1):
                    if e >= 2:
                        sp.wait_ge(low_ready, e - 1)
                    sp.dma_start(raw[:, e % 2, :], ffn1[:, e * EW:(e + 1) * EW]).then_inc(s_raw[e % 2], 16)
                sp.wait_ge(s_bias, 16)

            @block.vector
            def _(dve):
                for s in (xn_ready, l_used):
                    s.open(dve)

                def body(t):
                    if t.has(4):
                        g, v = t.group(4)
                        dve.wait_ge(t_done.sem, t_done.done(g - 2))
                        normalise(xn[:, v, :], g).then_inc(xn_ready.sem, 1)
                    if t.has(0):
                        g, v = t.group(0)
                        dve.wait_ge(l_done.sem, l_done.done(g))
                        nc.vector.tensor_copy(logits1[:, bass.ds(g * NB, NB), :],
                                              psL[v][:, 0:NB * E1].rearrange("p (a b) -> p a b", b=E1))\
                            .then_inc(l_used.sem, 1)

                over_groups(dve, body, ahead=4)

            @block.gpsimd
            def _(pool):
                for e in range(E1 + 1):
                    part = parts(e)
                    full = raw[:, e % 2, :].rearrange("p (l c) -> p l c", l=2)
                    pool.wait_ge(s_raw[e % 2], 16 * (e // 2 + 1))
                    nc.gpsimd.tensor_copy(part[:, :, 0, :], full).then_inc(high_ready, 1)
                    pool.wait_ge(high_ready, e + 1)
                    nc.gpsimd.tensor_tensor(part[:, :, 1, :], full, part[:, :, 0, :].bitcast(F32), ALU.subtract)\
                        .then_inc(low_ready, 1)

            @block.scalar
            def _(act):
                xnT_ready.open(act)
                lT_ready.open(act)

                def body(t):
                    if t.has(3):
                        g, v = t.group(3)
                        act.wait_ge(t_done.sem, t_done.done(g))
                        act.wait_ge(r_done.sem, r_done.done(g - 2))
                        nc.scalar.copy(xnT[:, v, :], psT[v][:, :]).then_inc(xnT_ready.sem, 1)
                    if t.has(2):
                        g, v = t.group(2)
                        act.wait_ge(r_done.sem, r_done.done(g))
                        act.wait_ge(l_done.sem, l_done.done(g - 2))
                        nc.scalar.copy(lT[0:E1, v, :], psR[v][0:E1, :]).then_inc(lT_ready.sem, 1)

                over_groups(act, body, ahead=4)

            @block.tensor
            def _(pe):
                for s in (t_done, r_done, l_done):
                    s.open(pe)

                def body(t):
                    if t.has(3):
                        turn(pe, *t.group(3), xn, psT, xn_ready, xnT_ready, t_done)
                    if t.has(0):
                        g, v = t.group(0)
                        pe.wait_ge(lT_ready.sem, lT_ready.done(g))
                        pe.wait_ge(l_used.sem, l_used.done(g - 2))
                    if t.has(2):
                        g, v = t.group(2)
                        pe.wait_ge(xnT_ready.sem, xnT_ready.done(g))
                        pe.wait_ge(lT_ready.sem, lT_ready.done(g - 2))
                        nc.tensor.matmul(psR[v][0:E1, :], cst("wr"), xnT[:, v, :], start=True, stop=True)\
                            .then_inc(r_done.sem, 1)
                    if t.has(0):
                        g, v = t.group(0)
                        for b in range(NB):
                            last = nc.tensor.transpose(psL[v][:, b * E1:(b + 1) * E1], lT[0:E1, v, b * P:(b + 1) * P],
                                                       ident[0:E1, 0:E1])
                        last.then_inc(l_done.sem, 1)

                over_groups(pe, body, ahead=4)

        route("1", logits1, prob1, tq1, tw1, sel1, small_t, cst("rank1"), E1, False)

        chosen, place, total = logits1, prob1, tw1
        upto_b = xn.rearrange("p a b -> p (a b)")[:, 0:B * E1].rearrange("p (a b) -> p a b", b=E1)
        ended = xnT.rearrange("p a b -> p (a b)")[:, 0:BLOCKS * E1].rearrange("p (a b) -> p a b", b=E1)
        counts = small_t[:, 0, 0:4 * E1].rearrange("p (a b) -> p a b", b=E1)
        counts_i = small_t[:, 0, 4 * E1:6 * E1].bitcast(I32).rearrange("p (a b) -> p a b", b=E1)
        slot_f = small_t[:, 1, :]
        own_f = raw[:, 0, 0:BLOCKS]
        with nc.Block() as block:
            chosen_ready, ranked = sem("chosen_ready"), sem("ranked")

            @block.tensor
            def _(pe):
                pe.wait_ge(chosen_ready, 1)
                for h in range(2):
                    rhs = chosen.rearrange("p a b -> p (a b)")[:, h * 512:(h + 1) * 512]
                    nc.tensor.matmul(banks[h][:, :], cst("below"), rhs, start=True, stop=True)
                    last = nc.tensor.matmul(banks[2 + h][:, :], cst("ones"), rhs, start=True, stop=True)
                last.then_inc(ranked, 1)

            @block.vector
            def _(dve):
                tt = nc.vector.tensor_tensor
                link(nc.vector.tensor_copy(pairw[:, 0, :], small_t[:, 3, :]))
                link(nc.vector.tensor_copy(pairw[:, 1, :], small_t[:, 2, :]))
                tt(chosen, sel1, tq1, ALU.add).then_inc(chosen_ready, 1)
                dve.wait_ge(ranked, 1)
                for h in range(2):
                    link(nc.vector.tensor_copy(place.rearrange("p a b -> p (a b)")[:, h * 512:(h + 1) * 512],
                                               banks[h][:, :]))
                    link(nc.vector.tensor_copy(total.rearrange("p a b -> p (a b)")[:, h * 512:(h + 1) * 512],
                                               banks[2 + h][:, :]))
                for e in range(E1):
                    link(nc.vector.tensor_tensor_scan(upto_b[:, :, e], cst("ones")[:, 0:B], total[:, :, e], 0.0,
                                                      ALU.mult, ALU.add))
                link(nc.vector.tensor_scalar(counts_i[:, 0, :], upto_b[:, B - 1, :], float(BLOCK - 1), None, ALU.add))
                link(nc.vector.tensor_scalar(counts_i[:, 1, :], counts_i[:, 0, :], BLOCK.bit_length() - 1, None,
                                             ALU.arith_shift_right))
                link(nc.vector.tensor_copy(counts[:, 1, :], counts_i[:, 1, :]))
                link(nc.vector.tensor_tensor_scan(counts[:, 2, :], cst("ones")[:, 0:E1], counts[:, 1, :], 0.0,
                                                  ALU.mult, ALU.add))
                link(tt(counts[:, 3, :], counts[:, 2, :], counts[:, 1, :], ALU.subtract))
                link(nc.vector.tensor_scalar(counts[:, 3, :], counts[:, 3, :], float(BLOCK), None, ALU.mult))
                link(tt(place, place, upto_b, ALU.add))
                link(tt(place, place, total, ALU.subtract))
                link(tt(place, place, counts[:, 3, :].unsqueeze(1).broadcast_to([P, B, E1]), ALU.add))
                for k, sel in ((0, sel1), (1, tq1)):
                    link(tt(sel, sel, place, ALU.mult))
                    link(nc.vector.tensor_reduce(slot_f, sel, AXX, ALU.add))
                    link(nc.vector.tensor_copy(slot[:, :, k], slot_f))
                link(nc.vector.tensor_copy(slot[:, :, 2], ids_sb[:, 0:B]))
                link(tt(ended, cst("blk").unsqueeze(2).broadcast_to([P, BLOCKS, E1]),
                        counts[:, 2, :].unsqueeze(1).broadcast_to([P, BLOCKS, E1]), ALU.is_ge))
                link(nc.vector.tensor_reduce(own_f, ended, AXX, ALU.add))
                link(nc.vector.tensor_scalar(own_f, own_f, float(E1 - 1), None, ALU.min))
                link(nc.vector.tensor_copy(owner, own_f))

        free()
        take = carve()
        xa = [take(NB, ROW) for _ in range(2)]
        idx = [take(2, NB, dt=I32) for _ in range(2)]
        xT = [[take(W, dt=F32R) for _ in range(2)] for _ in range(2)]
        gf = [take(W) for _ in range(2)]
        gs = [[take(W, dt=F32R) for _ in range(2)] for _ in range(FK)]
        yT = [take(W) for _ in range(2)]

        def unit(k):
            return (k + 3) // FK, (k + 3) % FK

        def chunk(k):
            return slice(k * D, (k + 1) * D)

        with nc.Block() as block:
            pads_ready = sem("s_pads_ready")
            groups_taken = sem("s_groups_taken")
            xa_ready = steps("s_xa_ready", 2)
            rows_sent = steps("s_rows_sent", 2)
            scattered = [sem(f"s_scattered{u}") for u in range(2)]
            PER = 16 * 2 * NB
            t_done = steps("s_t_done", 2)
            high_ready = steps("s_high_ready", 2)
            low_ready = steps("s_low_ready", 2)
            up_done = steps("s_up_done", 2 * FK)
            gelu_ready = steps("s_gelu_ready", 2 * FK)
            ghigh_ready = steps("s_ghigh_ready", 2 * FK)
            split_ready = steps("s_split_ready", 2 * FK)
            down_done = steps("s_down_done", 2 * FK)
            y_ready = steps("s_y_ready", 2)
            yt_done = steps("s_yt_done", 2)
            x_ready = steps("s_x_ready", 2)
            psU, psO, psT, psY = banks[0:4], banks[4:6], banks[6], banks[7]

            @block.gpsimd
            def _(pool):
                rows_sent.open(pool)
                pool.wait_ge(s_fill, 16 * BLOCKS)

                def send(v, b):
                    for k in range(2):
                        at = idx[v][:, k, b:b + 1].bitcast(U32)
                        nc.gpsimd.indirect_dma_start(rows_dram, bass.IndirectOffsetOnAxis(ap=at, axis=0),
                                                     xa[v][:, b, :], None).then_inc(scattered[v], 16)

                def body(t):
                    if t.has(0):
                        g, v = t.group(0)
                        pool.wait_ge(xa_ready.sem, xa_ready.done(g))
                        pool.sem_inc(groups_taken, 1)
                        send(v, 0)
                    if t.has(-1):
                        pool.wait_ge(scattered[(t.u - 1) % 2], PER * (t.it + (1 if t.u else 0)))
                        pool.sem_inc(rows_sent.sem, 1)
                    if t.has(0):
                        for b in range(1, NB):
                            send(v, b)

                over_groups(pool, body, ahead=0, behind=1)

            @block.vector
            def _(dve):
                for s in (xa_ready, low_ready, ghigh_ready, split_ready, x_ready):
                    s.open(dve)
                for u in range(2):
                    ins = nc.vector.memset(xa[u], 0.0)
                ins.then_inc(pads_ready, 1)
                dve.wait_ge(pads_ready, 1)

                def norm(g, v):
                    dve.wait_ge(t_done.sem, t_done.done(g - 2))
                    dve.wait_ge(rows_sent.sem, rows_sent.done(g - 2))
                    for b in range(NB):
                        nc.vector.tensor_scalar(xa[v][:, b, 0:D], X3[:, bass.ds(g * NB + b, 1), :],
                                                MEAN[:, bass.ds(g * NB + b, 1)], RSTD[:, bass.ds(g * NB + b, 1)],
                                                ALU.subtract, ALU.mult)
                    nc.vector.tensor_copy(idx[v], slot[:, bass.ds(g * NB, NB), 0:2].rearrange("p b k -> p k b"))
                    nc.vector.tensor_copy(xa[v][:, :, D:D + 2].bitcast(I32), slot[:, bass.ds(g * NB, NB), 1:3])\
                        .then_inc(xa_ready.sem, 1)

                def low(g, v):
                    dve.wait_ge(high_ready.sem, high_ready.done(g))
                    nc.vector.tensor_tensor(xT[v][1], psT[:, :], xT[v][0].bitcast(F32), ALU.subtract)\
                        .then_inc(low_ready.sem, 1)

                def split(g, v, k):
                    m = g * FK + k
                    dve.wait_ge(gelu_ready.sem, gelu_ready.done(m))
                    dve.wait_ge(down_done.sem, down_done.done(m - FK))
                    nc.vector.tensor_copy(gs[k][0], gf[k % 2]).then_inc(ghigh_ready.sem, 1)
                    dve.wait_ge(ghigh_ready.sem, ghigh_ready.done(m))
                    nc.vector.tensor_tensor(gs[k][1], gf[k % 2], gs[k][0].bitcast(F32), ALU.subtract)\
                        .then_inc(split_ready.sem, 1)

                def add(g, v):
                    dve.wait_ge(yt_done.sem, yt_done.done(g))
                    nc.vector.tensor_tensor(X[:, cols(g)], X[:, cols(g)], psY[:, :], ALU.add).then_inc(x_ready.sem, 1)

                def body(t):
                    for k in range(FK):
                        d, kk = unit(k)
                        if t.has(d):
                            split(*t.group(d), kk)
                        if k == 1 and t.has(3):
                            norm(*t.group(3))
                        if k == 2 and t.has(2):
                            low(*t.group(2))
                        if k == 3 and t.has(-1):
                            add(*t.group(-1))

                over_groups(dve, body, ahead=3, behind=1)

            @block.scalar
            def _(act):
                for s in (high_ready, gelu_ready, y_ready):
                    s.open(act)

                def high(g, v):
                    act.wait_ge(t_done.sem, t_done.done(g))
                    act.wait_ge(up_done.sem, up_done.done((g - 2) * FK + (FK - 1)))
                    nc.scalar.copy(xT[v][0], psT[:, :]).then_inc(high_ready.sem, 1)

                def gelu(g, v, k):
                    m = g * FK + k
                    act.wait_ge(up_done.sem, up_done.done(m))
                    act.wait_ge(split_ready.sem, split_ready.done(m - 2))
                    nc.scalar.activation(gf[k % 2], psU[k][:, :], ACT.Gelu, bias=biases[:, E1, k:k + 1])\
                        .then_inc(gelu_ready.sem, 1)

                def output(g, v):
                    act.wait_ge(down_done.sem, down_done.done(g * FK + (FK - 1)))
                    act.wait_ge(yt_done.sem, yt_done.done(g - 2))
                    nc.scalar.activation(yT[v], psO[v][:, :], ACT.Identity, bias=biases[:, E1, FK:FK + 1])\
                        .then_inc(y_ready.sem, 1)

                def body(t):
                    for k in range(FK):
                        d, kk = unit(k)
                        if k == 0 and t.has(-1):
                            output(*t.group(-1))
                        if t.has(d):
                            gelu(*t.group(d), kk)
                        if k == 2 and t.has(2):
                            high(*t.group(2))

                over_groups(act, body, ahead=3, behind=1)

            @block.tensor
            def _(pe):
                for s in (t_done, up_done, down_done, yt_done):
                    s.open(pe)

                def turn_rows(g, v):
                    pe.wait_ge(xa_ready.sem, xa_ready.done(g))
                    pe.wait_ge(low_ready.sem, low_ready.done(g - 1))
                    for b in range(NB):
                        last = nc.tensor.transpose(psT[:, b * P:(b + 1) * P], xa[v][:, b, 0:D], ident)
                    last.then_inc(t_done.sem, 1)

                def up(g, v, k):
                    m = g * FK + k
                    if k == 0:
                        pe.wait_ge(low_ready.sem, low_ready.done(g))
                    pe.wait_ge(gelu_ready.sem, gelu_ready.done(m - FK))
                    product(psU[k][:, :], WS[:, 0, chunk(k)], WS[:, 1, chunk(k)], xT[v][0], xT[v][1], True, True)\
                        .then_inc(up_done.sem, 1)

                def down(g, v, k):
                    m = g * FK + k
                    if k == 0:
                        pe.wait_ge(y_ready.sem, y_ready.done(g - 2))
                    pe.wait_ge(split_ready.sem, split_ready.done(m))
                    product(psO[v][:, :], WS[:, 2, chunk(k)], WS[:, 3, chunk(k)], gs[k][0], gs[k][1],
                            k == 0, k == FK - 1).then_inc(down_done.sem, 1)

                def turn_back(g, v):
                    pe.wait_ge(y_ready.sem, y_ready.done(g))
                    pe.wait_ge(x_ready.sem, x_ready.done(g - 1))
                    for b in range(NB):
                        last = nc.tensor.transpose(psY[:, b * D:(b + 1) * D], yT[v][:, b * P:(b + 1) * P], ident)
                    last.then_inc(yt_done.sem, 1)

                def body(t):
                    for k in range(FK):
                        d, kk = unit(k)
                        if t.has(d):
                            up(*t.group(d), kk)
                        if t.has(0):
                            down(*t.group(0), k)
                        if k == 0 and t.has(-1):
                            turn_back(*t.group(-1))
                        if k == 2 and t.has(2):
                            turn_rows(*t.group(2))

                over_groups(pe, body, ahead=3, behind=1)

        free(2)
        take = carve()
        w1s = [take(2, FK * D, dt=F32R) for _ in range(2)]
        w2s = [take(2, FK * D, dt=F32R) for _ in range(2)]
        b1s = [take(FK) for _ in range(2)]
        b2s = [take(1) for _ in range(2)]
        xrow = [take(NQ, ROW) for _ in range(2)]
        xT = [[take(W, dt=F32R) for _ in range(2)] for _ in range(2)]
        gf = [take(W) for _ in range(2)]
        gs = [[take(W, dt=F32R) for _ in range(2)] for _ in range(FK)]
        yT = [take(W) for _ in range(2)]
        yrow = [take(NQ, D) for _ in range(2)]
        id_in = [take(NQ, dt=I32) for _ in range(2)]
        spare_by = [take(NQ) for _ in range(2)]
        second = [take(NQ) for _ in range(2)]
        id_out = [take(NQ, dt=I32) for _ in range(2)]
        LAST = BLOCKS - 1

        def over_blocks(eng, body):
            body(0, 0, at=0)
            with eng.Fori(0, (BLOCKS - 4) // 2) as it:
                body(it, 1)
                body(it + 1, 0)
            for n in range(BLOCKS - 3, BLOCKS):
                body(n // 2, n % 2, at=n)

        with nc.Block() as block:
            loaded = [sem(f"b_loaded{u}") for u in range(2)]
            sent = [sem(f"b_sent{u}") for u in range(2)]
            PER = 16 * NQ
            blocks_taken = sem("b_blocks_taken")
            t_done = steps("b_t_done", 2)
            ids_kept = steps("b_ids_kept", 2)
            shifted = steps("b_shifted", 2)
            ids_out = steps("b_ids_out", 2)
            outs_sent = steps("b_outs_sent", 2)
            high_ready = steps("b_high_ready", 2)
            low_ready = steps("b_low_ready", 2)
            w1_ready = steps("b_w1_ready", 2)
            w2_ready = steps("b_w2_ready", 2)
            up_done = steps("b_up_done", 2 * FK)
            gelu_ready = steps("b_gelu_ready", 2 * FK)
            ghigh_ready = steps("b_ghigh_ready", 2 * FK)
            split_ready = steps("b_split_ready", 2 * FK)
            down_done = steps("b_down_done", 2 * FK)
            y_ready = steps("b_y_ready", 2)
            yt_done = steps("b_yt_done", 2)
            row_ready = steps("b_row_ready", 2)
            psU, psO, psT, psY = banks[0:4], banks[4:6], banks[6], banks[7]

            def next_unit(q, u, k):
                k += 3
                return q, u + k // FK, k % FK

            @block.sync
            def _(sp):
                def load(q, u, d=0):
                    n = q * 2 + u + d
                    sp.wait_ge(t_done.sem, t_done.done(n - 2))
                    sp.wait_ge(ids_kept.sem, ids_kept.done(n - 2))
                    sp.dma_start(xrow[u], rows_dram.rearrange("(n q p) c -> p n q c", p=P, q=NQ)[:, bass.ds(n, 1)])\
                        .then_inc(loaded[u], 16)

                with sp.Fori(0, BLOCKS // 2) as q:
                    load(q, 0)
                    load(q, 1)

            @block.gpsimd
            def _(pool):
                outs_sent.open(pool)

                def send(u, j):
                    at = id_out[u][:, j:j + 1].bitcast(U32)
                    nc.gpsimd.indirect_dma_start(outs_dram, bass.IndirectOffsetOnAxis(ap=at, axis=0),
                                                 yrow[u][:, j, :], None).then_inc(sent[u], 16)

                def arrived(q, u):
                    pool.wait_ge(sent[u], PER * (q + 1))
                    pool.sem_inc(outs_sent.sem, 1)

                def body(q, u, at=None):
                    n = q * 2 + u
                    pool.wait_ge(row_ready.sem, row_ready.done(n))
                    pool.wait_ge(ids_out.sem, ids_out.done(n))
                    pool.sem_inc(blocks_taken, 1)
                    send(u, 0)
                    if at != 0:
                        arrived(q if u else q - 1, 1 - u)
                    for j in range(1, NQ):
                        send(u, j)

                over_blocks(pool, body)
                arrived(LAST // 2, LAST % 2)

            @block.tensor
            def _(pe):
                for s in (t_done, up_done, down_done, yt_done):
                    s.open(pe)

                def turn(q, u):
                    pe.wait_ge(loaded[u], q * 16 + 16)
                    pe.wait_ge(low_ready.sem, low_ready.done(q * 2 + (u - 1)))
                    for j in range(NQ):
                        last = nc.tensor.transpose(psT[:, j * P:(j + 1) * P], xrow[u][:, j, 0:D], ident)
                    last.then_inc(t_done.sem, 1)

                def up(q, v, k):
                    u = v % 2
                    m = q * (2 * FK) + (v * FK + k)
                    if k == 0:
                        pe.wait_ge(low_ready.sem, low_ready.done(q * 2 + v))
                        pe.wait_ge(w1_ready.sem, w1_ready.done(q * 2 + v))
                    pe.wait_ge(gelu_ready.sem, gelu_ready.done(m - FK))
                    product(psU[k][:, :], w1s[u][:, 0, chunk(k)], w1s[u][:, 1, chunk(k)], xT[u][0], xT[u][1], True, True)\
                        .then_inc(up_done.sem, 1)

                def down(q, u, k):
                    n = q * 2 + u
                    m = q * (2 * FK) + (u * FK + k)
                    if k == 0:
                        pe.wait_ge(w2_ready.sem, w2_ready.done(n))
                        pe.wait_ge(y_ready.sem, y_ready.done(n - 2))
                    pe.wait_ge(split_ready.sem, split_ready.done(m))
                    product(psO[u][:, :], w2s[u][:, 0, chunk(k)], w2s[u][:, 1, chunk(k)], gs[k][0], gs[k][1],
                            k == 0, k == FK - 1).then_inc(down_done.sem, 1)

                def turn_back(q, v):
                    u = v % 2
                    n = q * 2 + v
                    pe.wait_ge(y_ready.sem, y_ready.done(n))
                    pe.wait_ge(row_ready.sem, row_ready.done(n - 1))
                    for j in range(NQ):
                        last = nc.tensor.transpose(psY[:, j * D:(j + 1) * D], yT[u][:, j * P:(j + 1) * P], ident)
                    last.then_inc(yt_done.sem, 1)

                def body(q, u, at=None):
                    for k in range(FK):
                        if at != LAST or k == 0:
                            up(*next_unit(q, u, k))
                        down(q, u, k)
                        if k == 2 and at != 0:
                            turn_back(q, u - 1)
                        if k == 1 and (at is None or at + 2 <= LAST):
                            turn(q + 1, u)

                turn(0, 0)
                turn(0, 1)
                for k in range(3):
                    up(0, 0, k)
                over_blocks(pe, body)
                turn_back(LAST // 2, LAST % 2)

            @block.scalar
            def _(act):
                for s in (high_ready, w1_ready, w2_ready, gelu_ready, y_ready):
                    s.open(act)

                def expert_of(n):
                    return nc.scalar.value_load(owner[0:1, bass.ds(n, 1)], min_val=0, max_val=E1 - 1)

                def take_w1(q, u):
                    n = q * 2 + u
                    e = expert_of(n)
                    act.wait_ge(up_done.sem, up_done.done(q * (2 * FK) + ((u - 2) * FK + FK - 1)))
                    act.wait_ge(gelu_ready.sem, gelu_ready.done(q * (2 * FK) + ((u - 2) * FK + FK - 1)))
                    nc.scalar.copy(b1s[u], biases[:, bass.ds(e, 1), 0:FK])
                    nc.scalar.copy(w1s[u], WB[:, bass.ds(e, 1), 0:2, :].bitcast(F32)).then_inc(w1_ready.sem, 1)

                def take_w2(q, v):
                    u = v % 2
                    n = q * 2 + v
                    e = expert_of(n)
                    act.wait_ge(down_done.sem, down_done.done(q * (2 * FK) + ((v - 2) * FK + FK - 1)))
                    act.wait_ge(y_ready.sem, y_ready.done(q * 2 + (v - 2)))
                    nc.scalar.copy(b2s[u], biases[:, bass.ds(e, 1), FK:FK + 1])
                    nc.scalar.copy(w2s[u], WB[:, bass.ds(e, 1), 2:4, :].bitcast(F32)).then_inc(w2_ready.sem, 1)

                def high(q, u):
                    act.wait_ge(t_done.sem, t_done.done(q * 2 + u))
                    act.wait_ge(up_done.sem, up_done.done(q * (2 * FK) + ((u - 2) * FK + FK - 1)))
                    nc.scalar.copy(xT[u][0], psT[:, :]).then_inc(high_ready.sem, 1)

                def gelu(q, v, k):
                    u = v % 2
                    m = q * (2 * FK) + (v * FK + k)
                    if k == 0:
                        act.wait_ge(w1_ready.sem, w1_ready.done(q * 2 + v))
                    act.wait_ge(up_done.sem, up_done.done(m))
                    act.wait_ge(split_ready.sem, split_ready.done(m - 2))
                    nc.scalar.activation(gf[k % 2], psU[k][:, :], ACT.Gelu, bias=b1s[u][:, k:k + 1])\
                        .then_inc(gelu_ready.sem, 1)

                def output(q, v):
                    u = v % 2
                    n = q * 2 + v
                    act.wait_ge(w2_ready.sem, w2_ready.done(n))
                    act.wait_ge(down_done.sem, down_done.done(q * (2 * FK) + (v * FK + FK - 1)))
                    act.wait_ge(yt_done.sem, yt_done.done(n - 2))
                    nc.scalar.activation(yT[u], psO[u][:, :], ACT.Identity, bias=b2s[u]).then_inc(y_ready.sem, 1)

                def body(q, u, at=None):
                    for k in range(FK):
                        if at != LAST or k == 0:
                            gelu(*next_unit(q, u, k))
                        if k == 0 and at != 0:
                            output(q, u - 1)
                        if k == 1 and at != LAST:
                            take_w2(q, u + 1)
                        if k == 2 and (at is None or at + 2 <= LAST):
                            high(q + 1, u)
                        if k == 3 and (at is None or at + 2 <= LAST):
                            take_w1(q + 1, u)

                take_w1(0, 0)
                high(0, 0)
                take_w2(0, 0)
                take_w1(0, 1)
                high(0, 1)
                for k in range(3):
                    gelu(0, 0, k)
                over_blocks(act, body)
                output(LAST // 2, LAST % 2)

            @block.vector
            def _(dve):
                for s in (ids_kept, shifted, ids_out, low_ready, ghigh_ready, split_ready, row_ready):
                    s.open(dve)

                def low(q, u):
                    dve.wait_ge(high_ready.sem, high_ready.done(q * 2 + u))
                    nc.vector.tensor_tensor(xT[u][1], psT[:, :], xT[u][0].bitcast(F32), ALU.subtract)\
                        .then_inc(low_ready.sem, 1)

                def keep_ids(q, u):
                    dve.wait_ge(loaded[u], q * 16 + 16)
                    dve.wait_ge(ids_out.sem, ids_out.done(q * 2 + (u - 2)))
                    nc.vector.tensor_scalar(spare_by[u], xrow[u][:, :, D + 1].bitcast(I32), float(2 * TOKENS),
                                            cst("blkrow")[:, bass.ds(q * 2 + u, 1)], ALU.is_ge, ALU.mult)
                    nc.vector.scalar_tensor_tensor(second[u], xrow[u][:, :, D].bitcast(I32),
                                                   cst("blkrow")[:, bass.ds(q * 2 + u, 1)], cst("pos"),
                                                   ALU.subtract, ALU.is_equal)
                    nc.vector.tensor_copy(id_in[u], xrow[u][:, :, D + 1].bitcast(I32)).then_inc(ids_kept.sem, 1)

                def shift_ids(q, u):
                    dve.wait_ge(ids_kept.sem, ids_kept.done(q * 2 + u))
                    nc.vector.scalar_tensor_tensor(second[u], second[u], float(TOKENS), spare_by[u],
                                                   ALU.mult, ALU.add).then_inc(shifted.sem, 1)

                def pass_ids(q, u):
                    dve.wait_ge(shifted.sem, shifted.done(q * 2 + u))
                    dve.wait_ge(outs_sent.sem, outs_sent.done(q * 2 + (u - 2)))
                    nc.vector.tensor_tensor(id_out[u], id_in[u], second[u], ALU.add).then_inc(ids_out.sem, 1)

                def split(q, v, k):
                    m = q * (2 * FK) + (v * FK + k)
                    dve.wait_ge(gelu_ready.sem, gelu_ready.done(m))
                    dve.wait_ge(down_done.sem, down_done.done(m - FK))
                    nc.vector.tensor_copy(gs[k][0], gf[k % 2]).then_inc(ghigh_ready.sem, 1)
                    dve.wait_ge(ghigh_ready.sem, ghigh_ready.done(m))
                    nc.vector.tensor_tensor(gs[k][1], gf[k % 2], gs[k][0].bitcast(F32), ALU.subtract)\
                        .then_inc(split_ready.sem, 1)

                def rows(q, v):
                    u = v % 2
                    dve.wait_ge(yt_done.sem, yt_done.done(q * 2 + v))
                    dve.wait_ge(outs_sent.sem, outs_sent.done(q * 2 + (v - 2)))
                    nc.vector.tensor_copy(yrow[u].rearrange("p a b -> p (a b)"), psY[:, :]).then_inc(row_ready.sem, 1)

                def body(q, u, at=None):
                    for k in range(FK):
                        if at != LAST or k == 0:
                            split(*next_unit(q, u, k))
                        before = (q, 0) if u else (q - 1, 1)
                        if k == 0 and at != 0:
                            shift_ids(*before)
                        if k == 1 and at != 0:
                            pass_ids(*before)
                            if at is None or at + 1 <= LAST:
                                keep_ids(before[0] + 1, before[1])
                        if k == 2 and (at is None or at + 2 <= LAST):
                            low(q + 1, u)
                        if k == 3 and at != 0:
                            rows(q, u - 1)

                for u in range(2):
                    keep_ids(0, u)
                    low(0, u)
                for k in range(3):
                    split(0, 0, k)
                over_blocks(dve, body)
                shift_ids(LAST // 2, LAST % 2)
                pass_ids(LAST // 2, LAST % 2)
                rows(LAST // 2, LAST % 2)

        free()
        take = carve()
        RING = 4
        ys = [take(2, NB, D) for _ in range(RING)]
        with nc.Block() as block:
            loaded = [sem(f"z_loaded{u}") for u in range(RING)]
            one_added = steps("z_one_added", RING)
            x_ready = steps("z_x_ready", RING)

            @block.sync
            def _(sp):
                with sp.Fori(0, G // RING) as q:
                    for u in range(RING):
                        n = q * RING + u
                        sp.wait_ge(x_ready.sem, x_ready.done(n - RING))
                        for k in range(2):
                            sp.dma_start(ys[u][:, k], outs_dram[0:2 * TOKENS, :].rearrange(
                                "(k b p) d -> k p b d", k=2, p=P)[k, :, bass.ds(n * NB, NB), :])\
                                .then_inc(loaded[u], 16)

            @block.vector
            def _(dve):
                one_added.open(dve)
                x_ready.open(dve)
                with dve.Fori(0, G // RING) as q:
                    for u in range(RING):
                        n = q * RING + u
                        dve.wait_ge(loaded[u], q * 32 + 32)
                        for k, s in ((0, one_added), (1, x_ready)):
                            for b in range(NB):
                                x_b = X[:, bass.ds(n * (NB * D) + b * D, D)]
                                ins = nc.vector.scalar_tensor_tensor(x_b, ys[u][:, k, b, :],
                                                                     pairw[:, k, bass.ds(n * NB + b, 1)], x_b,
                                                                     ALU.mult, ALU.add)
                            ins.then_inc(s.sem, 1)
                            if k == 0:
                                dve.wait_ge(s.sem, s.done(n))

            @block.scalar
            def _(act):
                with act.Fori(0, G) as n:
                    act.wait_ge(x_ready.sem, x_ready.done(n))
                    part = bass.ds(n * (NB * D), NB * D)
                    act.dma_start(out[:, part], X[:, part]).then_inc(s_out, 16)
                act.wait_ge(s_out, 16 * G)
        free(len(scopes))


def kernel(**inputs):
    import concourse.bacc as bacc
    from concourse.bass_utils import run_bass_kernel_spmd

    a = {k: np.asarray(v) for k, v in inputs.items()}

    def column(v):
        return v.reshape(-1, 1)

    def rows(v, n=P):
        return np.broadcast_to(v.reshape(1, -1), (n, v.size))

    def pad(v):
        full = np.zeros((P, v.shape[1]), np.float32)
        full[:v.shape[0]] = v
        return full

    ahead = np.zeros((D, HEADS), np.float32)
    for h in range(HEADS):
        ahead[h * (D // HEADS):(h + 1) * (D // HEADS), h] = a["L0_gnn_a"][h]
    idx = np.arange(P, dtype=np.float32)
    parts = {
        "ident": np.eye(P, dtype=np.float32),
        "iota": rows(np.arange(EDGES, dtype=np.float32)),
        "pidx": column(idx),
        "eidx": np.stack([idx + P * c for c in range(EC)], 1),
        "below": np.triu(np.ones((P, P), np.float32), 1),
        "blk": rows(np.arange(BLOCKS, dtype=np.float32)),
        "pos": idx[:, None] + P * np.arange(NQ, dtype=np.float32),
        "blkrow": rows(np.arange(BLOCKS, dtype=np.float32) * BLOCK),
        "ones": np.ones((P, P), np.float32),
        "rank0": rows(np.arange(E0, 0, -1, dtype=np.float32)),
        "rank1": rows(np.arange(E1, 0, -1, dtype=np.float32)),
        "wq": a["L0_gnn_W_lin"].T, "wv": a["L0_gnn_W_val"].T, "wout": a["L0_gnn_W_out"].T,
        "ahead": ahead, "adj": a["adj"], "adjT": a["adj"].T,
        "rw1": a["L0_ffn_router_w1"], "rb1": pad(column(a["L0_ffn_router_b1"])),
        "rw2": pad(a["L0_ffn_router_w2"]), "rb2": rows(a["L0_ffn_router_b2"]),
        "wg0": a["L1_gnn_Wg0"], "bg0": rows(a["L1_gnn_bg0"]),
        "wg1": a["L1_gnn_Wg1"], "bg1": rows(a["L1_gnn_bg1"]), "wr": a["L1_ffn_Wr"],
    }
    small = np.concatenate([parts[n] for n, _ in SMALL], 1)
    sd = np.stack([a["L0_gnn_src"], a["L0_gnn_dst"]])
    edges = np.concatenate([rows(sd), sd.reshape(2, EC, P).transpose(2, 1, 0).reshape(P, 2 * EC)], 1)
    ffn0 = np.concatenate(
        [a["L0_ffn_expert_w1"].transpose(1, 0, 2).reshape(D, -1),
         a["L0_ffn_expert_w2"].transpose(1, 0, 2).reshape(D, -1),
         a["L0_ffn_expert_w3"].transpose(1, 0, 2).reshape(D, -1),
         a["L0_ffn_expert_b1"].T, a["L0_ffn_expert_b2"].T, pad(a["L0_ffn_expert_b3"])], 1)
    lstm = np.concatenate(
        [a["L1_gnn_Wih"].transpose(2, 0, 1).reshape(D, -1), a["L1_gnn_Whh"].transpose(2, 0, 1).reshape(D, -1),
         a["L1_gnn_bih"].reshape(-1, D).T, a["L1_gnn_bhh"].reshape(-1, D).T], 1)
    w1 = np.concatenate([a["L1_ffn_W1p"], a["L1_ffn_W1s"][None]], 0)
    w2 = np.concatenate([a["L1_ffn_W2p"], a["L1_ffn_W2s"][None]], 0)
    b1 = np.concatenate([a["L1_ffn_b1p"], a["L1_ffn_b1s"][None]], 0)
    b2 = np.concatenate([a["L1_ffn_b2p"], a["L1_ffn_b2s"][None]], 0)
    ffn1 = np.concatenate(
        [np.concatenate([w1, w2.reshape(E1 + 1, FK, D, D).transpose(0, 2, 1, 3).reshape(E1 + 1, D, FK * D)], 2)
         .transpose(1, 0, 2).reshape(D, -1),
         np.concatenate([b1.reshape(E1 + 1, FK, D), b2.reshape(E1 + 1, 1, D)], 1).transpose(2, 0, 1).reshape(D, -1)], 1)
    tokid = (np.arange(B)[None] * P + np.arange(P)[:, None]).astype(np.int32)
    spare = (2 * TOKENS + np.arange(NQ)[None] * P + np.arange(P)[:, None]).astype(np.int32)
    ids = np.concatenate([tokid, np.full_like(spare, SLOTS), spare], 1)
    arrays = {"xT_dram": a["x"].transpose(1, 0, 2).reshape(P, B * D), "small_dram": small, "edges_dram": edges,
              "ids_dram": ids,
              "ffn0_dram": ffn0, "lstm_dram": lstm, "ffn1_dram": ffn1}
    arrays = {k: np.ascontiguousarray(v) for k, v in arrays.items()}

    nc = bacc.Bacc("TRN2", target_bir_lowering=False, num_devices=1)
    args = [nc.dram_tensor(n, v.shape, mybir.dt.from_np(v.dtype), kind="ExternalInput").ap() for n, v in arrays.items()]
    out = nc.dram_tensor("out_0_dram", (P, B * D), F32, kind="ExternalOutput").ap()
    build(nc, *args, out)
    r = run_bass_kernel_spmd(nc, [arrays], core_ids=[0])
    return r.results[0]["out_0_dram"].reshape(P, B, D).transpose(1, 0, 2)
```
